# Optimizing a Trainium2 kernel written in Bass

```python
import numpy as np
import jax
import jax.numpy as jnp

def _softmax(x, axis=-1):
    return jax.nn.softmax(x, axis=axis)

def _gelu(x):
    return jax.nn.gelu(x, approximate=True)

def _silu(x):
    return jax.nn.silu(x)

def _sigmoid(x):
    return jax.nn.sigmoid(x)

def _layernorm(x, axis=-1, eps=1e-05):
    m = jnp.mean(x, axis=axis, keepdims=True)
    v = jnp.var(x, axis=axis, keepdims=True)
    return (x - m) / jnp.sqrt(v + eps)

def _scatter_add(tgt, idx, src, axis=0):
    return tgt.at[idx].add(src)

def _segment_sum(src, seg, n):
    return jax.ops.segment_sum(src, seg, n)
kernel_name = 'mk_decoder_postln_d2_seqx_r8_648091'

def setup_inputs(seed: int=0):
    np.random.seed(seed)
    _w = jnp.asarray

    def _rec_inputs():
        import jax
        import jax.numpy as jnp
        _rk = jax.random.key(seed)
        x = 7.22e-05 + 1 * jax.random.normal(jax.random.fold_in(_rk, 1), (4, 256, 256), jnp.float32)
        _lenS = 256 - jax.random.randint(jax.random.fold_in(_rk, 7), (4,), 0, max(1, 256 // 4) + 1, jnp.int32)
        _lenS2 = 256 - jax.random.randint(jax.random.fold_in(_rk, 8), (4,), 0, max(1, 256 // 4) + 1, jnp.int32)
        _ctx_2048P = jax.random.normal(jax.random.fold_in(_rk, 11), (4, 16, 256), jnp.float32)
        _ctx_2048c = jax.random.dirichlet(jax.random.fold_in(_rk, 511), 0.3 * jnp.ones((16,), jnp.float32), (4, 256))
        _ctx_2048t = jnp.einsum('bsk,bkd->bsd', _ctx_2048c, _ctx_2048P)
        _ctx_2048t = _ctx_2048t * jax.lax.rsqrt(jnp.mean(jnp.square(_ctx_2048t)) + 1e-12) * 0.953939
        ctx_2048 = 4.13588e-05 + 0.999923 * (_ctx_2048t + 0.3 * jax.random.normal(jax.random.fold_in(_rk, 611), (4, 256, 256), jnp.float32))
        itok_BxS_13_99985 = jax.random.randint(jax.random.fold_in(_rk, 12), (4, 256), 13, 99986, jnp.int32)
        return (x, ctx_2048, itok_BxS_13_99985)
    x, ctx_2048, itok_BxS_13_99985 = _rec_inputs()

    def _L0_attn_setup():
        import jax, jax.numpy as jnp
        import numpy as np
        NUM_HEADS = 16
        ROPE_THETA = 10000.0

        def _rope(t, cos2, sin2):
            x_even = t[..., 0::2]
            x_odd = t[..., 1::2]
            rot = jnp.stack([-x_odd, x_even], axis=-1).reshape(t.shape)
            return t * cos2 + rot * sin2
        key = jax.random.key(seed)
        ks = jax.random.split(key, 5)
        B, S, D = (4, 256, 256)
        std = (2.0 / (D + D)) ** 0.5
        return {'x': jax.random.normal(ks[0], (B, S, D), dtype=jnp.float32), 'Wq': jax.random.normal(ks[1], (D, D), dtype=jnp.float32) * std, 'Wk': jax.random.normal(ks[2], (D, D), dtype=jnp.float32) * std, 'Wv': jax.random.normal(ks[3], (D, D), dtype=jnp.float32) * std, 'Wo': jax.random.normal(ks[4], (D, D), dtype=jnp.float32) * std}
    _L0_attn_all = _L0_attn_setup()
    _L0_attn_in = {k: v for k, v in _L0_attn_all.items() if k in ('Wq', 'Wk', 'Wv', 'Wo')}
    del _L0_attn_all

    def _L0_xattn_setup():
        import jax, jax.numpy as jnp
        import numpy as np
        N_HEAD = 8
        key = jax.random.key(seed)
        k1, k2, k3 = jax.random.split(key, 3)
        B, D, L = (4, 128, 256)
        q = jax.random.normal(k1, (B, D, L), dtype=jnp.float32)
        k = jax.random.normal(k2, (B, D, L), dtype=jnp.float32)
        v = jax.random.normal(k3, (B, D, L), dtype=jnp.float32)
        gamma = jnp.ones((), dtype=jnp.float32)
        return {'q': q, 'k': k, 'v': v, 'gamma': gamma}
    _L0_xattn_all = _L0_xattn_setup()
    _L0_xattn_in = {k: v for k, v in _L0_xattn_all.items() if k in ('gamma',)}
    del _L0_xattn_all

    def _L0_ffn_setup():
        import jax, jax.numpy as jnp
        import numpy as np

        def fwht(x):
            n = x.shape[-1]
            orig_shape = x.shape
            x = x.reshape(-1, n)
            h = 1
            while h < n:
                x = x.reshape(-1, n // (2 * h), 2, h)
                a = x[:, :, 0, :]
                b = x[:, :, 1, :]
                x = jnp.stack([a + b, a - b], axis=2)
                h *= 2
            x = x.reshape(orig_shape)
            return x * (1.0 / jnp.sqrt(jnp.asarray(n, dtype=x.dtype)))

        def act_quant(x, bits):
            qb = 2.0 ** (bits - 1) - 1.0
            scale = qb / jnp.clip(jnp.max(jnp.abs(x), axis=-1, keepdims=True), 1e-05, None)
            q = jnp.clip(jnp.round(x * scale), -qb, qb) / scale
            return x + jax.lax.stop_gradient(q - x)

        def weight_quant(w):
            scale = jnp.clip(jnp.mean(jnp.abs(w)), 1e-05, None)
            q = jnp.clip(jnp.round(w / scale), -1.0, 1.0) * scale
            return w + jax.lax.stop_gradient(q - w)

        def hbitlinear(x, w, bits):
            xh = fwht(x)
            xq = act_quant(xh, bits)
            wq = weight_quant(w)
            return jnp.einsum('bsh,oh->bso', xq, wq)
        key = jax.random.key(seed)
        k1, k2, k3 = jax.random.split(key, 3)
        B, S, H = (4, 256, 256)
        I = 512
        hidden_states = jax.random.normal(k1, (B, S, H), dtype=jnp.float32)
        w_up = jax.random.normal(k2, (I, H), dtype=jnp.float32) * 0.02
        w_down = jax.random.normal(k3, (H, I), dtype=jnp.float32) * 0.02
        return {'hidden_states': hidden_states, 'w_up': w_up, 'w_down': w_down}
    _L0_ffn_all = _L0_ffn_setup()
    _L0_ffn_in = {k: v for k, v in _L0_ffn_all.items() if k in ('w_up', 'w_down')}
    del _L0_ffn_all

    def _L1_attn_setup():
        import jax, jax.numpy as jnp
        import numpy as np
        B, S, M = (1, 256, 256)
        H, HKV, D = (32, 8, 64)
        SW = 128
        WAVELENGTH = 150000.0
        SCALE = D ** (-0.25)
        NEG = -1000000000.0

        def _cos_sin(seq_len, dtype):
            half = D // 2
            inv_freq = 1.0 / WAVELENGTH ** (jnp.arange(half, dtype=jnp.float32) * 2.0 / D)
            t = jnp.arange(seq_len, dtype=jnp.float32)
            freqs = t[:, None] * inv_freq[None, :]
            return (jnp.cos(freqs)[None, :, None, :].astype(dtype), jnp.sin(freqs)[None, :, None, :].astype(dtype))

        def _interleaved_rope(x, cos, sin):
            x_even = x[..., ::2]
            x_odd = x[..., 1::2]
            first = x_even * cos - x_odd * sin
            second = x_odd * cos + x_even * sin
            return jnp.stack([first, second], axis=-1).reshape(x.shape)
        key = jax.random.key(seed)
        ks = jax.random.split(key, 8)
        return {'hidden_states': jax.random.normal(ks[0], (B, S, M), jnp.float32), 'Wq': jax.random.normal(ks[1], (M, H, D), jnp.float32) * 0.02, 'bq': jnp.zeros((H, D), jnp.float32), 'Wk': jax.random.normal(ks[2], (M, HKV, D), jnp.float32) * 0.02, 'bk': jnp.zeros((HKV, D), jnp.float32), 'Wv': jax.random.normal(ks[3], (M, HKV, D), jnp.float32) * 0.02, 'bv': jnp.zeros((HKV, D), jnp.float32), 'Wo': jax.random.normal(ks[4], (H, D, M), jnp.float32) * 0.02, 'bo': jnp.zeros((M,), jnp.float32), 'sinks': jax.random.normal(ks[5], (H,), jnp.float32)}
    _L1_attn_all = _L1_attn_setup()
    _L1_attn_in = {k: v for k, v in _L1_attn_all.items() if k in ('Wq', 'bq', 'Wk', 'bk', 'Wv', 'bv', 'Wo', 'bo', 'sinks')}
    del _L1_attn_all

    def _L1_xattn_setup():
        import jax, jax.numpy as jnp
        import numpy as np
        B, S, D = (4, 512, 256)
        E = 4
        F = 1024 // E
        VOCAB = 12500
        key = jax.random.key(seed)
        k1, k2, k3, k4, k5 = jax.random.split(key, 5)
        hidden_states = jax.random.normal(k1, (B, S, D), dtype=jnp.float32)
        token_ids = jax.random.randint(k2, (B, S), 0, VOCAB, dtype=jnp.int64)
        Wg = jax.random.normal(k3, (E, F, D), dtype=jnp.float32) * 0.02
        Wu = jax.random.normal(k4, (E, F, D), dtype=jnp.float32) * 0.02
        Wd = jax.random.normal(k5, (E, D, F), dtype=jnp.float32) * 0.02
        return {'hidden_states': hidden_states, 'token_ids': token_ids, 'Wg': Wg, 'Wu': Wu, 'Wd': Wd}
    _L1_xattn_all = _L1_xattn_setup()
    _L1_xattn_in = {k: v for k, v in _L1_xattn_all.items() if k in ()}
    del _L1_xattn_all

    def _L1_ffn_setup():
        import jax, jax.numpy as jnp
        import numpy as np
        HIDDEN = 256
        NUM_EXPERTS = 32
        TOP_K = 4
        MOE_INTER = 96
        GROUP = 2
        NUM_CHUNK = NUM_EXPERTS // GROUP
        CHUNK_INTER = 128
        SMALL_SCALE = 0.05

        def _routing(x2d, gate_w):
            logits = x2d @ gate_w.T
            rw = jax.nn.softmax(logits.astype(jnp.float32), axis=-1)
            scores = jax.nn.sigmoid(logits.astype(jnp.float32))
            _, sel = jax.lax.top_k(scores, TOP_K)
            w = jnp.take_along_axis(rw, sel, axis=-1)
            w = w / w.sum(axis=-1, keepdims=True)
            return (w.astype(x2d.dtype), sel)

        def _moe(x2d, Wg, Wu, Wd, cw):
            g = jnp.einsum('th,ehi->eti', x2d, Wg)
            u = jnp.einsum('th,ehi->eti', x2d, Wu)
            a = jax.nn.silu(g) * u * cw.T[:, :, None]
            return jnp.einsum('eti,eih->th', a, Wd)
        key = jax.random.key(seed)
        ks = jax.random.split(key, 8)
        s = 0.02
        B, S = (2, 256)
        return {'hidden_states': jax.random.normal(ks[0], (B, S, HIDDEN), jnp.float32), 'gate_w': jax.random.normal(ks[1], (NUM_EXPERTS, HIDDEN), jnp.float32) * s, 'Wg': jax.random.normal(ks[2], (NUM_EXPERTS, HIDDEN, MOE_INTER), jnp.float32) * s, 'Wu': jax.random.normal(ks[3], (NUM_EXPERTS, HIDDEN, MOE_INTER), jnp.float32) * s, 'Wd': jax.random.normal(ks[4], (NUM_EXPERTS, MOE_INTER, HIDDEN), jnp.float32) * s, 'cWg': jax.random.normal(ks[5], (NUM_CHUNK, HIDDEN, CHUNK_INTER), jnp.float32) * s, 'cWu': jax.random.normal(ks[6], (NUM_CHUNK, HIDDEN, CHUNK_INTER), jnp.float32) * s, 'cWd': jax.random.normal(ks[7], (NUM_CHUNK, CHUNK_INTER, HIDDEN), jnp.float32) * s}
    _L1_ffn_all = _L1_ffn_setup()
    _L1_ffn_in = {k: v for k, v in _L1_ffn_all.items() if k in ('gate_w', 'Wg', 'Wu', 'Wd', 'cWg', 'cWu', 'cWd')}
    del _L1_ffn_all
    return {'x': x, 'ctx_2048': ctx_2048, 'itok_BxS_13_99985': itok_BxS_13_99985, 'L0_attn_Wq': _L0_attn_in['Wq'], 'L0_attn_Wk': _L0_attn_in['Wk'], 'L0_attn_Wv': _L0_attn_in['Wv'], 'L0_attn_Wo': _L0_attn_in['Wo'], 'L0_xattn_gamma': _L0_xattn_in['gamma'], 'L0_ffn_w_up': _L0_ffn_in['w_up'], 'L0_ffn_w_down': _L0_ffn_in['w_down'], 'L1_attn_Wq': _L1_attn_in['Wq'], 'L1_attn_bq': _L1_attn_in['bq'], 'L1_attn_Wk': _L1_attn_in['Wk'], 'L1_attn_bk': _L1_attn_in['bk'], 'L1_attn_Wv': _L1_attn_in['Wv'], 'L1_attn_bv': _L1_attn_in['bv'], 'L1_attn_Wo': _L1_attn_in['Wo'], 'L1_attn_bo': _L1_attn_in['bo'], 'L1_attn_sinks': _L1_attn_in['sinks'], 'L1_ffn_gate_w': _L1_ffn_in['gate_w'], 'L1_ffn_Wg': _L1_ffn_in['Wg'], 'L1_ffn_Wu': _L1_ffn_in['Wu'], 'L1_ffn_Wd': _L1_ffn_in['Wd'], 'L1_ffn_cWg': _L1_ffn_in['cWg'], 'L1_ffn_cWu': _L1_ffn_in['cWu'], 'L1_ffn_cWd': _L1_ffn_in['cWd']}

def reference(x, ctx_2048, itok_BxS_13_99985, L0_attn_Wq, L0_attn_Wk, L0_attn_Wv, L0_attn_Wo, L0_xattn_gamma, L0_ffn_w_up, L0_ffn_w_down, L1_attn_Wq, L1_attn_bq, L1_attn_Wk, L1_attn_bk, L1_attn_Wv, L1_attn_bv, L1_attn_Wo, L1_attn_bo, L1_attn_sinks, L1_ffn_gate_w, L1_ffn_Wg, L1_ffn_Wu, L1_ffn_Wd, L1_ffn_cWg, L1_ffn_cWu, L1_ffn_cWd):
    import jax
    import jax.numpy as jnp

    def _L0_attn_ref(x, Wq, Wk, Wv, Wo):
        import jax, jax.numpy as jnp
        import numpy as np
        NUM_HEADS = 16
        ROPE_THETA = 10000.0

        def _rope(t, cos2, sin2):
            x_even = t[..., 0::2]
            x_odd = t[..., 1::2]
            rot = jnp.stack([-x_odd, x_even], axis=-1).reshape(t.shape)
            return t * cos2 + rot * sin2
        B, S, D = x.shape
        H = NUM_HEADS
        dk = D // H
        Q = jnp.einsum('bsi,io->bso', x, Wq).reshape(B, S, H, dk).swapaxes(1, 2)
        K = jnp.einsum('bsi,io->bso', x, Wk).reshape(B, S, H, dk).swapaxes(1, 2)
        V = jnp.einsum('bsi,io->bso', x, Wv).reshape(B, S, H, dk).swapaxes(1, 2)
        inv_freq = 1.0 / ROPE_THETA ** (jnp.arange(0, dk, 2, dtype=jnp.float32) / dk)
        angles = jnp.outer(jnp.arange(S, dtype=jnp.float32), inv_freq)
        cos2 = jnp.repeat(jnp.cos(angles), 2, axis=-1).astype(x.dtype)
        sin2 = jnp.repeat(jnp.sin(angles), 2, axis=-1).astype(x.dtype)
        Q = _rope(Q, cos2, sin2)
        K = _rope(K, cos2, sin2)
        scores = jnp.einsum('bhqd,bhkd->bhqk', Q, K) / dk ** 0.5
        causal = jnp.tril(jnp.ones((S, S), dtype=jnp.bool_))
        scores = jnp.where(causal, scores, -jnp.inf)
        probs = jax.nn.softmax(scores, axis=-1)
        attn = jnp.einsum('bhqk,bhkd->bhqd', probs, V)
        attn = attn.swapaxes(1, 2).reshape(B, S, D)
        return jnp.einsum('bsi,io->bso', attn, Wo)

    def _L0_xattn_ref(q, k, v, gamma):
        import jax, jax.numpy as jnp
        import numpy as np
        N_HEAD = 8
        B, Dq, Lq = q.shape
        Dv, Lk = (v.shape[-2], v.shape[-1])
        h = N_HEAD
        dq = Dq // h
        dv = Dv // h
        qh = q.reshape(B, h, dq, Lq)
        kh = k.reshape(B, h, dq, Lk)
        vh = v.reshape(B, h, dv, Lk)
        scale = 1.0 / jnp.sqrt(jnp.asarray(dq, dtype=q.dtype))
        qk = jnp.einsum('bhdq,bhdl->bhql', qh, kh) * scale
        sm = jax.nn.softmax(qk, axis=-1)
        ret = jnp.einsum('bhql,bhdl->bhdq', sm, vh)
        ret = ret.reshape(B, Dv, Lq)
        return gamma * ret

    def _L0_ffn_ref(hidden_states, w_up, w_down):
        import jax, jax.numpy as jnp
        import numpy as np

        def fwht(x):
            n = x.shape[-1]
            orig_shape = x.shape
            x = x.reshape(-1, n)
            h = 1
            while h < n:
                x = x.reshape(-1, n // (2 * h), 2, h)
                a = x[:, :, 0, :]
                b = x[:, :, 1, :]
                x = jnp.stack([a + b, a - b], axis=2)
                h *= 2
            x = x.reshape(orig_shape)
            return x * (1.0 / jnp.sqrt(jnp.asarray(n, dtype=x.dtype)))

        def act_quant(x, bits):
            qb = 2.0 ** (bits - 1) - 1.0
            scale = qb / jnp.clip(jnp.max(jnp.abs(x), axis=-1, keepdims=True), 1e-05, None)
            q = jnp.clip(jnp.round(x * scale), -qb, qb) / scale
            return x + jax.lax.stop_gradient(q - x)

        def weight_quant(w):
            scale = jnp.clip(jnp.mean(jnp.abs(w)), 1e-05, None)
            q = jnp.clip(jnp.round(w / scale), -1.0, 1.0) * scale
            return w + jax.lax.stop_gradient(q - w)

        def hbitlinear(x, w, bits):
            xh = fwht(x)
            xq = act_quant(xh, bits)
            wq = weight_quant(w)
            return jnp.einsum('bsh,oh->bso', xq, wq)
        ACT_BITS = 8
        h = hbitlinear(hidden_states, w_up, ACT_BITS)
        h = jnp.square(jax.nn.relu(h))
        out = hbitlinear(h, w_down, ACT_BITS)
        return out

    def _L1_attn_ref(hidden_states, Wq, bq, Wk, bk, Wv, bv, Wo, bo, sinks):
        import jax, jax.numpy as jnp
        import numpy as np
        B, S, M = (1, 256, 256)
        H, HKV, D = (32, 8, 64)
        SW = 128
        WAVELENGTH = 150000.0
        SCALE = D ** (-0.25)
        NEG = -1000000000.0

        def _cos_sin(seq_len, dtype):
            half = D // 2
            inv_freq = 1.0 / WAVELENGTH ** (jnp.arange(half, dtype=jnp.float32) * 2.0 / D)
            t = jnp.arange(seq_len, dtype=jnp.float32)
            freqs = t[:, None] * inv_freq[None, :]
            return (jnp.cos(freqs)[None, :, None, :].astype(dtype), jnp.sin(freqs)[None, :, None, :].astype(dtype))

        def _interleaved_rope(x, cos, sin):
            x_even = x[..., ::2]
            x_odd = x[..., 1::2]
            first = x_even * cos - x_odd * sin
            second = x_odd * cos + x_even * sin
            return jnp.stack([first, second], axis=-1).reshape(x.shape)
        b, s, _ = hidden_states.shape
        groups = H // HKV
        q = jnp.einsum('bqm,muh->bquh', hidden_states, Wq) + bq
        k = jnp.einsum('bkm,mvh->bkvh', hidden_states, Wk) + bk
        v = jnp.einsum('bkm,mvh->bkvh', hidden_states, Wv) + bv
        cos, sin = _cos_sin(s, hidden_states.dtype)
        q = _interleaved_rope(q, cos, sin) * SCALE
        k = _interleaved_rope(k, cos, sin) * SCALE
        k = jnp.repeat(k, groups, axis=2)
        v = jnp.repeat(v, groups, axis=2)
        scores = jnp.einsum('bquh,bkuh->buqk', q, k)
        pos = jnp.arange(s)
        sw_mask = jnp.abs(pos[:, None] - pos[None, :]) <= SW
        scores = jnp.where(sw_mask[None, None, :, :], scores, NEG)
        sink_logits = jnp.broadcast_to(sinks[None, :, None, None], (b, H, s, 1))
        combined = jnp.concatenate([scores, sink_logits], axis=-1)
        probs = jax.nn.softmax(combined.astype(jnp.float32), axis=-1)
        attn = probs[..., :-1].astype(hidden_states.dtype)
        out = jnp.einsum('buqk,bkuh->bquh', attn, v)
        return jnp.einsum('bquh,uhm->bqm', out, Wo) + bo

    def _L1_xattn_ref(hidden_states, token_ids, Wg, Wu, Wd):
        import jax, jax.numpy as jnp
        import numpy as np
        B, S, D = (4, 512, 256)
        E = 4
        F = 1024 // E
        VOCAB = 12500
        tokens_per_expert = VOCAB // E
        tid = jnp.clip(token_ids, 0, VOCAB - 1)
        expert_ids = jnp.minimum(tid // tokens_per_expert, E - 1)
        out = jnp.zeros_like(hidden_states)
        for e in range(E):
            g = jax.nn.silu(jnp.einsum('bsd,fd->bsf', hidden_states, Wg[e]))
            u = jnp.einsum('bsd,fd->bsf', hidden_states, Wu[e])
            y = jnp.einsum('bsf,df->bsd', g * u, Wd[e])
            out = jnp.where((expert_ids == e)[..., None], y, out)
        return out

    def _L1_ffn_ref(hidden_states, gate_w, Wg, Wu, Wd, cWg, cWu, cWd):
        import jax, jax.numpy as jnp
        import numpy as np
        HIDDEN = 256
        NUM_EXPERTS = 32
        TOP_K = 4
        MOE_INTER = 96
        GROUP = 2
        NUM_CHUNK = NUM_EXPERTS // GROUP
        CHUNK_INTER = 128
        SMALL_SCALE = 0.05

        def _routing(x2d, gate_w):
            logits = x2d @ gate_w.T
            rw = jax.nn.softmax(logits.astype(jnp.float32), axis=-1)
            scores = jax.nn.sigmoid(logits.astype(jnp.float32))
            _, sel = jax.lax.top_k(scores, TOP_K)
            w = jnp.take_along_axis(rw, sel, axis=-1)
            w = w / w.sum(axis=-1, keepdims=True)
            return (w.astype(x2d.dtype), sel)

        def _moe(x2d, Wg, Wu, Wd, cw):
            g = jnp.einsum('th,ehi->eti', x2d, Wg)
            u = jnp.einsum('th,ehi->eti', x2d, Wu)
            a = jax.nn.silu(g) * u * cw.T[:, :, None]
            return jnp.einsum('eti,eih->th', a, Wd)
        B, S, H = hidden_states.shape
        T = B * S
        x = hidden_states.reshape(T, H)
        w, sel = _routing(x, gate_w)
        rows = jnp.arange(T)[:, None]
        cw_large = jnp.zeros((T, NUM_EXPERTS), x.dtype).at[rows, sel].add(w)
        cw_small = jnp.zeros((T, NUM_CHUNK), x.dtype).at[rows, sel // GROUP].add(w)
        large = _moe(x, Wg, Wu, Wd, cw_large)
        small = _moe(x, cWg, cWu, cWd, cw_small)
        return (large + SMALL_SCALE * small).reshape(B, S, H)
    x = _layernorm(x + _L0_attn_ref(x, L0_attn_Wq, L0_attn_Wk, L0_attn_Wv, L0_attn_Wo), axis=-1)
    x = _layernorm(x + _L0_xattn_ref(x, ctx_2048, ctx_2048, L0_xattn_gamma), axis=-1)
    x = _layernorm(x + _L0_ffn_ref(x, L0_ffn_w_up, L0_ffn_w_down), axis=-1)
    x = _layernorm(x + _L1_attn_ref(x, L1_attn_Wq, L1_attn_bq, L1_attn_Wk, L1_attn_bk, L1_attn_Wv, L1_attn_bv, L1_attn_Wo, L1_attn_bo, L1_attn_sinks), axis=-1)
    x = _layernorm(x + _L1_xattn_ref(x, itok_BxS_13_99985, ctx_2048, ctx_2048, ctx_2048), axis=-1)
    x = _layernorm(x + _L1_ffn_ref(x, L1_ffn_gate_w, L1_ffn_Wg, L1_ffn_Wu, L1_ffn_Wd, L1_ffn_cWg, L1_ffn_cWu, L1_ffn_cWd), axis=-1)
    return x

_drawn_inputs = setup_inputs


def setup_inputs(seed=0):
    import zlib

    import numpy as np

    out = dict(_drawn_inputs(seed))
    spreads = {'L1_attn_bq': (0.0, 0.8),
     'L1_attn_bk': (0.0, 0.8),
     'L1_attn_bv': (0.0, 0.1),
     'L1_attn_bo': (0.0, 0.1)}
    factors = {'L0_ffn_w_up': 2.954,
     'L0_ffn_w_down': 2.737,
     'L1_attn_Wq': 8.0,
     'L1_attn_Wk': 8.0,
     'L1_attn_sinks': 8.0,
     'L1_ffn_gate_w': 8.0,
     'L1_ffn_Wg': 8.0,
     'L1_ffn_Wu': 8.0,
     'L1_ffn_Wd': 8.0,
     'L1_ffn_cWg': 8.0,
     'L1_ffn_cWu': 8.0,
     'L1_ffn_cWd': 8.0}
    for name, (base, spread) in spreads.items():
        noise = np.random.default_rng([zlib.crc32(name.encode()), seed]).standard_normal(out[name].shape)
        drawn = base * np.exp(spread * noise) if base else spread * noise
        out[name] = jnp.asarray(drawn.astype(out[name].dtype))
    for name, factor in factors.items():
        out[name] = (out[name] * factor).astype(out[name].dtype)
    return out
```

```python
import concourse.bass as bass
from concourse import mybir
from contextlib import ExitStack

F32 = mybir.dt.float32
BF16 = mybir.dt.bfloat16
U32 = mybir.dt.uint32
ALU = mybir.AluOpType
ACT = mybir.ActivationFunctionType
AX = mybir.AxisListType

B, S, D = 4, 256, 256
P = 128
NT = B * S // P
KD = D // P
H0, DK0 = 16, 16
HX, DX = 8, 32
I0 = 512
H1, HKV, D1 = 32, 8, 64
NQ1, NKV1 = H1 * D1, HKV * D1
NE, INTER = 32, 96
NC, CINTER = 16, 128
TOPK = 4
EPS = 1e-5
SMALL_SCALE = 0.05
MAGIC = 12582912.0


def need(eng, sem, value):
    if not (isinstance(value, int) and value <= 0):
        eng.wait_ge(sem, value)


def hold(eng, passed):
    eng.sem_inc(passed, 1)


class Chain:

    def __init__(self, eng, sem):
        self.eng, self.sem, self.n = eng, sem, 0

    def link(self, ins):
        self.n += 1
        ins.then_inc(self.sem, 1)
        self.eng.wait_ge(self.sem, self.n)


class Store:

    def __init__(self, nc, stack, passing=True):
        self.nc, self.stack, self.passing = nc, stack, passing

    def sb(self, name, shape, dt=F32):
        return self.stack.enter_context(self.nc.sbuf_tensor(name, shape, dt))

    def ps(self, name, shape, dt=F32):
        return self.stack.enter_context(self.nc.psum_tensor(name, shape, dt))

    spent = []

    def sem(self, name):
        sem = self.nc.alloc_semaphore(name)
        if self.passing:
            Store.spent.append(sem)
        return sem


def recycle(nc):
    nc.clear_and_free_semaphores(Store.spent)
    Store.spent.clear()
    nc.all_engine_barrier()



def spread(pool, KM, keys, heads):
    shape = [P, KM.shape[1], S]
    return pool.tensor_tensor(KM, keys.unsqueeze(1).to_broadcast(shape),
                              heads.unsqueeze(2).to_broadcast(shape), ALU.mult)


def attention(nc, consts, name, units, stage_qk, stage_v, out_of, *, width, pairs, mask=None, causal=False,
              scale=1.0, sinks_of=None):
    NB = units // 2
    with ExitStack() as stack:
        st = Store(nc, stack)
        nq = 2 if pairs else 1
        Qs = st.sb(name + "_Qs", [P, 2, nq, S])
        nk = 2 if pairs else 4
        KM = st.sb(name + "_KM", [P, 2, nk, S])
        Vs = st.sb(name + "_Vs", [P, 2, 2, 64 if pairs else 128])
        Sm = st.sb(name + "_Sm", [P, 2, 4, S])
        Pr = st.sb(name + "_Pr", [P, 4, 4, S])
        PT = st.sb(name + "_PT", [P, 2, 4, 2, P])
        mx = st.sb(name + "_mx", [P, 4, 4])
        nm = st.sb(name + "_nm", [P, 4, 4])
        den = st.sb(name + "_den", [P, 4, 4])
        rd = st.sb(name + "_rd", [P, 4, 4])
        sk = st.sb(name + "_sk", [P, 4, 4])
        es = st.sb(name + "_es", [P, 4, 4])
        psS = st.ps(name + "_psS", [P, 2, 4, S])
        psT = st.ps(name + "_psT", [P, 4, 2, P])
        psO = st.ps(name + "_psO", [P, 2, 512])
        staged = st.sem(name + "_staged")
        staged_v = st.sem(name + "_staged_v")
        scored = st.sem(name + "_scored")
        maxed = st.sem(name + "_maxed")
        shifted = st.sem(name + "_shifted")
        expd = st.sem(name + "_expd")
        summed = st.sem(name + "_summed")
        recip = st.sem(name + "_recip")
        normed = st.sem(name + "_normed")
        turned = st.sem(name + "_turned")
        copied_a = st.sem(name + "_copied_a")
        copied_v = st.sem(name + "_copied_v")
        mixed = st.sem(name + "_mixed")
        passed_p = st.sem(name + "_passed_p")
        passed_v = st.sem(name + "_passed_v")
        stored = st.sem(name + "_stored")
        ident = consts["ident"]
        block = stack.enter_context(nc.Block())

        def keys(u):
            return P if causal and u % 2 == 0 else S

        def over_steps(eng, body):
            for u in range(4):
                body(u, u, 0)
            with eng.Fori(1, NB) as I:
                for u in range(4):
                    body(I * 4 + u, u, I)
            for u in range(3):
                body(4 * NB + u, u, NB)

        def lags(k, u, I, lag):
            return not (isinstance(I, int) and I == 0) or u >= lag

        def current(I):
            return not (isinstance(I, int) and I == NB)

        @block.gpsimd
        def _(pool):
            pool.memset(Vs[:], 0.0).then_inc(staged_v, 1)
            pool.wait_ge(staged_v, 1)
            for w in range(2):
                stage_qk(pool, Qs[:, w], KM[:, w], w, w, 0).then_inc(staged, 1)

            def norm(k, u):
                pool.wait_ge(recip, k + 1)
                p = Pr[:, u % 4, :, 0:keys(u)]
                pool.tensor_tensor(p, p, rd[:, u % 4, :].unsqueeze(2).to_broadcast([P, 4, keys(u)]),
                                   ALU.mult).then_inc(normed, 1)

            def rounds(I, last_round):
                for u in range(4):
                    k = 4 * I + u
                    norm(k, u)
                    if u % 2 == 0:
                        need(pool, mixed, k - 2)
                        hold(pool, passed_p)
                        stage_v(pool, Vs[:, u // 2], 2 * I + u // 2, u // 2, I).then_inc(staged_v, 1)
                    elif not last_round:
                        pool.wait_ge(scored, k + 1)
                        hold(pool, passed_p)
                        stage_qk(pool, Qs[:, u // 2], KM[:, u // 2], 2 * I + 2 + u // 2, u // 2,
                                 I + 1).then_inc(staged, 1)

            rounds(0, False)
            if NB > 2:
                with pool.Fori(1, NB - 1) as I:
                    rounds(I, False)
            rounds(NB - 1, True)

        @block.tensor
        def _(pe):
            def body(k, u, I):
                if current(I):
                    if u % 2 == 0:
                        pe.wait_ge(staged, k // 2 + 1 if isinstance(k, int) else 2 * I + u // 2 + 1)
                    need(pe, shifted if mask is not None else expd, k - 1)
                    n = keys(u)
                    for j in range(2):
                        q = Qs[:, u // 2, j if pairs else 0, (u % 2) * P:(u % 2) * P + P]
                        ks = KM[:, u // 2, 0:2, 0:n] if pairs else KM[:, u // 2, 2 * j:2 * j + 2, 0:n]
                        last = nc.tensor.matmul(psS[:, u % 2, 2 * j:2 * j + 2, 0:n], q, ks,
                                                start=True, stop=True)
                    last.then_inc(scored, 1)
                if lags(k, u, I, 2) and (current(I) or u < 2):
                    v = (u - 2) % 4
                    pe.wait_ge(normed, k - 1)
                    need(pe, copied_a, k - 2)
                    need(pe, copied_v, k - 2)
                    for h in range(4):
                        for t in range(keys(v) // P):
                            last = nc.tensor.transpose(psT[:, h, t, :], Pr[:, v, h, t * P:t * P + P],
                                                       ident[:, :])
                    last.then_inc(turned, 1)
                if lags(k, u, I, 3):
                    v = (u - 3) % 4
                    pe.wait_ge(copied_a, k - 2)
                    pe.wait_ge(copied_v, k - 2)
                    if v % 2 == 0:
                        pe.wait_ge(staged_v, (k - 3) // 2 + 2 if isinstance(k, int)
                                   else 2 * I + (u - 3) // 2 + 2)
                    need(pe, stored, k - 4)
                    nt = keys(v) // P
                    for j in range(2 if pairs else 1):
                        for t in range(nt):
                            for c in range(2 if pairs else 4):
                                h = 2 * j + c if pairs else c
                                vs = (Vs[:, v // 2, t, 0:width] if pairs
                                      else Vs[:, v // 2, t, h * width:(h + 1) * width])
                                last = nc.tensor.matmul(
                                    psO[c * width:(c + 1) * width, v % 2, j * P:(j + 1) * P], vs,
                                    PT[:, v % 2, h, t, :], start=(t == 0), stop=(t == nt - 1))
                    last.then_inc(mixed, 1)

            over_steps(pe, body)

        @block.scalar
        def _(act):
            def body(k, u, I):
                if current(I):
                    act.wait_ge(shifted, k + 1)
                    need(act, turned, k - 3)
                    n = keys(u)
                    for h in range(4):
                        src = Sm[:, u % 2, h, 0:n] if mask is not None else psS[:, u % 2, h, 0:n]
                        last = nc.scalar.activation(Pr[:, u, h, 0:n], src, ACT.Exp,
                                                    bias=nm[:, u, h:h + 1], scale=scale,
                                                    accum_out=den[:, u, h:h + 1])
                    if sinks_of is not None:
                        last = nc.scalar.activation(es[:, u, :], sk[:, u, :], ACT.Exp)
                    last.then_inc(expd, 1)
                if lags(k, u, I, 2) and (current(I) or u < 2):
                    v = (u - 2) % 4
                    act.wait_ge(turned, k - 1)
                    need(act, mixed, k - 3)
                    n = keys(v) // P
                    nc.scalar.activation(PT[:, v % 2, 0:2, 0:n, :], psT[:, 0:2, 0:n, :],
                                         ACT.Copy).then_inc(copied_a, 1)

            over_steps(act, body)

        @block.vector
        def _(dve):
            def body(k, u, I):
                if current(I):
                    dve.wait_ge(scored, k + 1)
                    hold(dve, passed_v)
                    n = keys(u)
                    if mask is not None:
                        for h in range(4):
                            last = nc.vector.tensor_tensor_reduce(
                                out=Sm[:, u % 2, h, 0:n], in0=psS[:, u % 2, h, 0:n],
                                in1=mask[:, u % 2, 0:n], scale=1.0, scalar=-3.0e38, op0=ALU.add,
                                op1=ALU.max, accum_out=mx[:, u, h:h + 1])
                    else:
                        last = nc.vector.tensor_reduce(mx[:, u, :], psS[:, u % 2, :, :], AX.X, ALU.max)
                    last.then_inc(maxed, 1)
                    dve.wait_ge(maxed, (2 * k if sinks_of else k) + 1)
                    if sinks_of is None:
                        nc.vector.tensor_scalar(nm[:, u, :], mx[:, u, :], -scale, None,
                                                ALU.mult).then_inc(shifted, 1)
                    else:
                        sinks, negs = sinks_of(2 * I + u // 2, u // 2, I)
                        nc.vector.scalar_tensor_tensor(out=nm[:, u, :], in0=mx[:, u, :], scalar=-1.0,
                                                       in1=negs, op0=ALU.mult,
                                                       op1=ALU.min).then_inc(maxed, 1)
                        dve.wait_ge(maxed, 2 * k + 2)
                        nc.vector.tensor_tensor(sk[:, u, :], nm[:, u, :], sinks,
                                                ALU.add).then_inc(shifted, 1)
                if lags(k, u, I, 1) and (current(I) or u < 1):
                    v = (u - 1) % 4
                    dve.wait_ge(expd, k)
                    if sinks_of is not None:
                        nc.vector.tensor_tensor(den[:, v, :], den[:, v, :], es[:, v, :],
                                                ALU.add).then_inc(summed, 1)
                        dve.wait_ge(summed, k)
                    nc.vector.reciprocal(rd[:, v, :], den[:, v, :]).then_inc(recip, 1)
                if lags(k, u, I, 2) and (current(I) or u < 2):
                    v = (u - 2) % 4
                    dve.wait_ge(turned, k - 1)
                    need(dve, mixed, k - 3)
                    n = keys(v) // P
                    nc.vector.tensor_copy(PT[:, v % 2, 2:4, 0:n, :],
                                          psT[:, 2:4, 0:n, :]).then_inc(copied_v, 1)
                if lags(k, u, I, 3):
                    v = (u - 3) % 4
                    dve.wait_ge(mixed, k - 2)
                    src = psO[:, v % 2, 0:2 * P].rearrange("p (j q) -> p j q", j=2) if pairs else psO[:, v % 2, 0:P]
                    w = (k - 3) // 2 if isinstance(k, int) else 2 * I + (u - 3) // 2
                    nc.vector.tensor_copy(out_of(w, v % 2), src).then_inc(stored, 1)

            over_steps(dve, body)



class Norm:

    def __init__(self, nc, consts, st, name):
        self.nc = nc
        self.R = st.sb(name + "_R", [P, NT, D])
        self.stats = st.sb(name + "_stats", [P, NT, 6])
        self.mv = st.sb(name + "_mv", [P, NT, 2])
        self.std = st.sb(name + "_std", [P, NT])
        self.rstd = st.sb(name + "_rstd", [P, NT])
        self.eps = consts["eps"]
        self.has_var = st.sem(name + "_has_var")
        self.has_std = st.sem(name + "_has_std")
        self.chain_sem = st.sem(name + "_dve")
        self.normed = st.sem(name + "_normed")

    def begin(self, dve):
        self.chain = Chain(dve, self.chain_sem)

    def stat(self, t):
        self.chain.link(self.nc.vector.bn_stats(self.stats[:, t, :], self.R[:, t, :]))
        last = self.nc.vector.bn_aggr(self.mv[:, t, :], self.stats[:, t, :])
        if t == NT - 1:
            last.then_inc(self.has_var, 1)

    def root(self, act):
        act.wait_ge(self.has_var, 1)
        self.nc.scalar.activation(self.std[:, :], self.mv[:, :, 1], ACT.Sqrt,
                                  bias=self.eps[:, 0:1]).then_inc(self.has_std, 1)

    def apply(self, dve, out):
        dve.wait_ge(self.has_std, 1)
        self.chain.link(self.nc.vector.reciprocal(self.rstd[:, :], self.std[:, :]))
        for t in range(NT):
            self.nc.vector.tensor_scalar(out[:, t, :], self.R[:, t, :], self.mv[:, t, 0:1],
                                         self.rstd[:, t:t + 1], ALU.subtract,
                                         ALU.mult).then_inc(self.normed, 1)


def staggered(stages):
    for time in range(NT + len(stages) - 1):
        for s in reversed(range(len(stages))):
            if 0 <= time - s < NT and stages[s] is not None:
                stages[s](time - s)



def project_0(nc, c, XT, W0, QT, KT, V, loads):
    with ExitStack() as stack:
        st = Store(nc, stack)
        ps = st.ps("p0_ps", [P, 8, 512])
        T1 = st.sb("p0_T1", [P, 2, 512])
        T2 = st.sb("p0_T2", [P, 2, 512])
        made = st.sem("p0_made")
        rot = st.sem("p0_rot")
        roped = st.sem("p0_roped")
        v_made = st.sem("p0_v_made")
        v_kept = st.sem("p0_v_kept")
        block = stack.enter_context(nc.Block())
        jobs = [(a, half, n) for a in range(2) for half in range(KD) for n in range(2)]

        @block.tensor
        def _(pe):
            pe.wait_ge(loads["w0"], 16)
            pe.wait_ge(loads["xT"], 16)
            for i, (a, half, n) in enumerate(jobs):
                need(pe, rot, 2 * (i - 1))
                for sw in range(2):
                    for k in range(KD):
                        last = nc.tensor.matmul(ps[:, 2 * (i % 2) + sw, :],
                                                W0[:, 2 * a + sw, k, half * P:(half + 1) * P],
                                                XT[:, k, n * 512:(n + 1) * 512],
                                                start=(k == 0), stop=(k == KD - 1))
                last.then_inc(made, 1)
            for t in range(NT):
                need(pe, v_kept, t - 3)
                for k in range(KD):
                    last = nc.tensor.matmul(ps[:, 4 + t % 4, 0:D], XT[:, k, t * P:(t + 1) * P],
                                            W0[:, 4, k, :], start=(k == 0), stop=(k == KD - 1))
                last.then_inc(v_made, 1)

        @block.vector
        def _(dve):
            dve.wait_ge(loads["consts"], 16)
            for i, (a, half, n) in enumerate(jobs):
                dve.wait_ge(made, i + 1)
                need(dve, roped, i - 1)
                for sw, T, table in ((0, T1, c["cos0"]), (1, T2, c["sin0"])):
                    nc.vector.tensor_tensor(
                        T[:, i % 2, :].rearrange("p (b s) -> p b s", b=2),
                        ps[:, 2 * (i % 2) + sw, :].rearrange("p (b s) -> p b s", b=2),
                        table.unsqueeze(1).to_broadcast([P, 2, S]), ALU.mult).then_inc(rot, 1)

        @block.gpsimd
        def _(pool):
            for i, (a, half, n) in enumerate(jobs):
                pool.wait_ge(rot, 2 * (i + 1))
                out = (QT, KT)[a].rearrange("p (b h) s -> p b h s", h=KD)[:, 2 * n:2 * n + 2, half, :]
                pool.tensor_tensor(out, T1[:, i % 2, :].rearrange("p (b s) -> p b s", b=2),
                                   T2[:, i % 2, :].rearrange("p (b s) -> p b s", b=2),
                                   ALU.add).then_inc(roped, 1)

        @block.scalar
        def _(act):
            for t in range(NT):
                act.wait_ge(v_made, t + 1)
                out = V.rearrange("p (b g) k c -> p b g k c", g=4)[:, t // 2, :, t % 2, :]
                nc.scalar.activation(out, ps[:, 4 + t % 4, 0:D].rearrange("p (g c) -> p g c", g=4),
                                     ACT.Copy).then_inc(v_kept, 1)


def output_norm(nc, c, name, X, product, tiles_in=None):
    with ExitStack() as stack:
        st = Store(nc, stack)
        ps = st.ps(name + "_ps", [P, 4, 512])
        ln = Norm(nc, c, st, name)
        made = st.sem(name + "_made")
        taken = st.sem(name + "_taken")
        block = stack.enter_context(nc.Block())

        @block.tensor
        def _(pe):
            for t in range(NT):
                need(pe, taken, t - 3)
                product(pe, ps[:, t % 4, 0:D], t).then_inc(made, 1)

        @block.vector
        def _(dve):
            ln.begin(dve)
            for t in range(NT):
                dve.wait_ge(made, t + 1)
                nc.vector.tensor_tensor(ln.R[:, t, :], ps[:, t % 4, 0:D], X[:, t, :],
                                        ALU.add).then_inc(taken, 1)
                dve.wait_ge(taken, t + 1)
                ln.stat(t)
            ln.apply(dve, X)

        @block.scalar
        def _(act):
            ln.root(act)


def cross_norm(nc, c, X, Y, gamma):
    with ExitStack() as stack:
        st = Store(nc, stack)
        ln = Norm(nc, c, st, "lx")
        block = stack.enter_context(nc.Block())

        @block.vector
        def _(dve):
            ln.begin(dve)
            for t in range(NT):
                ln.chain.link(nc.vector.scalar_tensor_tensor(
                    out=ln.R[:, t, :], in0=Y[:, t, :], scalar=gamma[:, 0:1], in1=X[:, t, :],
                    op0=ALU.mult, op1=ALU.add))
                ln.stat(t)
            ln.apply(dve, X)

        @block.scalar
        def _(act):
            ln.root(act)



def feed_forward_0(nc, c, X, HAD, WU, WD, loads):
    with ExitStack() as stack:
        st = Store(nc, stack)
        TU = st.sb("ff_TU", [P, KD, I0], BF16)
        TD = st.sb("ff_TD", [P, I0 // P, D], BF16)
        wtmp = st.sb("ff_wtmp", [P, 2, 1024])
        wabs = st.sb("ff_wabs", [P, 2])
        wsc = st.sb("ff_wsc", [P, 2])
        winv = st.sb("ff_winv", [P, 2])
        xt = st.sb("ff_xt", [P, KD, P])
        q1 = st.sb("ff_q1", [P, D])
        q1b = st.sb("ff_q1b", [P, D], BF16)
        q1T = st.sb("ff_q1T", [P, KD, P], BF16)
        hr = st.sb("ff_hr", [P, I0])
        h = st.sb("ff_h", [P, I0])
        hT = st.sb("ff_hT", [P, 4, P])
        q2 = st.sb("ff_q2", [P, I0])
        q2b = st.sb("ff_q2b", [P, I0], BF16)
        q2T = st.sb("ff_q2T", [P, 4, P], BF16)
        am = st.sb("ff_am", [P, 2, NT])
        m1 = st.sb("ff_m1", [P, 2, NT])
        rc = st.sb("ff_rc", [P, 2, NT])
        sc = st.sb("ff_sc", [P, 2, NT])
        dq = st.sb("ff_dq", [P, 2, NT])
        psX = st.ps("ff_psX", [P, 512])
        psR = st.ps("ff_psR", [P, 512])
        psQ = st.ps("ff_psQ", [P, 1024], BF16)
        psU = st.ps("ff_psU", [P, 512])
        psH = st.ps("ff_psH", [P, 4, P])
        psR2 = st.ps("ff_psR2", [P, 512])
        psQ2 = st.ps("ff_psQ2", [P, 1024], BF16)
        psY = st.ps("ff_psY", [P, 512])
        ln = Norm(nc, c, st, "ff")
        s = {n: st.sem("ff_" + n) for n in (
            "wabs", "wmean", "wq", "xT", "xt", "rot", "q1", "q1b", "q1T", "q1Tc", "up", "hr", "h",
            "hT", "hTc", "rot2", "q2", "q2b", "q2T", "q2Tc", "down", "taken")}
        ident, identb, ones = c["ident"], c["identb"], c["ones"]
        rd0 = 1.0 / 16.0
        rd1 = c["rsqrt512"]
        block = stack.enter_context(nc.Block())

        @block.tensor
        def _(pe):
            pe.wait_ge(s["wabs"], 1)
            nc.tensor.matmul(psY[:, 0:2], ones[:, :], wabs[:, :], start=True,
                             stop=True).then_inc(s["wmean"], 1)
            pe.wait_ge(loads["had"], 16)
            pe.wait_ge(s["wq"], 1)

            def x_turn(t):
                need(pe, s["xt"], t)
                for k in range(KD):
                    last = nc.tensor.transpose(psX[:, k * P:(k + 1) * P],
                                               X[:, t, k * P:(k + 1) * P], ident[:, :])
                last.then_inc(s["xT"], 1)

            def rotate(t):
                pe.wait_ge(s["xt"], t + 1)
                need(pe, s["q1"], t)
                for k in range(KD):
                    last = nc.tensor.matmul(psR[:, 0:D], xt[:, k, :], HAD[:, k, 0:D],
                                            start=(k == 0), stop=(k == KD - 1))
                last.then_inc(s["rot"], 1)

            def q_turn(t):
                pe.wait_ge(s["q1b"], t + 1)
                need(pe, s["q1Tc"], t)
                for k in range(KD):
                    last = nc.tensor.transpose(psQ[:, k * P:(k + 1) * P],
                                               q1b[:, k * P:(k + 1) * P], identb[:, :])
                last.then_inc(s["q1T"], 1)

            def up(t):
                pe.wait_ge(s["q1Tc"], t + 1)
                need(pe, s["hr"], t)
                for k in range(KD):
                    last = nc.tensor.matmul(psU[:, :], q1T[:, k, :], TU[:, k, :],
                                            start=(k == 0), stop=(k == KD - 1))
                last.then_inc(s["up"], 1)

            def h_turn(t):
                pe.wait_ge(s["h"], t + 1)
                need(pe, s["hTc"], t)
                for k in range(4):
                    last = nc.tensor.transpose(psH[:, k, :], h[:, k * P:(k + 1) * P], ident[:, :])
                last.then_inc(s["hT"], 1)

            def rotate2(t):
                pe.wait_ge(s["hTc"], t + 1)
                need(pe, s["q2"], t)
                for k in range(4):
                    last = nc.tensor.matmul(psR2[:, :], hT[:, k, :], HAD[:, k, :],
                                            start=(k == 0), stop=(k == 3))
                last.then_inc(s["rot2"], 1)

            def q2_turn(t):
                pe.wait_ge(s["q2b"], t + 1)
                need(pe, s["q2Tc"], t)
                for k in range(4):
                    last = nc.tensor.transpose(psQ2[:, k * P:(k + 1) * P],
                                               q2b[:, k * P:(k + 1) * P], identb[:, :])
                last.then_inc(s["q2T"], 1)

            def down(t):
                pe.wait_ge(s["q2Tc"], t + 1)
                need(pe, s["taken"], t)
                for k in range(4):
                    last = nc.tensor.matmul(psY[:, 0:D], q2T[:, k, :], TD[:, k, :],
                                            start=(k == 0), stop=(k == 3))
                last.then_inc(s["down"], 1)

            staggered([x_turn, rotate, q_turn, up, h_turn, rotate2, q2_turn, down])

        @block.scalar
        def _(act):
            def keep_xt(t):
                act.wait_ge(s["xT"], t + 1)
                need(act, s["rot"], t)
                nc.scalar.activation(xt[:, :, :], psX[:, 0:D].rearrange("p (k t) -> p k t", k=KD),
                                     ACT.Copy).then_inc(s["xt"], 1)

            def round1(t):
                act.wait_ge(s["q1"], t + 1)
                need(act, s["q1T"], t)
                nc.scalar.activation(q1b[:, :], q1[:, :], ACT.Copy, bias=-MAGIC).then_inc(s["q1b"], 1)

            def keep_q1(t):
                act.wait_ge(s["q1T"], t + 1)
                need(act, s["up"], t)
                nc.scalar.activation(q1T[:, :, :], psQ[:, 0:D].rearrange("p (k t) -> p k t", k=KD),
                                     ACT.Copy).then_inc(s["q1Tc"], 1)

            def relu(t):
                act.wait_ge(s["up"], t + 1)
                need(act, s["h"], t)
                nc.scalar.activation(hr[:, :], psU[:, :], ACT.Relu,
                                     scale=dq[:, 0, t:t + 1]).then_inc(s["hr"], 1)

            def keep_h(t):
                act.wait_ge(s["hT"], t + 1)
                need(act, s["rot2"], t)
                nc.scalar.activation(hT[:, :, :], psH[:, :, :], ACT.Copy).then_inc(s["hTc"], 1)

            def round2(t):
                act.wait_ge(s["q2"], t + 1)
                need(act, s["q2T"], t)
                nc.scalar.activation(q2b[:, :], q2[:, :], ACT.Copy, bias=-MAGIC).then_inc(s["q2b"], 1)

            def keep_q2(t):
                act.wait_ge(s["q2T"], t + 1)
                need(act, s["down"], t)
                nc.scalar.activation(q2T[:, :, :], psQ2[:, 0:I0].rearrange("p (k t) -> p k t", k=4),
                                     ACT.Copy).then_inc(s["q2Tc"], 1)

            staggered([keep_xt, round1, keep_q1, relu, keep_h, round2, keep_q2])
            ln.root(act)

        @block.gpsimd
        def _(pool):
            for t in range(NT):
                pool.wait_ge(s["hr"], t + 1)
                need(pool, s["hT"], t)
                pool.tensor_tensor(h[:, :], hr[:, :], hr[:, :], ALU.mult).then_inc(s["h"], 1)

        @block.vector
        def _(dve):
            ln.begin(dve)
            link = ln.chain.link
            dve.wait_ge(loads["wff"], 32)
            flat = [WU.rearrange("p k n -> p (k n)"), WD.rearrange("p k n -> p (k n)")]
            for i in range(2):
                last = nc.vector.tensor_reduce(wabs[:, i:i + 1], flat[i], AX.X, ALU.add,
                                               apply_absolute_value=True)
            last.then_inc(s["wabs"], 1)
            dve.wait_ge(s["wmean"], 1)
            link(nc.vector.tensor_scalar(wsc[:, :], psY[:, 0:2], 1.0 / (D * I0), 1e-5, ALU.mult, ALU.max))
            link(nc.vector.reciprocal(winv[:, :], wsc[:, :]))
            for i in range(2):
                link(nc.vector.tensor_scalar(wtmp[:, i, :], flat[i], winv[:, i:i + 1], 1.0,
                                             ALU.mult, ALU.min))
                link(nc.vector.tensor_scalar(wtmp[:, i, :], wtmp[:, i, :], -1.0, MAGIC,
                                             ALU.max, ALU.add))
                out = (TU, TD)[i][:, :, :].rearrange("p k n -> p (k n)")
                last = nc.vector.tensor_scalar(out, wtmp[:, i, :], MAGIC, None, ALU.subtract)
            last.then_inc(s["wq"], 1)

            def quantise(i, t, src, out, norm, done):
                link(nc.vector.tensor_reduce(am[:, i, t:t + 1], src, AX.X, ALU.max,
                                             apply_absolute_value=True))
                link(nc.vector.tensor_scalar(m1[:, i, t:t + 1], am[:, i, t:t + 1], norm, 1e-5,
                                             ALU.mult, ALU.max))
                link(nc.vector.reciprocal(rc[:, i, t:t + 1], m1[:, i, t:t + 1]))
                nc.vector.tensor_scalar(dq[:, i, t:t + 1], m1[:, i, t:t + 1], wsc[:, i:i + 1],
                                        1.0 / 127.0, ALU.mult, ALU.mult)
                link(nc.vector.tensor_scalar(sc[:, i, t:t + 1], rc[:, i, t:t + 1], 127.0, norm,
                                             ALU.mult, ALU.mult))
                link(nc.vector.tensor_scalar(out, src, sc[:, i, t:t + 1], 127.0, ALU.mult, ALU.min))
                nc.vector.tensor_scalar(out, out, -127.0, MAGIC, ALU.max, ALU.add).then_inc(done, 1)

            def quantise1(t):
                dve.wait_ge(s["rot"], t + 1)
                need(dve, s["q1b"], t)
                quantise(0, t, psR[:, 0:D], q1[:, :], rd0, s["q1"])

            def quantise2(t):
                dve.wait_ge(s["rot2"], t + 1)
                need(dve, s["q2b"], t)
                quantise(1, t, psR2[:, :], q2[:, :], rd1, s["q2"])

            def take(t):
                dve.wait_ge(s["down"], t + 1)
                nc.vector.scalar_tensor_tensor(out=ln.R[:, t, :], in0=psY[:, 0:D],
                                               scalar=dq[:, 1, t:t + 1], in1=X[:, t, :],
                                               op0=ALU.mult, op1=ALU.add).then_inc(s["taken"], 1)
                dve.wait_ge(s["taken"], t + 1)
                ln.stat(t)

            staggered([None, quantise1, None, None, None, quantise2, None, take])
            ln.apply(dve, X)



def project_1(nc, c, X, W1, BIAS, QT, KT, V, loads):
    CH = (NQ1 + 2 * NKV1) // 512
    with ExitStack() as stack:
        st = Store(nc, stack)
        xt = st.sb("p1_xt", [P, 2, KD, P])
        qs = st.sb("p1_qs", [P, 2, 512])
        T1 = st.sb("p1_T1", [P, 2, 512])
        T2 = st.sb("p1_T2", [P, 2, 512])
        qr = st.sb("p1_qr", [P, 2, 1024])
        ps = st.ps("p1_ps", [P, 2, 512])
        psX = st.ps("p1_psX", [P, 512])
        psT = st.ps("p1_psT", [P, 2, 2, 512])
        xT = st.sem("p1_xT")
        xk = st.sem("p1_xk")
        made = st.sem("p1_made")
        biased = st.sem("p1_biased")
        cosd = st.sem("p1_cosd")
        sind = st.sem("p1_sind")
        roped = st.sem("p1_roped")
        turned = st.sem("p1_turned")
        kept = st.sem("p1_kept")
        block = stack.enter_context(nc.Block())
        chunks = [(t, ch) for t in range(NT) for ch in range(CH)]
        rotary = [(t, ch) for t, ch in chunks if ch < CH - 1]
        seq = {tc: i for i, tc in enumerate(rotary)}
        w_of = lambda kv, t: kv * B + t // 2

        @block.tensor
        def _(pe):
            pe.wait_ge(loads["w1"], 16)

            def turn_x(t):
                need(pe, xk, t)
                for k in range(KD):
                    last = nc.tensor.transpose(psX[:, k * P:(k + 1) * P],
                                               X[:, t, k * P:(k + 1) * P], c["ident"][:, :])
                last.then_inc(xT, 1)

            def turn(r):
                t, ch = rotary[r]
                pe.wait_ge(roped, r + 1)
                need(pe, kept, r - 1)
                for j in range(4 if ch < 4 else 8):
                    last = nc.tensor.transpose(psT[:, r % 2, j // 4, (j % 4) * P:(j % 4 + 1) * P],
                                               qr[:, r % 2, j * P:(j + 1) * P], c["ident"][:, :])
                last.then_inc(turned, 1)

            turn_x(0)
            late = []
            for i, (t, ch) in enumerate(chunks):
                if ch == 0:
                    pe.wait_ge(xk, t + 1)
                need(pe, biased, i - 1)
                for k in range(KD):
                    last = nc.tensor.matmul(ps[:, i % 2, :], xt[:, t % 2, k, :],
                                            W1[:, k, ch * 512:(ch + 1) * 512],
                                            start=(k == 0), stop=(k == KD - 1))
                last.then_inc(made, 1)
                if ch == 2 and t + 1 < NT:
                    turn_x(t + 1)
                if (t, ch) in seq:
                    late.append(seq[(t, ch)])
                if len(late) > 2:
                    turn(late.pop(0))
            for r in late:
                turn(r)

        @block.scalar
        def _(act):
            def keep_x(t):
                act.wait_ge(xT, t + 1)
                need(act, made, (t - 1) * CH)
                nc.scalar.activation(xt[:, t % 2, :, :], psX[:, 0:D].rearrange("p (k t) -> p k t", k=KD),
                                     ACT.Copy).then_inc(xk, 1)

            keep_x(0)
            for r, (t, ch) in enumerate(rotary):
                if ch == 2 and t + 1 < NT:
                    keep_x(t + 1)
                act.wait_ge(turned, r + 1)
                at = slice((t % 2) * P, (t % 2 + 1) * P)
                if ch < 4:
                    for kv in range(2):
                        last = nc.scalar.activation(
                            QT[:, w_of(2 * ch + kv, t), :, at],
                            psT[:, r % 2, 0, kv * D:(kv + 1) * D].rearrange("p (j t) -> p j t", j=2),
                            ACT.Copy)
                else:
                    dst = KT.rearrange("p (v b) s -> p v b s", b=B)[:, :, t // 2, at]
                    last = nc.scalar.activation(dst, psT[:, r % 2, :, :].rearrange(
                        "p a (j t) -> p (a j) t", j=4), ACT.Copy)
                last.then_inc(kept, 1)

        @block.vector
        def _(dve):
            dve.wait_ge(loads["bias1"], 16)
            for i, (t, ch) in enumerate(chunks):
                dve.wait_ge(made, i + 1)
                if ch == CH - 1:
                    out = V.rearrange("p (v b) k d -> p v b k d", b=B)[:, :, t // 2, t % 2, :]
                    nc.vector.tensor_tensor(out, ps[:, i % 2, :].rearrange("p (v d) -> p v d", v=HKV),
                                            BIAS[:, ch * 512:(ch + 1) * 512].rearrange("p (v d) -> p v d", v=HKV),
                                            ALU.add).then_inc(biased, 1)
                    continue
                r = seq[(t, ch)]
                need(dve, cosd, r - 1)
                nc.vector.tensor_tensor(qs[:, r % 2, :], ps[:, i % 2, :], BIAS[:, ch * 512:(ch + 1) * 512],
                                        ALU.add).then_inc(biased, 1)
                dve.wait_ge(biased, i + 1)
                q = qs[:, r % 2, :].rearrange("p (h j e) -> p h j e", h=8, e=2)
                o = T2[:, r % 2, :].rearrange("p (h j e) -> p h j e", h=8, e=2)
                tab = c["sin1"][:, t % 2, :].rearrange("p (j e) -> p j e", e=2)
                for e in range(2):
                    last = nc.vector.tensor_tensor(
                        o[:, :, :, e], q[:, :, :, 1 - e],
                        tab[:, :, e].unsqueeze(1).to_broadcast([P, 8, 32]), ALU.mult)
                last.then_inc(sind, 1)
                dve.wait_ge(sind, r + 1)
                dve.wait_ge(cosd, r + 1)
                need(dve, turned, r - 1)
                if ch < 4:
                    nc.vector.tensor_tensor(qr[:, r % 2, 0:512], T1[:, r % 2, :], T2[:, r % 2, :],
                                            ALU.add).then_inc(roped, 1)
                else:
                    dup = qr[:, r % 2, :].rearrange("p (v a d) -> p v a d", v=HKV, a=2)
                    for a in range(2):
                        last = nc.vector.tensor_tensor(
                            dup[:, :, a, :], T1[:, r % 2, :].rearrange("p (v d) -> p v d", v=HKV),
                            T2[:, r % 2, :].rearrange("p (v d) -> p v d", v=HKV), ALU.add)
                    last.then_inc(roped, 1)

        @block.gpsimd
        def _(pool):
            for i, (t, ch) in enumerate(chunks):
                if (t, ch) not in seq:
                    continue
                r = seq[(t, ch)]
                pool.wait_ge(biased, i + 1)
                need(pool, roped, r - 1)
                pool.tensor_tensor(T1[:, r % 2, :].rearrange("p (h d) -> p h d", h=8),
                                   qs[:, r % 2, :].rearrange("p (h d) -> p h d", h=8),
                                   c["cos1"][:, t % 2, :].unsqueeze(1).to_broadcast([P, 8, D1]),
                                   ALU.mult).then_inc(cosd, 1)



def token_experts(nc, c, X, CT, TOK, loads):
    with ExitStack() as stack:
        st = Store(nc, stack)
        E = B
        tf = st.sb("te_tf", [P, NT])
        ge = st.sb("te_ge", [P, E + 1, NT])
        own = st.sb("te_own", [P, E, NT])
        xt = st.sb("te_xt", [P, KD, P])
        sg = st.sb("te_sg", [P, E, D])
        a = st.sb("te_a", [P, E, D])
        aT = st.sb("te_aT", [P, E * KD, P])
        psX = st.ps("te_psX", [P, 512])
        psH = st.ps("te_psH", [P, E, D])
        psA = st.ps("te_psA", [P, E * KD, P])
        psY = st.ps("te_psY", [P, 512])
        ln = Norm(nc, c, st, "te")
        s = {n: st.sem("te_" + n) for n in ("xT", "xt", "h", "sg", "a", "aT", "aTa", "aTv", "down", "taken")}
        block = stack.enter_context(nc.Block())

        @block.tensor
        def _(pe):
            pe.wait_ge(loads["ctxT"], 16)

            def x_turn(t):
                need(pe, s["xt"], t)
                for k in range(KD):
                    last = nc.tensor.transpose(psX[:, k * P:(k + 1) * P],
                                               X[:, t, k * P:(k + 1) * P], c["ident"][:, :])
                last.then_inc(s["xT"], 1)

            def up(t):
                pe.wait_ge(s["xt"], t + 1)
                need(pe, s["a"], t)
                for j in range(E // 2):
                    for k in range(KD):
                        last = nc.tensor.matmul(psH[:, 2 * j:2 * j + 2, :], xt[:, k, :],
                                                CT[:, 2 * j:2 * j + 2, k, :],
                                                start=(k == 0), stop=(k == KD - 1))
                last.then_inc(s["h"], 1)

            def a_turn(t):
                pe.wait_ge(s["a"], t + 1)
                need(pe, s["aTa"], t)
                need(pe, s["aTv"], t)
                for e in range(E):
                    for k in range(KD):
                        last = nc.tensor.transpose(psA[:, e * KD + k, :], a[:, e, k * P:(k + 1) * P],
                                                   c["ident"][:, :])
                last.then_inc(s["aT"], 1)

            def down(t):
                pe.wait_ge(s["aTa"], t + 1)
                pe.wait_ge(s["aTv"], t + 1)
                need(pe, s["taken"], t)
                for i in range(E * KD):
                    last = nc.tensor.matmul(psY[:, 0:D], aT[:, i, :], CT[:, i // KD, i % KD, :],
                                            start=(i == 0), stop=(i == E * KD - 1))
                last.then_inc(s["down"], 1)

            staggered([x_turn, up, a_turn, down])

        @block.scalar
        def _(act):
            def keep_xt(t):
                act.wait_ge(s["xT"], t + 1)
                need(act, s["h"], t)
                nc.scalar.activation(xt[:, :, :], psX[:, 0:D].rearrange("p (k t) -> p k t", k=KD),
                                     ACT.Copy).then_inc(s["xt"], 1)

            def silu(t):
                act.wait_ge(s["h"], t + 1)
                need(act, s["a"], t)
                nc.scalar.activation(sg[:, :, :], psH[:, :, :], ACT.Silu).then_inc(s["sg"], 1)

            def keep_a(t):
                act.wait_ge(s["aT"], t + 1)
                need(act, s["down"], t)
                nc.scalar.activation(aT[:, 0:E, :], psA[:, 0:E, :], ACT.Copy).then_inc(s["aTa"], 1)

            staggered([keep_xt, silu, keep_a])
            ln.root(act)

        @block.vector
        def _(dve):
            ln.begin(dve)
            link = ln.chain.link
            dve.wait_ge(loads["tok"], 16)
            link(nc.vector.tensor_copy(tf[:, :], TOK[:, :]))
            link(nc.vector.memset(ge[:, 0, :], 1.0))
            link(nc.vector.memset(ge[:, E, :], 0.0))
            for e in range(1, E):
                link(nc.vector.tensor_scalar(ge[:, e, :], tf[:, :], 3125.0 * e, None, ALU.is_ge))
            link(nc.vector.tensor_tensor(own[:, :, :], ge[:, 0:E, :], ge[:, 1:E + 1, :], ALU.subtract))

            def gated(t):
                dve.wait_ge(s["sg"], t + 1)
                need(dve, s["aT"], t)
                for e in range(E):
                    last = nc.vector.scalar_tensor_tensor(out=a[:, e, :], in0=psH[:, e, :],
                                                          scalar=own[:, e, t:t + 1], in1=sg[:, e, :],
                                                          op0=ALU.mult, op1=ALU.mult)
                last.then_inc(s["a"], 1)

            def keep_a(t):
                dve.wait_ge(s["aT"], t + 1)
                need(dve, s["down"], t)
                nc.vector.tensor_copy(aT[:, E:2 * E, :], psA[:, E:2 * E, :]).then_inc(s["aTv"], 1)

            def take(t):
                dve.wait_ge(s["down"], t + 1)
                nc.vector.tensor_tensor(ln.R[:, t, :], psY[:, 0:D], X[:, t, :],
                                        ALU.add).then_inc(s["taken"], 1)
                dve.wait_ge(s["taken"], t + 1)
                ln.stat(t)

            staggered([None, gated, keep_a, take])
            ln.apply(dve, X)



def route(nc, c, X, GW, XH, XL, CW, CWS, loads):
    with ExitStack() as stack:
        st = Store(nc, stack)
        XT = st.sb("ro_XT", [P, KD, NT, P])
        lg = st.sb("ro_lg", [P, NT, NE])
        nmx = st.sb("ro_nmx", [P, NT])
        ex = st.sb("ro_ex", [P, NT, NE])
        sc = st.sb("ro_sc", [P, NT, NE])
        top = st.sb("ro_top", [P, NT, 8])
        idx = st.sb("ro_idx", [P, NT, 8], U32)
        idf = st.sb("ro_idf", [P, NT, 8])
        sel = st.sb("ro_sel", [P, TOPK, NT, NE])
        tot = st.sb("ro_tot", [P, NT])
        inv = st.sb("ro_inv", [P, NT])
        psX = st.ps("ro_psX", [P, 2, 512])
        psL = st.ps("ro_psL", [P, 512])
        xT = st.sem("ro_xT")
        xt = st.sem("ro_xt")
        logits = st.sem("ro_logits")
        shift = st.sem("ro_shift")
        exped = st.sem("ro_exped")
        chain = st.sem("ro_dve")
        block = stack.enter_context(nc.Block())

        @block.tensor
        def _(pe):
            def turn(t):
                need(pe, xt, t - 1)
                for k in range(KD):
                    last = nc.tensor.transpose(psX[:, t % 2, k * P:(k + 1) * P],
                                               X[:, t, k * P:(k + 1) * P], c["ident"][:, :])
                last.then_inc(xT, 1)

            def logit(t):
                pe.wait_ge(xt, t + 1)
                if t == 0:
                    pe.wait_ge(loads["gate"], 16)
                for k in range(KD):
                    last = nc.tensor.matmul(psL[:, t * NE:(t + 1) * NE], XT[:, k, t, :], GW[:, k, :],
                                            start=(k == 0), stop=(k == KD - 1))
                if t == NT - 1:
                    last.then_inc(logits, 1)

            staggered([turn, logit])

        @block.scalar
        def _(act):
            for t in range(NT):
                act.wait_ge(xT, t + 1)
                nc.scalar.activation(XT[:, :, t, :], psX[:, t % 2, 0:D].rearrange("p (k t) -> p k t", k=KD),
                                     ACT.Copy).then_inc(xt, 1)
            act.wait_ge(shift, 1)
            nc.scalar.activation(sc[:, :, :], lg[:, :, :], ACT.Exp, scale=-1.0)
            for t in range(NT):
                last = nc.scalar.activation(ex[:, t, :], lg[:, t, :], ACT.Exp, bias=nmx[:, t:t + 1])
            last.then_inc(exped, 1)

        @block.vector
        def _(dve):
            link = Chain(dve, chain).link
            for t in range(NT):
                dve.wait_ge(xt, t + 1)
                link(nc.vector.tensor_copy(XH[:, :, t, :], XT[:, :, t, :]))
                nc.vector.tensor_tensor(XL[:, :, t, :], XT[:, :, t, :], XH[:, :, t, :].bitcast(F32),
                                        ALU.subtract)
            dve.wait_ge(logits, 1)
            link(nc.vector.tensor_copy(lg[:, :, :], psL[:, 0:NT * NE].rearrange("p (t e) -> p t e", t=NT)))
            nc.vector.tensor_reduce(nmx[:, :], lg[:, :, :], AX.X, ALU.max, negate=True).then_inc(shift, 1)
            dve.wait_ge(exped, 1)
            link(nc.vector.tensor_scalar(sc[:, :, :], sc[:, :, :], 1.0, None, ALU.add))
            link(nc.vector.reciprocal(sc[:, :, :], sc[:, :, :]))
            for t in range(NT):
                link(nc.vector.max(top[:, t, :], sc[:, t, :]))
                link(nc.vector.max_index(idx[:, t, :], top[:, t, :], sc[:, t, :]))
            link(nc.vector.tensor_copy(idf[:, :, :], idx[:, :, :]))
            for k in range(TOPK):
                link(nc.vector.tensor_tensor(sel[:, k, :, :],
                                             c["iota"].unsqueeze(1).to_broadcast([P, NT, NE]),
                                             idf[:, :, k:k + 1].to_broadcast([P, NT, NE]), ALU.is_equal))
            for k in range(1, TOPK):
                link(nc.vector.tensor_tensor(sel[:, 0, :, :], sel[:, 0, :, :], sel[:, k, :, :], ALU.add))
            link(nc.vector.tensor_tensor(ex[:, :, :], ex[:, :, :], sel[:, 0, :, :], ALU.mult))
            link(nc.vector.tensor_reduce(tot[:, :], ex[:, :, :], AX.X, ALU.add))
            link(nc.vector.reciprocal(inv[:, :], tot[:, :]))
            link(nc.vector.tensor_tensor(CW[:, :, :], ex[:, :, :],
                                         inv[:, :].unsqueeze(2).to_broadcast([P, NT, NE]), ALU.mult))
            pair = CW.rearrange("p t (c g) -> p t c g", g=2)
            link(nc.vector.tensor_tensor(CWS[:, :, :], pair[:, :, :, 0], pair[:, :, :, 1], ALU.add))
            link(nc.vector.tensor_scalar(CWS[:, :, :], CWS[:, :, :], SMALL_SCALE, None, ALU.mult))


F32R = mybir.dt.float32r
GE = 4


def experts(nc, c, name, XH, XL, CW, Y, w_in, w_out, count, width):
    NB = count // GE
    STEPS = NT * GE
    with ExitStack() as stack:
        st = Store(nc, stack)
        raw_in = st.sb(name + "_raw_in", [P, GE, KD, 2 * width])
        raw_out = st.sb(name + "_raw_out", [P, GE, D])
        WH = st.sb(name + "_WH", [P, 2, GE, KD, 2 * width], F32R)
        WL = st.sb(name + "_WL", [P, 2, GE, KD, 2 * width], F32R)
        DH = st.sb(name + "_DH", [P, 2, GE, D], F32R)
        DL = st.sb(name + "_DL", [P, 2, GE, D], F32R)
        sg = st.sb(name + "_sg", [P, 2, width])
        a = st.sb(name + "_a", [P, 4, width])
        ah = st.sb(name + "_ah", [P, 2, P], F32R)
        al = st.sb(name + "_al", [P, 2, P], F32R)
        psG = st.ps(name + "_psG", [P, 2, 512])
        psA = st.ps(name + "_psA", [P, 2, 512])
        psD = st.ps(name + "_psD", [P, 2, 512])
        loaded = st.sem(name + "_loaded")
        split = st.sem(name + "_split")
        split_own = st.sem(name + "_split_own")
        hidden = st.sem(name + "_hidden")
        gated = st.sem(name + "_gated")
        acted = st.sem(name + "_acted")
        turned = st.sem(name + "_turned")
        high = st.sem(name + "_high")
        low = st.sem(name + "_low")
        passed = st.sem(name + "_passed")
        downed = st.sem(name + "_downed")
        added = st.sem(name + "_added")
        block = stack.enter_context(nc.Block())

        def over_steps(eng, body):
            for u in range(STEPS):
                body(u, 0)
            with eng.Fori(1, NB) as I:
                for u in range(STEPS):
                    body(u, I)
            for u in range(3):
                body(u, NB)

        def lagging(u, I, lag):
            first = isinstance(I, int) and I == 0
            if first and u < lag or isinstance(I, int) and I == NB and u >= lag:
                return None
            J, v = (I, u - lag) if u >= lag else (I - 1, u - lag + STEPS)
            return J, v, J * STEPS + v

        @block.sync
        def _(sp):
            def load(I):
                need(sp, split, I)
                sp.dma_start(raw_in[:], w_in(I)).then_inc(loaded, 16)
                sp.dma_start(raw_out[0:width], w_out(I)).then_inc(loaded, 16)
            load(0)
            with sp.Fori(1, NB) as I:
                load(I)

        @block.gpsimd
        def _(pool):
            def part(I, r):
                pool.wait_ge(loaded, 32 * I + 32)
                need(pool, downed, (I - 1) * STEPS)
                hold(pool, passed)
                pool.tensor_copy(WH[:, r], raw_in[:]).then_inc(split_own, 1)
                pool.tensor_copy(DH[0:width, r], raw_out[0:width]).then_inc(split_own, 1)
                pool.wait_ge(split_own, 2 * I + 2)
                pool.tensor_tensor(WL[:, r], raw_in[:], WH[:, r].bitcast(F32), ALU.subtract)
                pool.tensor_tensor(DL[0:width, r], raw_out[0:width], DH[0:width, r].bitcast(F32),
                                   ALU.subtract).then_inc(split, 1)
            part(0, 0)
            part(1, 1)
            if NB > 2:
                with pool.Fori(1, NB // 2) as J:
                    part(2 * J, 0)
                    part(2 * J + 1, 1)

        @block.tensor
        def _(pe):
            def body(u, I):
                now = lagging(u, I, 0)
                if now:
                    t, e = u // GE, u % GE
                    k = now[2]
                    if u == 0:
                        pe.wait_ge(split, I + 1)
                    need(pe, acted, k - 1)
                    n = 0
                    for x, w in ((XH, WH), (XH, WL), (XL, WH)):
                        for kk in range(KD):
                            last = nc.tensor.matmul(psG[:, u % 2, 0:2 * width], x[:, kk, t, :],
                                                    w[:, I % 2, e, kk, :], start=(n == 0), stop=(n == 5))
                            n += 1
                    last.then_inc(hidden, 1)
                two = lagging(u, I, 2)
                if two:
                    J, v, j = two
                    pe.wait_ge(acted, j + 1)
                    need(pe, low, j - 1)
                    nc.tensor.transpose(psA[0:width, v % 2, 0:P], a[:, v % 4, :],
                                        c["ident"][:, :]).then_inc(turned, 1)
                three = lagging(u, I, 3)
                if three:
                    J, v, j = three
                    t, e = v // GE, v % GE
                    pe.wait_ge(low, j + 1)
                    if e == 0:
                        need(pe, added, J * NT + t - 1)
                    parts = ((ah, DH), (ah, DL), (al, DH))
                    for n, (x, w) in enumerate(parts):
                        last = nc.tensor.matmul(psD[:, t % 2, 0:D], x[0:width, v % 2, :],
                                                w[0:width, J % 2, e, :], start=(e == 0 and n == 0),
                                                stop=(e == GE - 1 and n == 2))
                    last.then_inc(downed, 1)

            over_steps(pe, body)

        @block.scalar
        def _(act):
            def body(u, I):
                now = lagging(u, I, 0)
                if now:
                    k = now[2]
                    act.wait_ge(hidden, k + 1)
                    need(act, acted, k - 1)
                    nc.scalar.activation(sg[:, u % 2, :], psG[:, u % 2, 0:width],
                                         ACT.Silu).then_inc(gated, 1)
                two = lagging(u, I, 2)
                if two:
                    J, v, j = two
                    act.wait_ge(turned, j + 1)
                    need(act, downed, j - 1)
                    nc.scalar.activation(ah[0:width, v % 2, :], psA[0:width, v % 2, 0:P],
                                         ACT.Copy).then_inc(high, 1)

            over_steps(act, body)

        @block.vector
        def _(dve):
            def body(u, I):
                now = lagging(u, I, 0)
                if now:
                    t, e = u // GE, u % GE
                    k = now[2]
                    dve.wait_ge(gated, k + 1)
                    need(dve, turned, k - 3)
                    nc.vector.scalar_tensor_tensor(
                        out=a[:, u % 4, :], in0=psG[:, u % 2, width:2 * width],
                        scalar=CW[:, t, bass.ds(I * GE + e, 1)], in1=sg[:, u % 2, :],
                        op0=ALU.mult, op1=ALU.mult).then_inc(acted, 1)
                two = lagging(u, I, 2)
                if two:
                    J, v, j = two
                    dve.wait_ge(high, j + 1)
                    nc.vector.tensor_tensor(al[0:width, v % 2, :], psA[0:width, v % 2, 0:P],
                                            ah[0:width, v % 2, :].bitcast(F32),
                                            ALU.subtract).then_inc(low, 1)
                three = lagging(u, I, 3)
                if three and three[1] % GE == GE - 1:
                    J, v, j = three
                    t = v // GE
                    dve.wait_ge(downed, j + 1)
                    nc.vector.tensor_tensor(Y[:, t, :], psD[:, t % 2, 0:D], Y[:, t, :],
                                            ALU.add).then_inc(added, 1)

            over_steps(dve, body)


def final_norm(nc, c, Y, out):
    with ExitStack() as stack:
        st = Store(nc, stack)
        ln = Norm(nc, c, st, "fn")
        X = st.sb("fn_X", [P, NT, D])
        written = st.sem("fn_written")
        block = stack.enter_context(nc.Block())

        @block.vector
        def _(dve):
            ln.begin(dve)
            for t in range(NT):
                ln.chain.link(nc.vector.tensor_copy(ln.R[:, t, :], Y[:, t, :]))
                ln.stat(t)
            ln.apply(dve, X)

        @block.scalar
        def _(act):
            ln.root(act)

        @block.sync
        def _(sp):
            for n in range(2):
                sp.wait_ge(ln.normed, 4 * n + 4)
                sp.dma_start(out[4 * n:4 * n + 4].rearrange("t p d -> p t d"),
                             X[:, 4 * n:4 * n + 4, :]).then_inc(written, 16)
            sp.wait_ge(written, 32)



TABLE = dict(ident=P, ones=P, hm=8, hx=4, pm=2, iota=NE, cos0=S, sin0=S, causal=2 * S, window=2 * S,
             cos1=2 * D1, sin1=2 * D1, eps=1)


def decoder(nc, x, xT, ctx, ctxT, tok, w0, wo0, gamma, wu, wd, had, w1, bias1, wo1, bo1, sinks, gate,
            w_in, w_out, c_in, c_out, table, out, stop=99):
    stack = ExitStack()
    with stack:
        Store.spent.clear()
        top = Store(nc, stack, passing=False)
        X = top.sb("X", [P, NT, D])
        TB = top.sb("table", [P, sum(TABLE.values())])
        identb = top.sb("identb", [P, P], BF16)
        CT = top.sb("CT", [P, B, KD, D])
        TOK = top.sb("TOK", [P, NT], mybir.dt.int32)
        GM = top.sb("GM", [P, 1])
        loads = {n: top.sem("load_" + n) for n in (
            "x", "xT", "w0", "consts", "ctx", "ctxT", "tok", "gamma", "wo0", "wff", "had", "w1",
            "bias1", "wo1", "gate")}
        c, at = {}, 0
        for n, width in TABLE.items():
            c[n] = TB[:, at:at + width]
            at += width
        for n in ("causal", "window"):
            c[n] = c[n].rearrange("p (h s) -> p h s", h=2)
        for n in ("cos1", "sin1"):
            c[n] = c[n].rearrange("p (h d) -> p h d", h=2)
        c["identb"] = identb
        c["rsqrt512"] = RSQRT512

        with ExitStack() as layer0:
            l0 = Store(nc, layer0)
            CTX = l0.sb("CTX", [P, NT, D])
            WO0 = l0.sb("WO0", [P, 4, D])
            WU = l0.sb("WU", [P, KD, I0])
            WD = l0.sb("WD", [P, I0 // P, D])
            HAD = l0.sb("HAD", [P, 4, I0])
            with ExitStack() as attn0:
                a0 = Store(nc, attn0)
                XT = a0.sb("XT", [P, KD, B * S])
                W0 = a0.sb("W0", [P, 5, KD, D])
                QT = a0.sb("QT", [P, B * KD, S])
                KT = a0.sb("KT", [P, B * KD, S])
                V = a0.sb("V", [P, 16, 2, 64])
                AT = a0.sb("AT", [P, 16, S])
                with nc.Block() as block:
                    @block.sync
                    def _(sp):
                        sp.dma_start(XT[:], xT.rearrange("(k p) s -> p k s", p=P)).then_inc(loads["xT"], 16)
                        sp.dma_start(W0[:], w0.rearrange("m (k p) o -> p (m k) o", p=P)).then_inc(loads["w0"], 16)
                        sp.dma_start(TB[:], table).then_inc(loads["consts"], 16)
                        sp.dma_start(X[:], x.rearrange("t p d -> p t d")).then_inc(loads["x"], 16)
                        sp.dma_start(WO0[:], wo0.rearrange("g p o -> p g o")).then_inc(loads["wo0"], 16)
                        sp.dma_start(WU[:], wu.rearrange("(k p) o -> p k o", p=P)).then_inc(loads["wff"], 16)
                        sp.dma_start(WD[:], wd.rearrange("(k p) o -> p k o", p=P)).then_inc(loads["wff"], 16)
                        sp.dma_start(HAD[:], had.rearrange("(k p) o -> p k o", p=P)).then_inc(loads["had"], 16)

                    @block.scalar
                    def _(act):
                        act.dma_start(CTX[:], ctx.rearrange("t p d -> p t d")).then_inc(loads["ctx"], 16)
                        act.dma_start(CT[:], ctxT.rearrange("b (k p) s -> p (b k) s", p=P)).then_inc(loads["ctxT"], 16)
                        act.dma_start(TOK[:], tok).then_inc(loads["tok"], 16)
                        act.dma_start(GM[:], gamma.to_broadcast([P, 1])).then_inc(loads["gamma"], 16)

                project_0(nc, c, XT, W0, QT, KT, V, loads)

                def stage_qk0(pool, Qs, KM, w, r, I):
                    at = w // 2 if isinstance(w, int) else I
                    pool.tensor_copy(Qs[:, 0, :], QT[:, at, :])
                    return spread(pool, KM, KT[:, at, :], c["hm"][:, 4 * r:4 * r + 4])

                def stage_v0(pool, Vs, w, r, I):
                    return pool.tensor_copy(Vs.rearrange("p k (h d) -> p k h d", h=4)[:, :, :, 0:DK0],
                                            V[:, w, :, :].rearrange("p k (h d) -> p k h d", h=4))

                attention(nc, c, "a0", 16, stage_qk0, stage_v0,
                          lambda w, half: AT[:, w, half * P:(half + 1) * P], width=32, pairs=False,
                          mask=c["causal"], causal=True, scale=0.25)

                def product0(pe, out, t):
                    if t == 0:
                        pe.wait_ge(loads["wo0"], 16)
                    for g in range(4):
                        last = nc.tensor.matmul(out, AT[:, (t // 2) * 4 + g, (t % 2) * P:(t % 2 + 1) * P],
                                                WO0[:, g, :], start=(g == 0), stop=(g == 3))
                    return last

                with nc.Block() as block:
                    @block.vector
                    def _(dve):
                        dve.wait_ge(loads["x"], 16)
                        nc.vector.tensor_copy(identb[:], c["ident"])
                output_norm(nc, c, "o0", X, product0)

            if stop > 1:
                with ExitStack() as attnx:
                    ax = Store(nc, attnx)
                    Y = ax.sb("Y", [P, NT, D])

                    def stage_qkx(pool, Qs, KM, w, r, I):
                        if isinstance(w, int) and w == 0:
                            pool.wait_ge(loads["ctx"], 16)
                            pool.wait_ge(loads["ctxT"], 16)
                        pool.tensor_copy(Qs[:, 0, :], X[:, w, :])
                        return spread(pool, KM, CTX[:, w, :], c["hx"])

                    def stage_vx(pool, Vs, w, r, I):
                        return pool.tensor_copy(Vs, CT[:, I, :, r * P:(r + 1) * P])

                    attention(nc, c, "ax", 8, stage_qkx, stage_vx,
                              lambda w, half: Y[:, w, half * P:(half + 1) * P], width=32, pairs=False,
                              scale=INV_SQRT32)
                    with nc.Block() as block:
                        @block.vector
                        def _(dve):
                            dve.wait_ge(loads["gamma"], 16)
                    cross_norm(nc, c, X, Y, GM)

            if stop > 2:
                feed_forward_0(nc, c, X, HAD, WU, WD, loads)

        recycle(nc)
        if stop > 3:
            with ExitStack() as layer1:
                l1 = Store(nc, layer1)
                BO1 = l1.sb("BO1", [P, D])
                SK = l1.sb("SK", [P, H1])
                NSK = l1.sb("NSK", [P, H1])
                QT1 = l1.sb("QT1", [P, 32, 2, S])
                KT1 = l1.sb("KT1", [P, 32, S])
                V1 = l1.sb("V1", [P, 32, 2, D1])
                with ExitStack() as proj1:
                    p1 = Store(nc, proj1)
                    W1 = p1.sb("W1", [P, KD, NQ1 + 2 * NKV1])
                    BIAS = p1.sb("BIAS", [P, NQ1 + 2 * NKV1])
                    with nc.Block() as block:
                        @block.sync
                        def _(sp):
                            sp.dma_start(W1[:], w1.rearrange("(k p) o -> p k o", p=P)).then_inc(loads["w1"], 16)
                            sp.dma_start(BIAS[:], bias1.to_broadcast([P, NQ1 + 2 * NKV1])).then_inc(loads["bias1"], 16)
                            sp.dma_start(SK[:], sinks.to_broadcast([P, H1])).then_inc(loads["x"], 16)
                            sp.dma_start(BO1[:], bo1.to_broadcast([P, D])).then_inc(loads["x"], 16)
                    project_1(nc, c, X, W1, BIAS, QT1, KT1, V1, loads)
                WO1 = l1.sb("WO1", [P, HKV, 2, D])
                with nc.Block() as block:
                    @block.sync
                    def _(sp):
                        sp.dma_start(WO1[:], wo1.rearrange("(v j p) o -> p (v j) o", p=P, j=2)).then_inc(loads["wo1"], 16)

                    @block.vector
                    def _(dve):
                        dve.wait_ge(loads["x"], 48)
                        nc.vector.tensor_scalar(NSK[:], SK[:], -1.0, None, ALU.mult)

                def stage_qk1(pool, Qs, KM, w, r, I):
                    pool.tensor_copy(Qs, QT1[:, w, :, :])
                    return spread(pool, KM, KT1[:, w, :], c["pm"])

                def stage_v1(pool, Vs, w, r, I):
                    return pool.tensor_copy(Vs, V1[:, w, :, :])

                def sinks_of(w, r, I):
                    at = bass.ds((I // 2) * 4, 4)
                    return SK[:, at], NSK[:, at]

                attention(nc, c, "a1", 32, stage_qk1, stage_v1,
                          lambda w, half: QT1[:, w, :, half * P:(half + 1) * P], width=64, pairs=True,
                          mask=c["window"], sinks_of=sinks_of)

                with nc.Block() as block:
                    add_bias = top.sem("bo_added")

                    @block.vector
                    def _(dve):
                        for t in range(NT):
                            nc.vector.tensor_tensor(X[:, t, :], X[:, t, :], BO1[:], ALU.add)

                def product1(pe, out, t):
                    if t == 0:
                        pe.wait_ge(loads["wo1"], 16)
                    for i in range(2 * HKV):
                        last = nc.tensor.matmul(
                            out, QT1[:, (i // 2) * B + t // 2, i % 2, (t % 2) * P:(t % 2 + 1) * P],
                            WO1[:, i // 2, i % 2, :], start=(i == 0), stop=(i == 2 * HKV - 1))
                    return last

                output_norm(nc, c, "o1", X, product1)

        if stop > 4:
            token_experts(nc, c, X, CT, TOK, loads)

        if stop > 5:
            with ExitStack() as moe:
                m = Store(nc, moe)
                GW = m.sb("GW", [P, KD, NE])
                XH = m.sb("XH", [P, KD, NT, P], F32R)
                XL = m.sb("XL", [P, KD, NT, P], F32R)
                CW = m.sb("CW", [P, NT, NE])
                CWS = m.sb("CWS", [P, NT, NC])
                with nc.Block() as block:
                    @block.sync
                    def _(sp):
                        sp.dma_start(GW[:], gate.rearrange("(k p) e -> p k e", p=P)).then_inc(loads["gate"], 16)
                route(nc, c, X, GW, XH, XL, CW, CWS, loads)
                wi = w_in.rearrange("(r e) (k p) n -> r p (e k) n", e=GE, p=P)
                wo = w_out.rearrange("(r e) p n -> r p e n", e=GE)
                experts(nc, c, "ex", XH, XL, CW, X, lambda I: wi[I], lambda I: wo[I], NE, INTER)
                ci = c_in.rearrange("(r e) (k p) n -> r p (e k) n", e=GE, p=P)
                co = c_out.rearrange("(r e) p n -> r p e n", e=GE)
                experts(nc, c, "ch", XH, XL, CWS, X, lambda I: ci[I], lambda I: co[I], NC, CINTER)
        if stop > 5:
            final_norm(nc, c, X, out)
        else:
            with nc.Block() as block:
                @block.sync
                def _(sp):
                    wr = top.sem("dbg")
                    sp.dma_start(out.rearrange("t p d -> p t d"), X[:]).then_inc(wr, 16)
                    sp.wait_ge(wr, 16)
                    for n in ("ctx", "ctxT", "tok", "gamma","wo0","had","w0","xT","x","consts"):
                        sp.wait_ge(loads[n],16)
                    sp.wait_ge(loads["wff"],32)


import numpy as np

RSQRT512 = float(np.float32(1.0) / np.sqrt(np.float32(512.0)))
INV_SQRT32 = float(np.float32(1.0) / np.sqrt(np.float32(32.0)))


def constants():
    f = np.float32
    part = np.arange(P)
    inv0 = f(1.0) / f(10000.0) ** (np.arange(0, DK0, 2, dtype=f) / f(DK0))
    ang0 = np.outer(np.arange(S, dtype=f), inv0).astype(f)
    row = (part % DK0) // 2
    sign = np.where(part % 2 == 0, -1.0, 1.0).astype(f)[:, None]
    inv1 = f(1.0) / f(150000.0) ** (np.arange(D1 // 2, dtype=f) * f(2.0) / f(D1))
    ang1 = (np.arange(S, dtype=f)[:, None] * inv1[None, :]).astype(f)
    scale1 = f(D1 ** (-0.25))
    cos1 = np.repeat(np.cos(ang1), 2, axis=-1) * scale1
    sin1 = np.repeat(np.sin(ang1), 2, axis=-1) * np.tile(np.array([-1, 1], f), D1 // 2) * scale1
    q, k = np.arange(S)[:, None], np.arange(S)[None, :]
    halves = lambda m: m.reshape(2, P, -1).transpose(1, 0, 2).reshape(P, -1)
    values = dict(
        ident=np.eye(P), ones=np.ones((P, P)), hm=part[:, None] // DK0 == np.arange(8),
        hx=part[:, None] // DX == np.arange(4), pm=part[:, None] // D1 == np.arange(2),
        iota=np.tile(np.arange(NE), (P, 1)), cos0=np.cos(ang0).T[row], sin0=np.sin(ang0).T[row] * sign,
        causal=halves(np.where(k <= q, 0.0, -1e30)), window=halves(np.where(abs(q - k) <= 128, 0.0, -1e30)),
        cos1=halves(cos1), sin1=halves(sin1), eps=np.full((P, 1), EPS))
    table = np.concatenate([np.asarray(values[n], f) for n in TABLE], axis=1)
    had = np.array([[1.0]], f)
    while had.shape[0] < I0:
        had = np.block([[had, had], [had, -had]])
    return np.ascontiguousarray(table), np.ascontiguousarray(had.astype(f))


def arrays_of(inputs):
    g = {n: np.asarray(a) for n, a in inputs.items()}
    x, ctx = g["x"], g["ctx_2048"]
    swap = np.arange(D) ^ 1
    wq, wk, wv = g["L0_attn_Wq"], g["L0_attn_Wk"], g["L0_attn_Wv"]
    wo0 = np.zeros((4, 4, 32, D), np.float32)
    wo0[:, :, 0:DK0] = g["L0_attn_Wo"].reshape(4, 4, DK0, D)
    flat = lambda a: a.reshape(D, -1)
    table, had = constants()
    return dict(
        x=x.reshape(NT, P, D), xT=x.reshape(B * S, D).T, ctx=ctx.reshape(NT, P, D),
        ctxT=ctx.transpose(0, 2, 1), tok=g["itok_BxS_13_99985"].reshape(NT, P).T,
        w0=np.stack([wq, wq[:, swap], wk, wk[:, swap], wv]), wo0=wo0.reshape(4, P, D),
        gamma=g["L0_xattn_gamma"].reshape(1, 1), wu=g["L0_ffn_w_up"].T, wd=g["L0_ffn_w_down"].T, had=had,
        w1=np.concatenate([flat(g["L1_attn_Wq"]), flat(g["L1_attn_Wk"]), flat(g["L1_attn_Wv"])], axis=1),
        bias1=np.concatenate([g["L1_attn_bq"].reshape(-1), g["L1_attn_bk"].reshape(-1),
                              g["L1_attn_bv"].reshape(-1)]).reshape(1, -1),
        wo1=g["L1_attn_Wo"].reshape(NQ1, D), bo1=g["L1_attn_bo"].reshape(1, D),
        sinks=g["L1_attn_sinks"].reshape(1, H1), gate=g["L1_ffn_gate_w"].T,
        w_in=np.concatenate([g["L1_ffn_Wg"], g["L1_ffn_Wu"]], axis=2), w_out=g["L1_ffn_Wd"],
        c_in=np.concatenate([g["L1_ffn_cWg"], g["L1_ffn_cWu"]], axis=2), c_out=g["L1_ffn_cWd"], table=table)


def kernel(**inputs):
    import concourse.bacc as bacc
    from concourse.bass_utils import run_bass_kernel_spmd

    nc = bacc.Bacc("TRN2", target_bir_lowering=False, num_devices=1)
    arrays, args = {}, []
    for name, a in arrays_of(inputs).items():
        a = np.ascontiguousarray(a)
        arrays["in_" + name] = a
        args.append(nc.dram_tensor("in_" + name, a.shape, mybir.dt.from_np(a.dtype), kind="ExternalInput").ap())
    out = nc.dram_tensor("out_0", (NT, P, D), F32, kind="ExternalOutput").ap()
    decoder(nc, *args, out)
    r = run_bass_kernel_spmd(nc, [arrays], core_ids=[0])
    return r.results[0]["out_0"].reshape(B, S, D)
```

```python
import concourse.bass as bass
from concourse import mybir
from contextlib import ExitStack

F32 = mybir.dt.float32
F32R = mybir.dt.float32r
BF16 = mybir.dt.bfloat16
U32 = mybir.dt.uint32
ALU = mybir.AluOpType
ACT = mybir.ActivationFunctionType
AX = mybir.AxisListType

B, S, D = 4, 256, 256
P = 128
NT = B * S // P
KD = D // P
H0, DK0 = 16, 16
HX, DX = 8, 32
I0 = 512
H1, HKV, D1 = 32, 8, 64
NQ1, NKV1 = H1 * D1, HKV * D1
NE, INTER = 32, 96
NC, CINTER = 16, 128
TOPK = 4
NTILE = TOPK * NT + NE
EPS = 1e-5
SMALL_SCALE = 0.05
MAGIC = 12582912.0


def need(eng, sem, value):
    if not (isinstance(value, int) and value <= 0):
        eng.wait_ge(sem, value)


def hold(eng, passed):
    eng.sem_inc(passed, 1)


class Chain:

    def __init__(self, eng, sem):
        self.eng, self.sem, self.n = eng, sem, 0

    def link(self, ins):
        self.n += 1
        ins.then_inc(self.sem, 1)
        self.eng.wait_ge(self.sem, self.n)


class Store:

    def __init__(self, nc, stack, passing=True):
        self.nc, self.stack, self.passing = nc, stack, passing

    def sb(self, name, shape, dt=F32):
        return self.stack.enter_context(self.nc.sbuf_tensor(name, shape, dt))

    def ps(self, name, shape, dt=F32):
        return self.stack.enter_context(self.nc.psum_tensor(name, shape, dt))

    spent = []

    def sem(self, name):
        sem = self.nc.alloc_semaphore(name)
        if self.passing:
            Store.spent.append(sem)
        return sem


def recycle(nc):
    nc.clear_and_free_semaphores(Store.spent)
    Store.spent.clear()
    nc.all_engine_barrier()



def spread(pool, KM, keys, heads):
    shape = [P, KM.shape[1], S]
    return pool.tensor_tensor(KM, keys.unsqueeze(1).to_broadcast(shape),
                              heads.unsqueeze(2).to_broadcast(shape), ALU.mult)


def attention(nc, consts, name, units, stage_qk, stage_v, out_of, *, width, pairs, mask=None, causal=False,
              scale=1.0, sinks_of=None):
    NB = units // 2
    with ExitStack() as stack:
        st = Store(nc, stack)
        nq = 2 if pairs else 1
        Qs = st.sb(name + "_Qs", [P, 2, nq, S])
        nk = 2 if pairs else 4
        KM = st.sb(name + "_KM", [P, 2, nk, S])
        Vs = st.sb(name + "_Vs", [P, 2, 2, 64 if pairs else 128])
        Sm = st.sb(name + "_Sm", [P, 2, 4, S])
        Pr = st.sb(name + "_Pr", [P, 4, 4, S])
        PT = st.sb(name + "_PT", [P, 2, 4, 2, P])
        mx = st.sb(name + "_mx", [P, 4, 4])
        nm = st.sb(name + "_nm", [P, 4, 4])
        den = st.sb(name + "_den", [P, 4, 4])
        rd = st.sb(name + "_rd", [P, 4, 4])
        sk = st.sb(name + "_sk", [P, 4, 4])
        es = st.sb(name + "_es", [P, 4, 4])
        psS = st.ps(name + "_psS", [P, 2, 4, S])
        psT = st.ps(name + "_psT", [P, 4, 2, P])
        psO = st.ps(name + "_psO", [P, 2, 512])
        staged = st.sem(name + "_staged")
        staged_v = st.sem(name + "_staged_v")
        scored = st.sem(name + "_scored")
        maxed = st.sem(name + "_maxed")
        shifted = st.sem(name + "_shifted")
        expd = st.sem(name + "_expd")
        summed = st.sem(name + "_summed")
        recip = st.sem(name + "_recip")
        normed = st.sem(name + "_normed")
        turned = st.sem(name + "_turned")
        copied_a = st.sem(name + "_copied_a")
        copied_v = st.sem(name + "_copied_v")
        mixed = st.sem(name + "_mixed")
        passed_p = st.sem(name + "_passed_p")
        passed_v = st.sem(name + "_passed_v")
        stored = st.sem(name + "_stored")
        ident = consts["ident"]
        block = stack.enter_context(nc.Block())

        def keys(u):
            return P if causal and u % 2 == 0 else S

        def over_steps(eng, body):
            for u in range(4):
                body(u, u, 0)
            with eng.Fori(1, NB) as I:
                for u in range(4):
                    body(I * 4 + u, u, I)
            for u in range(3):
                body(4 * NB + u, u, NB)

        def lags(k, u, I, lag):
            return not (isinstance(I, int) and I == 0) or u >= lag

        def current(I):
            return not (isinstance(I, int) and I == NB)

        @block.gpsimd
        def _(pool):
            pool.memset(Vs[:], 0.0).then_inc(staged_v, 1)
            pool.wait_ge(staged_v, 1)
            for w in range(2):
                stage_qk(pool, Qs[:, w], KM[:, w], w, w, 0).then_inc(staged, 1)

            def norm(k, u):
                pool.wait_ge(recip, k + 1)
                p = Pr[:, u % 4, :, 0:keys(u)]
                pool.tensor_tensor(p, p, rd[:, u % 4, :].unsqueeze(2).to_broadcast([P, 4, keys(u)]),
                                   ALU.mult).then_inc(normed, 1)

            def rounds(I, last_round):
                for u in range(4):
                    k = 4 * I + u
                    norm(k, u)
                    if u % 2 == 0:
                        need(pool, mixed, k - 2)
                        hold(pool, passed_p)
                        stage_v(pool, Vs[:, u // 2], 2 * I + u // 2, u // 2, I).then_inc(staged_v, 1)
                    elif not last_round:
                        pool.wait_ge(scored, k + 1)
                        hold(pool, passed_p)
                        stage_qk(pool, Qs[:, u // 2], KM[:, u // 2], 2 * I + 2 + u // 2, u // 2,
                                 I + 1).then_inc(staged, 1)

            rounds(0, False)
            if NB > 2:
                with pool.Fori(1, NB - 1) as I:
                    rounds(I, False)
            rounds(NB - 1, True)

        @block.tensor
        def _(pe):
            def body(k, u, I):
                if current(I):
                    if u % 2 == 0:
                        pe.wait_ge(staged, k // 2 + 1 if isinstance(k, int) else 2 * I + u // 2 + 1)
                    need(pe, shifted if mask is not None else expd, k - 1)
                    n = keys(u)
                    for j in range(2):
                        q = Qs[:, u // 2, j if pairs else 0, (u % 2) * P:(u % 2) * P + P]
                        ks = KM[:, u // 2, 0:2, 0:n] if pairs else KM[:, u // 2, 2 * j:2 * j + 2, 0:n]
                        last = nc.tensor.matmul(psS[:, u % 2, 2 * j:2 * j + 2, 0:n], q, ks,
                                                start=True, stop=True)
                    last.then_inc(scored, 1)
                if lags(k, u, I, 2) and (current(I) or u < 2):
                    v = (u - 2) % 4
                    pe.wait_ge(normed, k - 1)
                    need(pe, copied_a, k - 2)
                    need(pe, copied_v, k - 2)
                    for h in range(4):
                        for t in range(keys(v) // P):
                            last = nc.tensor.transpose(psT[:, h, t, :], Pr[:, v, h, t * P:t * P + P],
                                                       ident[:, :])
                    last.then_inc(turned, 1)
                if lags(k, u, I, 3):
                    v = (u - 3) % 4
                    pe.wait_ge(copied_a, k - 2)
                    pe.wait_ge(copied_v, k - 2)
                    if v % 2 == 0:
                        pe.wait_ge(staged_v, (k - 3) // 2 + 2 if isinstance(k, int)
                                   else 2 * I + (u - 3) // 2 + 2)
                    need(pe, stored, k - 4)
                    nt = keys(v) // P
                    for j in range(2 if pairs else 1):
                        for t in range(nt):
                            for c in range(2 if pairs else 4):
                                h = 2 * j + c if pairs else c
                                vs = (Vs[:, v // 2, t, 0:width] if pairs
                                      else Vs[:, v // 2, t, h * width:(h + 1) * width])
                                last = nc.tensor.matmul(
                                    psO[c * width:(c + 1) * width, v % 2, j * P:(j + 1) * P], vs,
                                    PT[:, v % 2, h, t, :], start=(t == 0), stop=(t == nt - 1))
                    last.then_inc(mixed, 1)

            over_steps(pe, body)

        @block.scalar
        def _(act):
            def body(k, u, I):
                if current(I):
                    act.wait_ge(shifted, k + 1)
                    need(act, turned, k - 3)
                    n = keys(u)
                    for h in range(4):
                        src = Sm[:, u % 2, h, 0:n] if mask is not None else psS[:, u % 2, h, 0:n]
                        last = nc.scalar.activation(Pr[:, u, h, 0:n], src, ACT.Exp,
                                                    bias=nm[:, u, h:h + 1], scale=scale,
                                                    accum_out=den[:, u, h:h + 1])
                    if sinks_of is not None:
                        last = nc.scalar.activation(es[:, u, :], sk[:, u, :], ACT.Exp)
                    last.then_inc(expd, 1)
                if lags(k, u, I, 2) and (current(I) or u < 2):
                    v = (u - 2) % 4
                    act.wait_ge(turned, k - 1)
                    need(act, mixed, k - 3)
                    n = keys(v) // P
                    nc.scalar.activation(PT[:, v % 2, 0:2, 0:n, :], psT[:, 0:2, 0:n, :],
                                         ACT.Copy).then_inc(copied_a, 1)

            over_steps(act, body)

        @block.vector
        def _(dve):
            def body(k, u, I):
                if current(I):
                    dve.wait_ge(scored, k + 1)
                    hold(dve, passed_v)
                    n = keys(u)
                    if mask is not None:
                        for h in range(4):
                            last = nc.vector.tensor_tensor_reduce(
                                out=Sm[:, u % 2, h, 0:n], in0=psS[:, u % 2, h, 0:n],
                                in1=mask[:, u % 2, 0:n], scale=1.0, scalar=-3.0e38, op0=ALU.add,
                                op1=ALU.max, accum_out=mx[:, u, h:h + 1])
                    else:
                        last = nc.vector.tensor_reduce(mx[:, u, :], psS[:, u % 2, :, :], AX.X, ALU.max)
                    last.then_inc(maxed, 1)
                    dve.wait_ge(maxed, (2 * k if sinks_of else k) + 1)
                    if sinks_of is None:
                        nc.vector.tensor_scalar(nm[:, u, :], mx[:, u, :], -scale, None,
                                                ALU.mult).then_inc(shifted, 1)
                    else:
                        sinks, negs = sinks_of(2 * I + u // 2, u // 2, I)
                        nc.vector.scalar_tensor_tensor(out=nm[:, u, :], in0=mx[:, u, :], scalar=-1.0,
                                                       in1=negs, op0=ALU.mult,
                                                       op1=ALU.min).then_inc(maxed, 1)
                        dve.wait_ge(maxed, 2 * k + 2)
                        nc.vector.tensor_tensor(sk[:, u, :], nm[:, u, :], sinks,
                                                ALU.add).then_inc(shifted, 1)
                if lags(k, u, I, 1) and (current(I) or u < 1):
                    v = (u - 1) % 4
                    dve.wait_ge(expd, k)
                    if sinks_of is not None:
                        nc.vector.tensor_tensor(den[:, v, :], den[:, v, :], es[:, v, :],
                                                ALU.add).then_inc(summed, 1)
                        dve.wait_ge(summed, k)
                    nc.vector.reciprocal(rd[:, v, :], den[:, v, :]).then_inc(recip, 1)
                if lags(k, u, I, 2) and (current(I) or u < 2):
                    v = (u - 2) % 4
                    dve.wait_ge(turned, k - 1)
                    need(dve, mixed, k - 3)
                    n = keys(v) // P
                    nc.vector.tensor_copy(PT[:, v % 2, 2:4, 0:n, :],
                                          psT[:, 2:4, 0:n, :]).then_inc(copied_v, 1)
                if lags(k, u, I, 3):
                    v = (u - 3) % 4
                    dve.wait_ge(mixed, k - 2)
                    src = psO[:, v % 2, 0:2 * P].rearrange("p (j q) -> p j q", j=2) if pairs else psO[:, v % 2, 0:P]
                    w = (k - 3) // 2 if isinstance(k, int) else 2 * I + (u - 3) // 2
                    nc.vector.tensor_copy(out_of(w, v % 2), src).then_inc(stored, 1)

            over_steps(dve, body)



class Norm:

    def __init__(self, nc, consts, st, name):
        self.nc = nc
        self.R = st.sb(name + "_R", [P, NT, D])
        self.stats = st.sb(name + "_stats", [P, NT, 6])
        self.mv = st.sb(name + "_mv", [P, NT, 2])
        self.std = st.sb(name + "_std", [P, NT])
        self.rstd = st.sb(name + "_rstd", [P, NT])
        self.eps = consts["eps"]
        self.has_var = st.sem(name + "_has_var")
        self.has_std = st.sem(name + "_has_std")
        self.chain_sem = st.sem(name + "_dve")
        self.normed = st.sem(name + "_normed")

    def begin(self, dve):
        self.chain = Chain(dve, self.chain_sem)

    def stat(self, t, last=None):
        self.chain.link(self.nc.vector.bn_stats(self.stats[:, t, :], self.R[:, t, :]))
        done = self.nc.vector.bn_aggr(self.mv[:, t, :], self.stats[:, t, :])
        if t == NT - 1 if last is None else last:
            done.then_inc(self.has_var, 1)

    def root(self, act):
        act.wait_ge(self.has_var, 1)
        self.nc.scalar.activation(self.std[:, :], self.mv[:, :, 1], ACT.Sqrt,
                                  bias=self.eps[:, 0:1]).then_inc(self.has_std, 1)

    def apply(self, dve, out):
        dve.wait_ge(self.has_std, 1)
        self.chain.link(self.nc.vector.reciprocal(self.rstd[:, :], self.std[:, :]))
        for t in range(NT):
            self.nc.vector.tensor_scalar(out[:, t, :], self.R[:, t, :], self.mv[:, t, 0:1],
                                         self.rstd[:, t:t + 1], ALU.subtract,
                                         ALU.mult).then_inc(self.normed, 1)


def staggered(stages):
    for time in range(NT + len(stages) - 1):
        for s in reversed(range(len(stages))):
            if 0 <= time - s < NT and stages[s] is not None:
                stages[s](time - s)



def project_0(nc, c, XT, W0, QT, KT, V, loads):
    with ExitStack() as stack:
        st = Store(nc, stack)
        ps = st.ps("p0_ps", [P, 8, 512])
        T1 = st.sb("p0_T1", [P, 2, 512])
        T2 = st.sb("p0_T2", [P, 2, 512])
        made = st.sem("p0_made")
        rot = st.sem("p0_rot")
        roped = st.sem("p0_roped")
        v_made = st.sem("p0_v_made")
        v_kept = st.sem("p0_v_kept")
        block = stack.enter_context(nc.Block())
        jobs = [(a, half, n) for a in range(2) for half in range(KD) for n in range(2)]

        @block.tensor
        def _(pe):
            pe.wait_ge(loads["w0"], 16)
            pe.wait_ge(loads["xT"], 16)
            for i, (a, half, n) in enumerate(jobs):
                need(pe, rot, 2 * (i - 1))
                for sw in range(2):
                    for k in range(KD):
                        last = nc.tensor.matmul(ps[:, 2 * (i % 2) + sw, :],
                                                W0[:, 2 * a + sw, k, half * P:(half + 1) * P],
                                                XT[:, k, n * 512:(n + 1) * 512],
                                                start=(k == 0), stop=(k == KD - 1))
                last.then_inc(made, 1)
            for t in range(NT):
                need(pe, v_kept, t - 3)
                for k in range(KD):
                    last = nc.tensor.matmul(ps[:, 4 + t % 4, 0:D], XT[:, k, t * P:(t + 1) * P],
                                            W0[:, 4, k, :], start=(k == 0), stop=(k == KD - 1))
                last.then_inc(v_made, 1)

        @block.vector
        def _(dve):
            dve.wait_ge(loads["consts"], 16)
            for i, (a, half, n) in enumerate(jobs):
                dve.wait_ge(made, i + 1)
                need(dve, roped, i - 1)
                for sw, T, table in ((0, T1, c["cos0"]), (1, T2, c["sin0"])):
                    nc.vector.tensor_tensor(
                        T[:, i % 2, :].rearrange("p (b s) -> p b s", b=2),
                        ps[:, 2 * (i % 2) + sw, :].rearrange("p (b s) -> p b s", b=2),
                        table.unsqueeze(1).to_broadcast([P, 2, S]), ALU.mult).then_inc(rot, 1)

        @block.gpsimd
        def _(pool):
            for i, (a, half, n) in enumerate(jobs):
                pool.wait_ge(rot, 2 * (i + 1))
                out = (QT, KT)[a].rearrange("p (b h) s -> p b h s", h=KD)[:, 2 * n:2 * n + 2, half, :]
                pool.tensor_tensor(out, T1[:, i % 2, :].rearrange("p (b s) -> p b s", b=2),
                                   T2[:, i % 2, :].rearrange("p (b s) -> p b s", b=2),
                                   ALU.add).then_inc(roped, 1)

        @block.scalar
        def _(act):
            for t in range(NT):
                act.wait_ge(v_made, t + 1)
                out = V.rearrange("p (b g) k c -> p b g k c", g=4)[:, t // 2, :, t % 2, :]
                nc.scalar.activation(out, ps[:, 4 + t % 4, 0:D].rearrange("p (g c) -> p g c", g=4),
                                     ACT.Copy).then_inc(v_kept, 1)


def output_norm(nc, c, name, X, product, tiles_in=None):
    with ExitStack() as stack:
        st = Store(nc, stack)
        ps = st.ps(name + "_ps", [P, 4, 512])
        ln = Norm(nc, c, st, name)
        made = st.sem(name + "_made")
        taken = st.sem(name + "_taken")
        block = stack.enter_context(nc.Block())

        @block.tensor
        def _(pe):
            for t in range(NT):
                need(pe, taken, t - 3)
                product(pe, ps[:, t % 4, 0:D], t).then_inc(made, 1)

        @block.vector
        def _(dve):
            ln.begin(dve)
            for t in range(NT):
                dve.wait_ge(made, t + 1)
                nc.vector.tensor_tensor(ln.R[:, t, :], ps[:, t % 4, 0:D], X[:, t, :],
                                        ALU.add).then_inc(taken, 1)
                dve.wait_ge(taken, t + 1)
                ln.stat(t)
            ln.apply(dve, X)

        @block.scalar
        def _(act):
            ln.root(act)


def cross_norm(nc, c, X, Y, gamma):
    with ExitStack() as stack:
        st = Store(nc, stack)
        ln = Norm(nc, c, st, "lx")
        block = stack.enter_context(nc.Block())

        @block.vector
        def _(dve):
            ln.begin(dve)
            for t in range(NT):
                ln.chain.link(nc.vector.scalar_tensor_tensor(
                    out=ln.R[:, t, :], in0=Y[:, t, :], scalar=gamma[:, 0:1], in1=X[:, t, :],
                    op0=ALU.mult, op1=ALU.add))
                ln.stat(t)
            ln.apply(dve, X)

        @block.scalar
        def _(act):
            ln.root(act)



def feed_forward_0(nc, c, X, HAD, WU, WD, loads):
    with ExitStack() as stack:
        st = Store(nc, stack)
        TU = st.sb("ff_TU", [P, KD, I0], BF16)
        TD = st.sb("ff_TD", [P, I0 // P, D], BF16)
        wtmp = st.sb("ff_wtmp", [P, 2, 1024])
        wabs = st.sb("ff_wabs", [P, 2])
        wsc = st.sb("ff_wsc", [P, 2])
        winv = st.sb("ff_winv", [P, 2])
        xt = st.sb("ff_xt", [P, KD, P])
        q1 = st.sb("ff_q1", [P, D])
        q1b = st.sb("ff_q1b", [P, D], BF16)
        q1T = st.sb("ff_q1T", [P, KD, P], BF16)
        hr = st.sb("ff_hr", [P, I0])
        h = st.sb("ff_h", [P, I0])
        hT = st.sb("ff_hT", [P, 4, P])
        q2 = st.sb("ff_q2", [P, I0])
        q2b = st.sb("ff_q2b", [P, I0], BF16)
        q2T = st.sb("ff_q2T", [P, 4, P], BF16)
        am = st.sb("ff_am", [P, 2, NT])
        m1 = st.sb("ff_m1", [P, 2, NT])
        rc = st.sb("ff_rc", [P, 2, NT])
        sc = st.sb("ff_sc", [P, 2, NT])
        dq = st.sb("ff_dq", [P, 2, NT])
        psX = st.ps("ff_psX", [P, 512])
        psR = st.ps("ff_psR", [P, 512])
        psQ = st.ps("ff_psQ", [P, 1024], BF16)
        psU = st.ps("ff_psU", [P, 512])
        psH = st.ps("ff_psH", [P, 4, P])
        psR2 = st.ps("ff_psR2", [P, 512])
        psQ2 = st.ps("ff_psQ2", [P, 1024], BF16)
        psY = st.ps("ff_psY", [P, 512])
        ln = Norm(nc, c, st, "ff")
        s = {n: st.sem("ff_" + n) for n in (
            "wabs", "wmean", "wq", "xT", "xt", "rot", "q1", "q1b", "q1T", "q1Tc", "up", "hr", "h",
            "hT", "hTc", "rot2", "q2", "q2b", "q2T", "q2Tc", "down", "taken")}
        ident, identb, ones = c["ident"], c["identb"], c["ones"]
        rd0 = 1.0 / 16.0
        rd1 = c["rsqrt512"]
        block = stack.enter_context(nc.Block())

        @block.tensor
        def _(pe):
            pe.wait_ge(s["wabs"], 1)
            nc.tensor.matmul(psY[:, 0:2], ones[:, :], wabs[:, :], start=True,
                             stop=True).then_inc(s["wmean"], 1)
            pe.wait_ge(loads["had"], 16)
            pe.wait_ge(s["wq"], 1)

            def x_turn(t):
                need(pe, s["xt"], t)
                for k in range(KD):
                    last = nc.tensor.transpose(psX[:, k * P:(k + 1) * P],
                                               X[:, t, k * P:(k + 1) * P], ident[:, :])
                last.then_inc(s["xT"], 1)

            def rotate(t):
                pe.wait_ge(s["xt"], t + 1)
                need(pe, s["q1"], t)
                for k in range(KD):
                    last = nc.tensor.matmul(psR[:, 0:D], xt[:, k, :], HAD[:, k, 0:D],
                                            start=(k == 0), stop=(k == KD - 1))
                last.then_inc(s["rot"], 1)

            def q_turn(t):
                pe.wait_ge(s["q1b"], t + 1)
                need(pe, s["q1Tc"], t)
                for k in range(KD):
                    last = nc.tensor.transpose(psQ[:, k * P:(k + 1) * P],
                                               q1b[:, k * P:(k + 1) * P], identb[:, :])
                last.then_inc(s["q1T"], 1)

            def up(t):
                pe.wait_ge(s["q1Tc"], t + 1)
                need(pe, s["hr"], t)
                for k in range(KD):
                    last = nc.tensor.matmul(psU[:, :], q1T[:, k, :], TU[:, k, :],
                                            start=(k == 0), stop=(k == KD - 1))
                last.then_inc(s["up"], 1)

            def h_turn(t):
                pe.wait_ge(s["h"], t + 1)
                need(pe, s["hTc"], t)
                for k in range(4):
                    last = nc.tensor.transpose(psH[:, k, :], h[:, k * P:(k + 1) * P], ident[:, :])
                last.then_inc(s["hT"], 1)

            def rotate2(t):
                pe.wait_ge(s["hTc"], t + 1)
                need(pe, s["q2"], t)
                for k in range(4):
                    last = nc.tensor.matmul(psR2[:, :], hT[:, k, :], HAD[:, k, :],
                                            start=(k == 0), stop=(k == 3))
                last.then_inc(s["rot2"], 1)

            def q2_turn(t):
                pe.wait_ge(s["q2b"], t + 1)
                need(pe, s["q2Tc"], t)
                for k in range(4):
                    last = nc.tensor.transpose(psQ2[:, k * P:(k + 1) * P],
                                               q2b[:, k * P:(k + 1) * P], identb[:, :])
                last.then_inc(s["q2T"], 1)

            def down(t):
                pe.wait_ge(s["q2Tc"], t + 1)
                need(pe, s["taken"], t)
                for k in range(4):
                    last = nc.tensor.matmul(psY[:, 0:D], q2T[:, k, :], TD[:, k, :],
                                            start=(k == 0), stop=(k == 3))
                last.then_inc(s["down"], 1)

            staggered([x_turn, rotate, q_turn, up, h_turn, rotate2, q2_turn, down])

        @block.scalar
        def _(act):
            def keep_xt(t):
                act.wait_ge(s["xT"], t + 1)
                need(act, s["rot"], t)
                nc.scalar.activation(xt[:, :, :], psX[:, 0:D].rearrange("p (k t) -> p k t", k=KD),
                                     ACT.Copy).then_inc(s["xt"], 1)

            def round1(t):
                act.wait_ge(s["q1"], t + 1)
                need(act, s["q1T"], t)
                nc.scalar.activation(q1b[:, :], q1[:, :], ACT.Copy, bias=-MAGIC).then_inc(s["q1b"], 1)

            def keep_q1(t):
                act.wait_ge(s["q1T"], t + 1)
                need(act, s["up"], t)
                nc.scalar.activation(q1T[:, :, :], psQ[:, 0:D].rearrange("p (k t) -> p k t", k=KD),
                                     ACT.Copy).then_inc(s["q1Tc"], 1)

            def relu(t):
                act.wait_ge(s["up"], t + 1)
                need(act, s["h"], t)
                nc.scalar.activation(hr[:, :], psU[:, :], ACT.Relu,
                                     scale=dq[:, 0, t:t + 1]).then_inc(s["hr"], 1)

            def keep_h(t):
                act.wait_ge(s["hT"], t + 1)
                need(act, s["rot2"], t)
                nc.scalar.activation(hT[:, :, :], psH[:, :, :], ACT.Copy).then_inc(s["hTc"], 1)

            def round2(t):
                act.wait_ge(s["q2"], t + 1)
                need(act, s["q2T"], t)
                nc.scalar.activation(q2b[:, :], q2[:, :], ACT.Copy, bias=-MAGIC).then_inc(s["q2b"], 1)

            def keep_q2(t):
                act.wait_ge(s["q2T"], t + 1)
                need(act, s["down"], t)
                nc.scalar.activation(q2T[:, :, :], psQ2[:, 0:I0].rearrange("p (k t) -> p k t", k=4),
                                     ACT.Copy).then_inc(s["q2Tc"], 1)

            staggered([keep_xt, round1, keep_q1, relu, keep_h, round2, keep_q2])
            ln.root(act)

        @block.gpsimd
        def _(pool):
            for t in range(NT):
                pool.wait_ge(s["hr"], t + 1)
                need(pool, s["hT"], t)
                pool.tensor_tensor(h[:, :], hr[:, :], hr[:, :], ALU.mult).then_inc(s["h"], 1)

        @block.vector
        def _(dve):
            ln.begin(dve)
            link = ln.chain.link
            dve.wait_ge(loads["wff"], 32)
            flat = [WU.rearrange("p k n -> p (k n)"), WD.rearrange("p k n -> p (k n)")]
            for i in range(2):
                last = nc.vector.tensor_reduce(wabs[:, i:i + 1], flat[i], AX.X, ALU.add,
                                               apply_absolute_value=True)
            last.then_inc(s["wabs"], 1)
            dve.wait_ge(s["wmean"], 1)
            link(nc.vector.tensor_scalar(wsc[:, :], psY[:, 0:2], 1.0 / (D * I0), 1e-5, ALU.mult, ALU.max))
            link(nc.vector.reciprocal(winv[:, :], wsc[:, :]))
            for i in range(2):
                link(nc.vector.tensor_scalar(wtmp[:, i, :], flat[i], winv[:, i:i + 1], 1.0,
                                             ALU.mult, ALU.min))
                link(nc.vector.tensor_scalar(wtmp[:, i, :], wtmp[:, i, :], -1.0, MAGIC,
                                             ALU.max, ALU.add))
                out = (TU, TD)[i][:, :, :].rearrange("p k n -> p (k n)")
                last = nc.vector.tensor_scalar(out, wtmp[:, i, :], MAGIC, None, ALU.subtract)
            last.then_inc(s["wq"], 1)

            def quantise(i, t, src, out, norm, done):
                link(nc.vector.tensor_reduce(am[:, i, t:t + 1], src, AX.X, ALU.max,
                                             apply_absolute_value=True))
                link(nc.vector.tensor_scalar(m1[:, i, t:t + 1], am[:, i, t:t + 1], norm, 1e-5,
                                             ALU.mult, ALU.max))
                link(nc.vector.reciprocal(rc[:, i, t:t + 1], m1[:, i, t:t + 1]))
                nc.vector.tensor_scalar(dq[:, i, t:t + 1], m1[:, i, t:t + 1], wsc[:, i:i + 1],
                                        1.0 / 127.0, ALU.mult, ALU.mult)
                link(nc.vector.tensor_scalar(sc[:, i, t:t + 1], rc[:, i, t:t + 1], 127.0, norm,
                                             ALU.mult, ALU.mult))
                link(nc.vector.tensor_scalar(out, src, sc[:, i, t:t + 1], 127.0, ALU.mult, ALU.min))
                nc.vector.tensor_scalar(out, out, -127.0, MAGIC, ALU.max, ALU.add).then_inc(done, 1)

            def quantise1(t):
                dve.wait_ge(s["rot"], t + 1)
                need(dve, s["q1b"], t)
                quantise(0, t, psR[:, 0:D], q1[:, :], rd0, s["q1"])

            def quantise2(t):
                dve.wait_ge(s["rot2"], t + 1)
                need(dve, s["q2b"], t)
                quantise(1, t, psR2[:, :], q2[:, :], rd1, s["q2"])

            def take(t):
                dve.wait_ge(s["down"], t + 1)
                nc.vector.scalar_tensor_tensor(out=ln.R[:, t, :], in0=psY[:, 0:D],
                                               scalar=dq[:, 1, t:t + 1], in1=X[:, t, :],
                                               op0=ALU.mult, op1=ALU.add).then_inc(s["taken"], 1)
                dve.wait_ge(s["taken"], t + 1)
                ln.stat(t)

            staggered([None, quantise1, None, None, None, quantise2, None, take])
            ln.apply(dve, X)



def project_1(nc, c, X, W1, BIAS, QT, KT, V, loads):
    CH = (NQ1 + 2 * NKV1) // 512
    with ExitStack() as stack:
        st = Store(nc, stack)
        xt = st.sb("p1_xt", [P, 2, KD, P])
        qs = st.sb("p1_qs", [P, 2, 512])
        T1 = st.sb("p1_T1", [P, 2, 512])
        T2 = st.sb("p1_T2", [P, 2, 512])
        qr = st.sb("p1_qr", [P, 2, 1024])
        ps = st.ps("p1_ps", [P, 2, 512])
        psX = st.ps("p1_psX", [P, 512])
        psT = st.ps("p1_psT", [P, 2, 2, 512])
        xT = st.sem("p1_xT")
        xk = st.sem("p1_xk")
        made = st.sem("p1_made")
        biased = st.sem("p1_biased")
        cosd = st.sem("p1_cosd")
        sind = st.sem("p1_sind")
        roped = st.sem("p1_roped")
        turned = st.sem("p1_turned")
        kept = st.sem("p1_kept")
        block = stack.enter_context(nc.Block())
        chunks = [(t, ch) for t in range(NT) for ch in range(CH)]
        rotary = [(t, ch) for t, ch in chunks if ch < CH - 1]
        seq = {tc: i for i, tc in enumerate(rotary)}
        w_of = lambda kv, t: kv * B + t // 2

        @block.tensor
        def _(pe):
            pe.wait_ge(loads["w1"], 16)

            def turn_x(t):
                need(pe, xk, t)
                for k in range(KD):
                    last = nc.tensor.transpose(psX[:, k * P:(k + 1) * P],
                                               X[:, t, k * P:(k + 1) * P], c["ident"][:, :])
                last.then_inc(xT, 1)

            def turn(r):
                t, ch = rotary[r]
                pe.wait_ge(roped, r + 1)
                need(pe, kept, r - 1)
                for j in range(4 if ch < 4 else 8):
                    last = nc.tensor.transpose(psT[:, r % 2, j // 4, (j % 4) * P:(j % 4 + 1) * P],
                                               qr[:, r % 2, j * P:(j + 1) * P], c["ident"][:, :])
                last.then_inc(turned, 1)

            turn_x(0)
            late = []
            for i, (t, ch) in enumerate(chunks):
                if ch == 0:
                    pe.wait_ge(xk, t + 1)
                need(pe, biased, i - 1)
                for k in range(KD):
                    last = nc.tensor.matmul(ps[:, i % 2, :], xt[:, t % 2, k, :],
                                            W1[:, k, ch * 512:(ch + 1) * 512],
                                            start=(k == 0), stop=(k == KD - 1))
                last.then_inc(made, 1)
                if ch == 2 and t + 1 < NT:
                    turn_x(t + 1)
                if (t, ch) in seq:
                    late.append(seq[(t, ch)])
                if len(late) > 2:
                    turn(late.pop(0))
            for r in late:
                turn(r)

        @block.scalar
        def _(act):
            def keep_x(t):
                act.wait_ge(xT, t + 1)
                need(act, made, (t - 1) * CH)
                nc.scalar.activation(xt[:, t % 2, :, :], psX[:, 0:D].rearrange("p (k t) -> p k t", k=KD),
                                     ACT.Copy).then_inc(xk, 1)

            keep_x(0)
            for r, (t, ch) in enumerate(rotary):
                if ch == 2 and t + 1 < NT:
                    keep_x(t + 1)
                act.wait_ge(turned, r + 1)
                at = slice((t % 2) * P, (t % 2 + 1) * P)
                if ch < 4:
                    for kv in range(2):
                        last = nc.scalar.activation(
                            QT[:, w_of(2 * ch + kv, t), :, at],
                            psT[:, r % 2, 0, kv * D:(kv + 1) * D].rearrange("p (j t) -> p j t", j=2),
                            ACT.Copy)
                else:
                    dst = KT.rearrange("p (v b) s -> p v b s", b=B)[:, :, t // 2, at]
                    last = nc.scalar.activation(dst, psT[:, r % 2, :, :].rearrange(
                        "p a (j t) -> p (a j) t", j=4), ACT.Copy)
                last.then_inc(kept, 1)

        @block.vector
        def _(dve):
            dve.wait_ge(loads["bias1"], 16)
            for i, (t, ch) in enumerate(chunks):
                dve.wait_ge(made, i + 1)
                if ch == CH - 1:
                    out = V.rearrange("p (v b) k d -> p v b k d", b=B)[:, :, t // 2, t % 2, :]
                    nc.vector.tensor_tensor(out, ps[:, i % 2, :].rearrange("p (v d) -> p v d", v=HKV),
                                            BIAS[:, ch * 512:(ch + 1) * 512].rearrange("p (v d) -> p v d", v=HKV),
                                            ALU.add).then_inc(biased, 1)
                    continue
                r = seq[(t, ch)]
                need(dve, cosd, r - 1)
                nc.vector.tensor_tensor(qs[:, r % 2, :], ps[:, i % 2, :], BIAS[:, ch * 512:(ch + 1) * 512],
                                        ALU.add).then_inc(biased, 1)
                dve.wait_ge(biased, i + 1)
                q = qs[:, r % 2, :].rearrange("p (h j e) -> p h j e", h=8, e=2)
                o = T2[:, r % 2, :].rearrange("p (h j e) -> p h j e", h=8, e=2)
                tab = c["sin1"][:, t % 2, :].rearrange("p (j e) -> p j e", e=2)
                for e in range(2):
                    last = nc.vector.tensor_tensor(
                        o[:, :, :, e], q[:, :, :, 1 - e],
                        tab[:, :, e].unsqueeze(1).to_broadcast([P, 8, 32]), ALU.mult)
                last.then_inc(sind, 1)
                dve.wait_ge(sind, r + 1)
                dve.wait_ge(cosd, r + 1)
                need(dve, turned, r - 1)
                if ch < 4:
                    nc.vector.tensor_tensor(qr[:, r % 2, 0:512], T1[:, r % 2, :], T2[:, r % 2, :],
                                            ALU.add).then_inc(roped, 1)
                else:
                    dup = qr[:, r % 2, :].rearrange("p (v a d) -> p v a d", v=HKV, a=2)
                    for a in range(2):
                        last = nc.vector.tensor_tensor(
                            dup[:, :, a, :], T1[:, r % 2, :].rearrange("p (v d) -> p v d", v=HKV),
                            T2[:, r % 2, :].rearrange("p (v d) -> p v d", v=HKV), ALU.add)
                    last.then_inc(roped, 1)

        @block.gpsimd
        def _(pool):
            for i, (t, ch) in enumerate(chunks):
                if (t, ch) not in seq:
                    continue
                r = seq[(t, ch)]
                pool.wait_ge(biased, i + 1)
                need(pool, roped, r - 1)
                pool.tensor_tensor(T1[:, r % 2, :].rearrange("p (h d) -> p h d", h=8),
                                   qs[:, r % 2, :].rearrange("p (h d) -> p h d", h=8),
                                   c["cos1"][:, t % 2, :].unsqueeze(1).to_broadcast([P, 8, D1]),
                                   ALU.mult).then_inc(cosd, 1)



def token_experts(nc, c, X, CT, TOK, loads):
    with ExitStack() as stack:
        st = Store(nc, stack)
        E = B
        tf = st.sb("te_tf", [P, NT])
        ge = st.sb("te_ge", [P, E + 1, NT])
        own = st.sb("te_own", [P, E, NT])
        xt = st.sb("te_xt", [P, KD, P])
        sg = st.sb("te_sg", [P, E, D])
        a = st.sb("te_a", [P, E, D])
        aT = st.sb("te_aT", [P, E * KD, P])
        psX = st.ps("te_psX", [P, 512])
        psH = st.ps("te_psH", [P, E, D])
        psA = st.ps("te_psA", [P, E * KD, P])
        psY = st.ps("te_psY", [P, 512])
        ln = Norm(nc, c, st, "te")
        s = {n: st.sem("te_" + n) for n in ("xT", "xt", "h", "sg", "a", "aT", "aTa", "aTv", "down", "taken")}
        block = stack.enter_context(nc.Block())

        @block.tensor
        def _(pe):
            pe.wait_ge(loads["ctxT"], 16)

            def x_turn(t):
                need(pe, s["xt"], t)
                for k in range(KD):
                    last = nc.tensor.transpose(psX[:, k * P:(k + 1) * P],
                                               X[:, t, k * P:(k + 1) * P], c["ident"][:, :])
                last.then_inc(s["xT"], 1)

            def up(t):
                pe.wait_ge(s["xt"], t + 1)
                need(pe, s["a"], t)
                for j in range(E // 2):
                    for k in range(KD):
                        last = nc.tensor.matmul(psH[:, 2 * j:2 * j + 2, :], xt[:, k, :],
                                                CT[:, 2 * j:2 * j + 2, k, :],
                                                start=(k == 0), stop=(k == KD - 1))
                last.then_inc(s["h"], 1)

            def a_turn(t):
                pe.wait_ge(s["a"], t + 1)
                need(pe, s["aTa"], t)
                need(pe, s["aTv"], t)
                for e in range(E):
                    for k in range(KD):
                        last = nc.tensor.transpose(psA[:, e * KD + k, :], a[:, e, k * P:(k + 1) * P],
                                                   c["ident"][:, :])
                last.then_inc(s["aT"], 1)

            def down(t):
                pe.wait_ge(s["aTa"], t + 1)
                pe.wait_ge(s["aTv"], t + 1)
                need(pe, s["taken"], t)
                for i in range(E * KD):
                    last = nc.tensor.matmul(psY[:, 0:D], aT[:, i, :], CT[:, i // KD, i % KD, :],
                                            start=(i == 0), stop=(i == E * KD - 1))
                last.then_inc(s["down"], 1)

            staggered([x_turn, up, a_turn, down])

        @block.scalar
        def _(act):
            def keep_xt(t):
                act.wait_ge(s["xT"], t + 1)
                need(act, s["h"], t)
                nc.scalar.activation(xt[:, :, :], psX[:, 0:D].rearrange("p (k t) -> p k t", k=KD),
                                     ACT.Copy).then_inc(s["xt"], 1)

            def silu(t):
                act.wait_ge(s["h"], t + 1)
                need(act, s["a"], t)
                nc.scalar.activation(sg[:, :, :], psH[:, :, :], ACT.Silu).then_inc(s["sg"], 1)

            def keep_a(t):
                act.wait_ge(s["aT"], t + 1)
                need(act, s["down"], t)
                nc.scalar.activation(aT[:, 0:E, :], psA[:, 0:E, :], ACT.Copy).then_inc(s["aTa"], 1)

            staggered([keep_xt, silu, keep_a])
            ln.root(act)

        @block.vector
        def _(dve):
            ln.begin(dve)
            link = ln.chain.link
            dve.wait_ge(loads["tok"], 16)
            link(nc.vector.tensor_copy(tf[:, :], TOK[:, :]))
            link(nc.vector.memset(ge[:, 0, :], 1.0))
            link(nc.vector.memset(ge[:, E, :], 0.0))
            for e in range(1, E):
                link(nc.vector.tensor_scalar(ge[:, e, :], tf[:, :], 3125.0 * e, None, ALU.is_ge))
            link(nc.vector.tensor_tensor(own[:, :, :], ge[:, 0:E, :], ge[:, 1:E + 1, :], ALU.subtract))

            def gated(t):
                dve.wait_ge(s["sg"], t + 1)
                need(dve, s["aT"], t)
                for e in range(E):
                    last = nc.vector.scalar_tensor_tensor(out=a[:, e, :], in0=psH[:, e, :],
                                                          scalar=own[:, e, t:t + 1], in1=sg[:, e, :],
                                                          op0=ALU.mult, op1=ALU.mult)
                last.then_inc(s["a"], 1)

            def keep_a(t):
                dve.wait_ge(s["aT"], t + 1)
                need(dve, s["down"], t)
                nc.vector.tensor_copy(aT[:, E:2 * E, :], psA[:, E:2 * E, :]).then_inc(s["aTv"], 1)

            def take(t):
                dve.wait_ge(s["down"], t + 1)
                nc.vector.tensor_tensor(ln.R[:, t, :], psY[:, 0:D], X[:, t, :],
                                        ALU.add).then_inc(s["taken"], 1)
                dve.wait_ge(s["taken"], t + 1)
                ln.stat(t)

            staggered([None, gated, keep_a, take])
            ln.apply(dve, X)



def route(nc, c, X, GW, tiles, loads, rows):
    with ExitStack() as stack:
        st = Store(nc, stack)
        PAIRS = TOPK * NT
        XT = st.sb("ro_XT", [P, 2, KD, P])
        lg = st.sb("ro_lg", [P, NT, NE])
        nmx = st.sb("ro_nmx", [P, NT])
        ex = st.sb("ro_ex", [P, NT, NE])
        sc = st.sb("ro_sc", [P, NT, NE])
        top = st.sb("ro_top", [P, NT, 8])
        idx = st.sb("ro_idx", [P, NT, 8], U32)
        idf = st.sb("ro_idf", [P, NT, 8])
        sel = st.sb("ro_sel", [P, TOPK, NT, NE])
        picked = st.sb("ro_picked", [P, TOPK, NT, NE])
        chosen = st.sb("ro_chosen", [P, NT, NE], BF16)
        before = st.sb("ro_before", [P, P], BF16)
        ones = st.sb("ro_ones", [P, P], BF16)
        full = st.sb("ro_full", [P, NE])
        ends = st.sb("ro_ends", [P, 2, NE + NE // 2])
        first = st.sb("ro_first", [P, NE])
        slot = st.sb("ro_slot", [P, NT, NE])
        pos = st.sb("ro_pos", [P, PAIRS])
        tile = st.sb("ro_tile", [P, PAIRS])
        place = st.sb("ro_place", [P, PAIRS])
        in_tile = st.sb("ro_in_tile", [P, PAIRS, NTILE], F32R)
        in_place = st.sb("ro_in_place", [P, PAIRS, P], F32R)
        number = st.sb("ro_number", [P, NTILE])
        empty = st.sb("ro_empty", [P, NTILE])
        over = st.sb("ro_over", [1, NTILE, NE])
        owner = st.sb("ro_owner", [1, 2, NTILE])
        tot = st.sb("ro_tot", [P, NT])
        psX = st.ps("ro_psX", [P, 2, 512])
        psL = st.ps("ro_psL", [P, 512])
        psR = st.ps("ro_psR", [P, 512])
        psN = st.ps("ro_psN", [P, 512])
        psP = st.ps("ro_psP", [P, 512])
        s = {n: st.sem("ro_" + n) for n in (
            "xT", "xt", "logits", "shift", "exped", "dve", "bf16", "chosen", "ranked", "located",
            "numbered", "placed", "ordered", "rows")}
        block = stack.enter_context(nc.Block())

        @block.sync
        def _(sp):
            sp.dma_start(rows.rearrange("(t p) d -> p t d", p=P), X[:]).then_inc(s["rows"], 16)
            sp.wait_ge(s["rows"], 16)

        @block.tensor
        def _(pe):
            def turn(t):
                need(pe, s["xt"], t - 1)
                for k in range(KD):
                    last = nc.tensor.transpose(psX[:, t % 2, k * P:(k + 1) * P],
                                               X[:, t, k * P:(k + 1) * P], c["ident"][:, :])
                last.then_inc(s["xT"], 1)

            def logit(t):
                pe.wait_ge(s["xt"], t + 1)
                if t == 0:
                    pe.wait_ge(loads["gate"], 16)
                for k in range(KD):
                    last = nc.tensor.matmul(psL[:, t * NE:(t + 1) * NE], XT[:, t % 2, k, :], GW[:, k, :],
                                            start=(k == 0), stop=(k == KD - 1))
                last.then_inc(s["logits"], 1)

            staggered([turn, logit])
            pe.wait_ge(s["bf16"], 1)
            pe.wait_ge(s["chosen"], 1)
            for t in range(NT):
                nc.tensor.matmul(psN[:, 0:NE], ones[:, :], chosen[:, t, :], start=(t == 0), stop=(t == NT - 1))
            nc.tensor.matmul(psR[:, 0:NT * NE], before[:, :], chosen.rearrange("p t e -> p (t e)"),
                             start=True, stop=False)
            for t in range(NT - 1):
                later = NT - 1 - t
                last = nc.tensor.matmul(psR[:, (t + 1) * NE:NT * NE], ones[:, :],
                                        chosen[:, t, :].unsqueeze(1).to_broadcast([P, later, NE]),
                                        start=False, stop=(t == NT - 2))
            last.then_inc(s["ranked"], 1)
            for i in range(PAIRS):
                if i % NT == 0:
                    pe.wait_ge(s["numbered"], i // NT + 1)
                    pe.wait_ge(s["placed"], i // NT + 1)
                last = nc.tensor.matmul(psP[:, 0:NTILE], in_place[:, i, :], in_tile[:, i, :],
                                        start=(i == 0), stop=(i == PAIRS - 1))
            last.then_inc(s["ordered"], 1)

        @block.scalar
        def _(act):
            nc.scalar.activation(before[:, :], c["before"], ACT.Copy)
            nc.scalar.activation(ones[:, :], c["ones"], ACT.Copy).then_inc(s["bf16"], 1)
            for t in range(NT):
                act.wait_ge(s["xT"], t + 1)
                need(act, s["logits"], t - 1)
                nc.scalar.activation(XT[:, t % 2], psX[:, t % 2, 0:D].rearrange("p (k t) -> p k t", k=KD),
                                     ACT.Copy).then_inc(s["xt"], 1)
            act.wait_ge(s["logits"], NT)
            nc.scalar.activation(sc[:, :, :], psL[:, 0:NT * NE].rearrange("p (t e) -> p t e", t=NT),
                                 ACT.Exp, scale=-1.0).then_inc(s["exped"], 1)
            act.wait_ge(s["shift"], 1)
            for t in range(NT):
                last = nc.scalar.activation(ex[:, t, :], lg[:, t, :], ACT.Exp, bias=nmx[:, t:t + 1])
            last.then_inc(s["exped"], 1)

        @block.gpsimd
        def _(pool):
            for k in range(TOPK):
                which = slice(k * NT, (k + 1) * NT)
                pool.wait_ge(s["located"], k + 1)
                pool.tensor_tensor(in_tile[:, which, :], in_tile[:, which, :].bitcast(F32),
                                   c["pairs"][:, which].unsqueeze(2).to_broadcast([P, NT, NTILE]),
                                   ALU.mult).then_inc(s["numbered"], 1)

        @block.vector
        def _(dve):
            link = Chain(dve, s["dve"]).link
            nc.vector.memset(tiles.owner[:, :], 0)
            nc.vector.memset(tiles.chunk[:, :], 0)
            nc.vector.memset(tiles.index[:, :, :], 0)
            link(nc.vector.memset(ends[:, :, :], 0.0))
            dve.wait_ge(s["exped"], 1)
            link(nc.vector.tensor_scalar(sc[:, :, :], sc[:, :, :], 1.0, None, ALU.add))
            link(nc.vector.reciprocal(sc[:, :, :], sc[:, :, :]))
            for t in range(NT):
                last = nc.vector.max(top[:, t, :], sc[:, t, :])
            link(last)
            for t in range(NT):
                last = nc.vector.max_index(idx[:, t, :], top[:, t, :], sc[:, t, :])
            link(last)
            link(nc.vector.tensor_copy(idf[:, :, :], idx[:, :, :]))
            link(nc.vector.tensor_tensor(
                sel[:, :, :, :], c["slots"][:, 0:NE].unsqueeze(1).unsqueeze(1).to_broadcast([P, TOPK, NT, NE]),
                idf[:, :, 0:TOPK].rearrange("p t k -> p k t").unsqueeze(3).to_broadcast([P, TOPK, NT, NE]),
                ALU.is_equal))
            link(nc.vector.tensor_reduce(lg[:, :, :], sel.rearrange("p k t e -> p t e k"), AX.X, ALU.add))
            nc.vector.tensor_copy(chosen[:, :, :], lg[:, :, :]).then_inc(s["chosen"], 1)
            dve.wait_ge(s["chosen"], 1)
            link(nc.vector.tensor_copy(lg[:, :, :], psL[:, 0:NT * NE].rearrange("p (t e) -> p t e", t=NT)))
            nc.vector.tensor_reduce(nmx[:, :], lg[:, :, :], AX.X, ALU.max, negate=True).then_inc(s["shift"], 1)
            dve.wait_ge(s["ranked"], 1)
            link(nc.vector.tensor_scalar(full[:, :], psN[:, 0:NE], 1.0 / P, (P - 1) / (2.0 * P), ALU.mult, ALU.add))
            link(nc.vector.tensor_scalar(full[:, :], full[:, :], MAGIC, MAGIC, ALU.add, ALU.subtract))
            pad = NE // 2
            link(nc.vector.tensor_copy(ends[:, 0, pad:], full[:, :]))
            a, step = 0, 1
            while step < NE:
                link(nc.vector.tensor_tensor(ends[:, 1 - a, pad:], ends[:, a, pad:],
                                             ends[:, a, pad - step:pad + NE - step], ALU.add))
                a, step = 1 - a, 2 * step
            end = ends[:, a, pad:]
            link(nc.vector.tensor_tensor(first[:, :], end, full[:, :], ALU.subtract))
            link(nc.vector.tensor_scalar(first[:, :], first[:, :], float(P), None, ALU.mult))
            link(nc.vector.tensor_tensor(slot[:, :, :], psR[:, 0:NT * NE].rearrange("p (t e) -> p t e", t=NT),
                                         first[:, :].unsqueeze(1).to_broadcast([P, NT, NE]), ALU.add))
            link(nc.vector.tensor_tensor(picked[:, :, :, :], sel[:, :, :, :],
                                         slot[:, :, :].unsqueeze(1).to_broadcast([P, TOPK, NT, NE]), ALU.mult))
            link(nc.vector.tensor_reduce(pos[:, :], picked.rearrange("p k t e -> p (k t) e"), AX.X, ALU.add))
            link(nc.vector.tensor_scalar(tile[:, :], pos[:, :], 1.0 / P, -(P - 1) / (2.0 * P), ALU.mult, ALU.add))
            link(nc.vector.tensor_scalar(tile[:, :], tile[:, :], MAGIC, MAGIC, ALU.add, ALU.subtract))
            link(nc.vector.scalar_tensor_tensor(out=place[:, :], in0=tile[:, :], scalar=-float(P), in1=pos[:, :],
                                                op0=ALU.mult, op1=ALU.add))
            for k in range(TOPK):
                which = slice(k * NT, (k + 1) * NT)
                for out, width, of, done in ((in_tile, NTILE, tile, "located"), (in_place, P, place, "placed")):
                    nc.vector.tensor_tensor(out[:, which, :],
                                            c["slots"][:, 0:width].unsqueeze(1).to_broadcast([P, NT, width]),
                                            of[:, which].unsqueeze(2).to_broadcast([P, NT, width]),
                                            ALU.is_equal).then_inc(s[done], 1)
            link(nc.vector.tensor_tensor(
                over[:, :, :], c["slots"][0:1, 0:NTILE].unsqueeze(2).to_broadcast([1, NTILE, NE]),
                end[0:1, :].unsqueeze(1).to_broadcast([1, NTILE, NE]), ALU.is_ge))
            link(nc.vector.tensor_reduce(owner[:, 0, :], over[:, :, :], AX.X, ALU.add))
            link(nc.vector.tensor_reduce(owner[:, 1, :], over.rearrange("p n (c g) -> p n c g", g=2)[:, :, :, 1],
                                         AX.X, ALU.add))
            nc.vector.tensor_scalar(tiles.owner[:, 4:4 + NTILE], owner[:, 0, :], NE - 1.0, None, ALU.min)
            nc.vector.tensor_scalar(tiles.chunk[:, 4:4 + NTILE], owner[:, 1, :], NC - 1.0, None, ALU.min)
            dve.wait_ge(s["ordered"], 1)
            link(nc.vector.tensor_scalar(empty[:, :], psP[:, 0:NTILE], 0.0, c["past"][:, 0:1],
                                         ALU.is_equal, ALU.mult))
            link(nc.vector.scalar_tensor_tensor(out=number[:, :], in0=psP[:, 0:NTILE], scalar=-1.0,
                                                in1=empty[:, :], op0=ALU.add, op1=ALU.add))
            target = tiles.index[:, LAG:LAG + NTILE, 1]
            link(nc.vector.tensor_copy(target, number[:, :]))
            nc.vector.tensor_scalar(tiles.index[:, 0:NTILE, 0], target, NT * P - 1, None, ALU.bitwise_and)
            dve.wait_ge(s["exped"], 2)
            link(nc.vector.tensor_tensor(picked[:, :, :, :], sel[:, :, :, :],
                                         ex[:, :, :].unsqueeze(1).to_broadcast([P, TOPK, NT, NE]), ALU.mult))
            link(nc.vector.tensor_reduce(tiles.weight[:, :, :], picked[:, :, :, :], AX.X, ALU.add))
            link(nc.vector.tensor_reduce(tot[:, :], tiles.weight.rearrange("p k t -> p t k"), AX.X, ALU.add))
            link(nc.vector.reciprocal(tot[:, :], tot[:, :]))
            nc.vector.tensor_tensor(tiles.weight[:, :, :], tiles.weight[:, :, :],
                                    tot[:, :].unsqueeze(1).to_broadcast([P, TOPK, NT]), ALU.mult)


class Weights:

    def __init__(self, st):
        self.w_in = st.sb("w_in", [P, NE * KD, 2 * INTER])
        self.c_in = st.sb("c_in", [P, NC * KD, 2 * CINTER])
        self.w_out = st.sb("w_out", [P, NE, D])
        self.c_out = st.sb("c_out", [P, NC, D])


LAG = 6


class Tiles:

    def __init__(self, st):
        self.owner = st.sb("ti_owner", [1, NTILE + 8], mybir.dt.int32)
        self.chunk = st.sb("ti_chunk", [1, NTILE + 8], mybir.dt.int32)
        self.index = st.sb("ti_index", [P, NTILE + 8, 2], U32)
        self.weight = st.sb("ti_weight", [P, TOPK, NT])


def experts(nc, c, tiles, W, rows, pairs, loads):
    NB = NTILE // 4
    with ExitStack() as stack:
        st = Store(nc, stack)
        xg = st.sb("ex_xg", [P, 4, D])
        xt = st.sb("ex_xt", [P, 2, KD, P])
        sg = st.sb("ex_sg", [P, 2, INTER + CINTER])
        a = st.sb("ex_a", [P, 2, 2, P])
        aT = st.sb("ex_aT", [P, 2, 2, P])
        y = st.sb("ex_y", [P, 4, D])
        index = st.sb("ex_index", [P, 4, 2], U32)
        psX = st.ps("ex_psX", [P, 2, 512])
        psG = st.ps("ex_psG", [P, 2, 512])
        psA = st.ps("ex_psA", [P, 2, 512])
        psD = st.ps("ex_psD", [P, 2, 512])
        gathered = [st.sem("ex_gathered%d" % i) for i in range(4)]
        scattered = [st.sem("ex_scattered%d" % i) for i in range(4)]
        s = {n: st.sem("ex_" + n) for n in (
            "padded",
            "passed",
            "aimed",
            "xturned", "xcopied", "hidden", "gated", "acted", "aturned", "acopied", "downed", "ycopied")}
        block = stack.enter_context(nc.Block())

        def run(eng, body, lag, peeled=1):
            for I in range(peeled):
                for u in range(4):
                    body(4 * I + u, u, I)
            with eng.Fori(peeled, NB) as I:
                for u in range(4):
                    body(I * 4 + u, u, I)
            for k in range(NTILE, NTILE + lag):
                body(k, k % 4, k // 4)

        def lagging(k, u, I, lag):
            if isinstance(k, int) and not 0 <= k - lag < NTILE:
                return None
            return k - lag, (u - lag) % 4, I + (u - lag) // 4

        @block.gpsimd
        def _(pool):
            for n in range(2):
                last = pool.memset(a[:, n, 0, :], 0.0)
            last.then_inc(s["padded"], 1)

            def aim(n, K, J):
                for u in (2 * n, 2 * n + 1):
                    need(pool, gathered[u], 16 * (min(J, NB) if isinstance(J, int) else J))
                    need(pool, scattered[(u - LAG) % 4], 16 * (J + (u - LAG) // 4))
                hold(pool, s["passed"])
                pool.tensor_copy(index[:, 2 * n:2 * n + 2, :],
                                 tiles.index[:, bass.ds(K + 2 * n, 2), :]).then_inc(s["aimed"], 1)

            def body(k, u, I):
                if u == 1:
                    aim(1, k - 1, I)
                if u == 3:
                    aim(0, k + 1, I + 1)
                now = lagging(k, u, I, 0)
                if now:
                    pool.wait_ge(s["aimed"], 2 * I + 1 + u // 2)
                    need(pool, s["xturned"], k - 3)
                    hold(pool, s["passed"])
                    pool.indirect_dma_start(
                        out=xg[:, u, :], out_offset=None, in_=rows,
                        in_offset=bass.IndirectOffsetOnAxis(ap=index[:, u, 0:1], axis=0),
                        bounds_check=NT * P - 1, oob_is_err=True).then_inc(gathered[u], 16)
                late = lagging(k, u, I, LAG)
                if late:
                    j, v, J = late
                    pool.wait_ge(s["ycopied"], j + 1)
                    if not now:
                        pool.wait_ge(s["aimed"], 2 * I + 1 + u // 2)
                    hold(pool, s["passed"])
                    pool.indirect_dma_start(
                        out=pairs, out_offset=bass.IndirectOffsetOnAxis(ap=index[:, u, 1:2], axis=0),
                        in_=y[:, v, :], in_offset=None, bounds_check=TOPK * NT * P - 1,
                        oob_is_err=False).then_inc(scattered[v], 16)

            aim(0, 0, 0)
            run(pool, body, LAG, peeled=2)
            for v in range(4):
                pool.wait_ge(scattered[v], 16 * NB)
                pool.wait_ge(gathered[v], 16 * NB)

        @block.tensor
        def _(pe):
            held = []

            def body(k, u, I):
                now = lagging(k, u, I, 0)
                one = lagging(k, u, I, 1)
                if u == 0:
                    held[:] = [nc.values_load_multi_w_load_instructions(
                        table[0:1, bass.ds(k, 8)], engines=(mybir.EngineType.PE,), min_val=0, max_val=n - 1,
                        skip_runtime_bounds_check_because="route takes the minimum with n - 1")[1]
                        for table, n in ((tiles.owner, NE), (tiles.chunk, NC))]

                def expert_of(lag):
                    return held[0][4 + u - lag], held[1][4 + u - lag]

                if now:
                    pe.wait_ge(gathered[u], 16 * I + 16)
                    need(pe, s["xcopied"], k - 1)
                    for kk in range(KD):
                        last = nc.tensor.transpose(psX[:, u % 2, kk * P:(kk + 1) * P],
                                                   xg[:, u, kk * P:(kk + 1) * P], c["ident"][:, :])
                    last.then_inc(s["xturned"], 1)
                if one:
                    j, v, J = one
                    e, ch = expert_of(1)
                    pe.wait_ge(s["xcopied"], j + 1)
                    need(pe, s["acted"], j - 1)
                    if isinstance(j, int) and j == 0:
                        pe.wait_ge(loads["w_in"], 16)
                        pe.wait_ge(loads["c_in"], 16)
                    for kk in range(KD):
                        nc.tensor.matmul(psG[:, v % 2, 0:2 * INTER], xt[:, v % 2, kk, :],
                                         W.w_in[:, bass.ds(e * KD + kk, 1), :].rearrange("p a n -> p (a n)"),
                                         start=(kk == 0), stop=(kk == KD - 1))
                    for kk in range(KD):
                        last = nc.tensor.matmul(psG[:, v % 2, 2 * INTER:2 * (INTER + CINTER)], xt[:, v % 2, kk, :],
                                                W.c_in[:, bass.ds(ch * KD + kk, 1), :].rearrange("p a n -> p (a n)"),
                                                start=(kk == 0), stop=(kk == KD - 1))
                    last.then_inc(s["hidden"], 1)
                three = lagging(k, u, I, 3)
                two = lagging(k, u, I, 2)
                if two:
                    j, v, J = two
                    pe.wait_ge(s["acted"], j + 1)
                    need(pe, s["acopied"], j - 1)
                    for n in range(2):
                        last = nc.tensor.transpose(psA[:, v % 2, n * P:(n + 1) * P], a[:, v % 2, n, :],
                                                   c["ident"][:, :])
                    last.then_inc(s["aturned"], 1)
                if three:
                    j, v, J = three
                    e, ch = expert_of(3)
                    pe.wait_ge(s["acopied"], j + 1)
                    need(pe, s["ycopied"], j - 1)
                    if isinstance(j, int) and j == 0:
                        pe.wait_ge(loads["w_out"], 16)
                        pe.wait_ge(loads["c_out"], 16)
                    nc.tensor.matmul(psD[:, v % 2, 0:D], aT[0:INTER, v % 2, 0, :],
                                     W.w_out[0:INTER, bass.ds(e, 1), :].rearrange("p a n -> p (a n)"),
                                     start=True, stop=False)
                    nc.tensor.matmul(psD[:, v % 2, 0:D], aT[:, v % 2, 1, :],
                                     W.c_out[:, bass.ds(ch, 1), :].rearrange("p a n -> p (a n)"),
                                     start=False, stop=True).then_inc(s["downed"], 1)

            run(pe, body, 3)

        @block.scalar
        def _(act):
            def body(k, u, I):
                now = lagging(k, u, I, 0)
                if now:
                    act.wait_ge(s["xturned"], k + 1)
                    need(act, s["hidden"], k - 1)
                    nc.scalar.activation(xt[:, u % 2], psX[:, u % 2, 0:D].rearrange("p (k t) -> p k t", k=KD),
                                         ACT.Copy).then_inc(s["xcopied"], 1)
                one = lagging(k, u, I, 1)
                if one:
                    j, v, J = one
                    act.wait_ge(s["hidden"], j + 1)
                    need(act, s["acted"], j - 1)
                    nc.scalar.activation(sg[:, v % 2, 0:INTER], psG[:, v % 2, 0:INTER], ACT.Silu)
                    nc.scalar.activation(sg[:, v % 2, INTER:], psG[:, v % 2, 2 * INTER:2 * INTER + CINTER],
                                         ACT.Silu).then_inc(s["gated"], 1)
                three = lagging(k, u, I, 3)
                if three:
                    j, v, J = three
                    act.wait_ge(s["downed"], j + 1)
                    need(act, scattered[v], 16 * J)
                    nc.scalar.activation(y[:, v, :], psD[:, v % 2, 0:D], ACT.Copy).then_inc(s["ycopied"], 1)

            run(act, body, 3)

        @block.vector
        def _(dve):
            dve.wait_ge(s["padded"], 1)

            def body(k, u, I):
                one = lagging(k, u, I, 1)
                if one:
                    j, v, J = one
                    dve.wait_ge(s["gated"], j + 1)
                    need(dve, s["aturned"], j - 1)
                    nc.vector.tensor_tensor(a[:, v % 2, 0, 0:INTER], psG[:, v % 2, INTER:2 * INTER],
                                            sg[:, v % 2, 0:INTER], ALU.mult)
                    nc.vector.scalar_tensor_tensor(out=a[:, v % 2, 1, :],
                                                   in0=psG[:, v % 2, 2 * INTER + CINTER:2 * (INTER + CINTER)],
                                                   scalar=SMALL_SCALE, in1=sg[:, v % 2, INTER:],
                                                   op0=ALU.mult, op1=ALU.mult).then_inc(s["acted"], 1)
                two = lagging(k, u, I, 2)
                if two:
                    j, v, J = two
                    dve.wait_ge(s["aturned"], j + 1)
                    need(dve, s["downed"], j - 1)
                    nc.vector.tensor_copy(aT[:, v % 2], psA[:, v % 2, 0:2 * P].rearrange("p (n t) -> p n t", n=2)
                                          ).then_inc(s["acopied"], 1)

            run(dve, body, 3)


def combine(nc, c, X, tiles, pairs, out):
    with ExitStack() as stack:
        st = Store(nc, stack)
        ln = Norm(nc, c, st, "co")
        Z = st.sb("co_Z", [P, NT, D])
        G = st.sb("co_G", [P, NT, TOPK, D])
        came = [st.sem("co_came%d" % t) for t in range(NT)]
        written = st.sem("co_written")
        summed = st.sem("co_summed")
        order = st.sem("co_pool")
        by_pool = (1, 4)
        view = pairs.rearrange("(k t p) d -> t p k d", k=TOPK, p=P)
        block = stack.enter_context(nc.Block())

        @block.sync
        def _(sp):
            for t in range(0, NT, 2):
                sp.dma_start(G[:, t], view[t]).then_inc(came[t], 16)
            for n in range(2):
                sp.wait_ge(ln.normed, 4 * n + 4)
                sp.dma_start(out[4 * n:4 * n + 4].rearrange("t p d -> p t d"),
                             Z[:, 4 * n:4 * n + 4, :]).then_inc(written, 16)
            sp.wait_ge(written, 32)

        @block.scalar
        def _(act):
            for t in range(1, NT, 2):
                act.dma_start(G[:, t], view[t]).then_inc(came[t], 16)
            ln.root(act)

        @block.gpsimd
        def _(pool):
            link = Chain(pool, order).link
            for t in by_pool:
                pool.wait_ge(came[t], 16)
                for k in range(TOPK):
                    last = pool.tensor_scalar(G[:, t, k, :], G[:, t, k, :], tiles.weight[:, k, t:t + 1],
                                              None, ALU.mult)
                link(last)
                for k in range(TOPK):
                    last = pool.tensor_tensor(ln.R[:, t, :], X[:, t, :] if k == 0 else ln.R[:, t, :],
                                              G[:, t, k, :], ALU.add)
                    if k < TOPK - 1:
                        link(last)
                last.then_inc(summed, 1)

        @block.vector
        def _(dve):
            ln.begin(dve)
            for t in range(NT):
                if t not in by_pool:
                    dve.wait_ge(came[t], 16)
                    for k in range(TOPK):
                        ln.chain.link(nc.vector.scalar_tensor_tensor(
                            out=ln.R[:, t, :], in0=G[:, t, k, :], scalar=tiles.weight[:, k, t:t + 1],
                            in1=X[:, t, :] if k == 0 else ln.R[:, t, :], op0=ALU.mult, op1=ALU.add))
                    ln.stat(t, last=False)
            for n, t in enumerate(by_pool):
                dve.wait_ge(summed, n + 1)
                ln.stat(t, last=(n == len(by_pool) - 1))
            ln.apply(dve, Z)



TABLE = dict(ident=P, ones=P, hm=8, hx=4, pm=2, slots=P, before=P, pairs=TOPK * NT, past=1, cos0=S, sin0=S, causal=2 * S, window=2 * S,
             cos1=2 * D1, sin1=2 * D1, eps=1)


def decoder(nc, x, xT, ctx, ctxT, tok, w0, wo0, gamma, wu, wd, had, w1, bias1, wo1, bo1, sinks, gate,
            w_in, w_out, c_in, c_out, table, out, stop=99):
    stack = ExitStack()
    with stack:
        Store.spent.clear()
        top = Store(nc, stack, passing=False)
        X = top.sb("X", [P, NT, D])
        TB = top.sb("table", [P, sum(TABLE.values())])
        identb = top.sb("identb", [P, P], BF16)
        CT = top.sb("CT", [P, B, KD, D])
        TOK = top.sb("TOK", [P, NT], mybir.dt.int32)
        GM = top.sb("GM", [P, 1])
        loads = {n: top.sem("load_" + n) for n in (
            "x", "xT", "w0", "consts", "ctx", "ctxT", "tok", "gamma", "wo0", "wff", "had", "w1",
            "bias1", "wo1", "gate", "w_in", "c_in", "w_out", "c_out")}
        rows = nc.dram_tensor("rows", (NT * P, D), F32, kind="Internal").ap()
        pairs = nc.dram_tensor("pairs", (TOPK * NT * P, D), F32, kind="Internal").ap()
        c, at = {}, 0
        for n, width in TABLE.items():
            c[n] = TB[:, at:at + width]
            at += width
        for n in ("causal", "window"):
            c[n] = c[n].rearrange("p (h s) -> p h s", h=2)
        for n in ("cos1", "sin1"):
            c[n] = c[n].rearrange("p (h d) -> p h d", h=2)
        c["identb"] = identb
        c["rsqrt512"] = RSQRT512

        with ExitStack() as layer0:
            l0 = Store(nc, layer0)
            CTX = l0.sb("CTX", [P, NT, D])
            WO0 = l0.sb("WO0", [P, 4, D])
            WU = l0.sb("WU", [P, KD, I0])
            WD = l0.sb("WD", [P, I0 // P, D])
            HAD = l0.sb("HAD", [P, 4, I0])
            with ExitStack() as attn0:
                a0 = Store(nc, attn0)
                XT = a0.sb("XT", [P, KD, B * S])
                W0 = a0.sb("W0", [P, 5, KD, D])
                QT = a0.sb("QT", [P, B * KD, S])
                KT = a0.sb("KT", [P, B * KD, S])
                V = a0.sb("V", [P, 16, 2, 64])
                AT = a0.sb("AT", [P, 16, S])
                with nc.Block() as block:
                    @block.sync
                    def _(sp):
                        sp.dma_start(XT[:], xT.rearrange("(k p) s -> p k s", p=P)).then_inc(loads["xT"], 16)
                        sp.dma_start(W0[:], w0.rearrange("m (k p) o -> p (m k) o", p=P)).then_inc(loads["w0"], 16)
                        sp.dma_start(TB[:], table).then_inc(loads["consts"], 16)
                        sp.dma_start(X[:], x.rearrange("t p d -> p t d")).then_inc(loads["x"], 16)
                        sp.dma_start(WO0[:], wo0.rearrange("g p o -> p g o")).then_inc(loads["wo0"], 16)
                        sp.dma_start(WU[:], wu.rearrange("(k p) o -> p k o", p=P)).then_inc(loads["wff"], 16)
                        sp.dma_start(WD[:], wd.rearrange("(k p) o -> p k o", p=P)).then_inc(loads["wff"], 16)
                        sp.dma_start(HAD[:], had.rearrange("(k p) o -> p k o", p=P)).then_inc(loads["had"], 16)

                    @block.scalar
                    def _(act):
                        act.dma_start(CTX[:], ctx.rearrange("t p d -> p t d")).then_inc(loads["ctx"], 16)
                        act.dma_start(CT[:], ctxT.rearrange("b (k p) s -> p (b k) s", p=P)).then_inc(loads["ctxT"], 16)
                        act.dma_start(TOK[:], tok).then_inc(loads["tok"], 16)
                        act.dma_start(GM[:], gamma.to_broadcast([P, 1])).then_inc(loads["gamma"], 16)

                project_0(nc, c, XT, W0, QT, KT, V, loads)

                def stage_qk0(pool, Qs, KM, w, r, I):
                    at = w // 2 if isinstance(w, int) else I
                    pool.tensor_copy(Qs[:, 0, :], QT[:, at, :])
                    return spread(pool, KM, KT[:, at, :], c["hm"][:, 4 * r:4 * r + 4])

                def stage_v0(pool, Vs, w, r, I):
                    return pool.tensor_copy(Vs.rearrange("p k (h d) -> p k h d", h=4)[:, :, :, 0:DK0],
                                            V[:, w, :, :].rearrange("p k (h d) -> p k h d", h=4))

                attention(nc, c, "a0", 16, stage_qk0, stage_v0,
                          lambda w, half: AT[:, w, half * P:(half + 1) * P], width=32, pairs=False,
                          mask=c["causal"], causal=True, scale=0.25)

                def product0(pe, out, t):
                    if t == 0:
                        pe.wait_ge(loads["wo0"], 16)
                    for g in range(4):
                        last = nc.tensor.matmul(out, AT[:, (t // 2) * 4 + g, (t % 2) * P:(t % 2 + 1) * P],
                                                WO0[:, g, :], start=(g == 0), stop=(g == 3))
                    return last

                with nc.Block() as block:
                    @block.vector
                    def _(dve):
                        dve.wait_ge(loads["x"], 16)
                        nc.vector.tensor_copy(identb[:], c["ident"])
                output_norm(nc, c, "o0", X, product0)

            if stop > 1:
                with ExitStack() as attnx:
                    ax = Store(nc, attnx)
                    Y = ax.sb("Y", [P, NT, D])

                    def stage_qkx(pool, Qs, KM, w, r, I):
                        if isinstance(w, int) and w == 0:
                            pool.wait_ge(loads["ctx"], 16)
                            pool.wait_ge(loads["ctxT"], 16)
                        pool.tensor_copy(Qs[:, 0, :], X[:, w, :])
                        return spread(pool, KM, CTX[:, w, :], c["hx"])

                    def stage_vx(pool, Vs, w, r, I):
                        return pool.tensor_copy(Vs, CT[:, I, :, r * P:(r + 1) * P])

                    attention(nc, c, "ax", 8, stage_qkx, stage_vx,
                              lambda w, half: Y[:, w, half * P:(half + 1) * P], width=32, pairs=False,
                              scale=INV_SQRT32)
                    with nc.Block() as block:
                        @block.vector
                        def _(dve):
                            dve.wait_ge(loads["gamma"], 16)
                    cross_norm(nc, c, X, Y, GM)

            if stop > 2:
                feed_forward_0(nc, c, X, HAD, WU, WD, loads)

        recycle(nc)
        if stop > 3:
            with ExitStack() as layer1:
                l1 = Store(nc, layer1)
                BO1 = l1.sb("BO1", [P, D])
                SK = l1.sb("SK", [P, H1])
                NSK = l1.sb("NSK", [P, H1])
                QT1 = l1.sb("QT1", [P, 32, 2, S])
                KT1 = l1.sb("KT1", [P, 32, S])
                V1 = l1.sb("V1", [P, 32, 2, D1])
                with ExitStack() as proj1:
                    p1 = Store(nc, proj1)
                    W1 = p1.sb("W1", [P, KD, NQ1 + 2 * NKV1])
                    BIAS = p1.sb("BIAS", [P, NQ1 + 2 * NKV1])
                    with nc.Block() as block:
                        @block.sync
                        def _(sp):
                            sp.dma_start(W1[:], w1.rearrange("(k p) o -> p k o", p=P)).then_inc(loads["w1"], 16)
                            sp.dma_start(BIAS[:], bias1.to_broadcast([P, NQ1 + 2 * NKV1])).then_inc(loads["bias1"], 16)
                            sp.dma_start(SK[:], sinks.to_broadcast([P, H1])).then_inc(loads["x"], 16)
                            sp.dma_start(BO1[:], bo1.to_broadcast([P, D])).then_inc(loads["x"], 16)
                    project_1(nc, c, X, W1, BIAS, QT1, KT1, V1, loads)
                WO1 = l1.sb("WO1", [P, HKV, 2, D])
                with nc.Block() as block:
                    @block.sync
                    def _(sp):
                        sp.dma_start(WO1[:], wo1.rearrange("(v j p) o -> p (v j) o", p=P, j=2)).then_inc(loads["wo1"], 16)

                    @block.vector
                    def _(dve):
                        dve.wait_ge(loads["x"], 48)
                        nc.vector.tensor_scalar(NSK[:], SK[:], -1.0, None, ALU.mult)

                def stage_qk1(pool, Qs, KM, w, r, I):
                    pool.tensor_copy(Qs, QT1[:, w, :, :])
                    return spread(pool, KM, KT1[:, w, :], c["pm"])

                def stage_v1(pool, Vs, w, r, I):
                    return pool.tensor_copy(Vs, V1[:, w, :, :])

                def sinks_of(w, r, I):
                    at = bass.ds((I // 2) * 4, 4)
                    return SK[:, at], NSK[:, at]

                attention(nc, c, "a1", 32, stage_qk1, stage_v1,
                          lambda w, half: QT1[:, w, :, half * P:(half + 1) * P], width=64, pairs=True,
                          mask=c["window"], sinks_of=sinks_of)

                with nc.Block() as block:
                    add_bias = top.sem("bo_added")

                    @block.vector
                    def _(dve):
                        for t in range(NT):
                            nc.vector.tensor_tensor(X[:, t, :], X[:, t, :], BO1[:], ALU.add)

                def product1(pe, out, t):
                    if t == 0:
                        pe.wait_ge(loads["wo1"], 16)
                    for i in range(2 * HKV):
                        last = nc.tensor.matmul(
                            out, QT1[:, (i // 2) * B + t // 2, i % 2, (t % 2) * P:(t % 2 + 1) * P],
                            WO1[:, i // 2, i % 2, :], start=(i == 0), stop=(i == 2 * HKV - 1))
                    return last

                output_norm(nc, c, "o1", X, product1)

        tiles = Tiles(top)
        if stop > 4:
            with ExitStack() as moe:
                m = Store(nc, moe)
                W = Weights(m)
                GW = m.sb("GW", [P, KD, NE])
                with nc.Block() as block:
                    @block.sync
                    def _(sp):
                        sp.dma_start(GW[:], gate.rearrange("(k p) e -> p k e", p=P)).then_inc(loads["gate"], 16)
                        sp.dma_start(W.w_in[:], w_in).then_inc(loads["w_in"], 16)
                        sp.dma_start(W.c_in[:], c_in).then_inc(loads["c_in"], 16)
                        sp.dma_start(W.w_out[0:INTER], w_out).then_inc(loads["w_out"], 16)
                        sp.dma_start(W.c_out[:], c_out).then_inc(loads["c_out"], 16)
                token_experts(nc, c, X, CT, TOK, loads)
                if stop > 5:
                    route(nc, c, X, GW, tiles, loads, rows)
                    experts(nc, c, tiles, W, rows, pairs, loads)
            if stop > 5:
                combine(nc, c, X, tiles, pairs, out)
        if stop > 5:
            pass
        else:
            with nc.Block() as block:
                @block.sync
                def _(sp):
                    wr = top.sem("dbg")
                    sp.dma_start(out.rearrange("t p d -> p t d"), X[:]).then_inc(wr, 16)
                    sp.wait_ge(wr, 16)
                    for n in ("ctx", "ctxT", "tok", "gamma","wo0","had","w0","xT","x","consts"):
                        sp.wait_ge(loads[n],16)
                    sp.wait_ge(loads["wff"],32)


import numpy as np

RSQRT512 = float(np.float32(1.0) / np.sqrt(np.float32(512.0)))
INV_SQRT32 = float(np.float32(1.0) / np.sqrt(np.float32(32.0)))


def constants():
    f = np.float32
    part = np.arange(P)
    inv0 = f(1.0) / f(10000.0) ** (np.arange(0, DK0, 2, dtype=f) / f(DK0))
    ang0 = np.outer(np.arange(S, dtype=f), inv0).astype(f)
    row = (part % DK0) // 2
    sign = np.where(part % 2 == 0, -1.0, 1.0).astype(f)[:, None]
    inv1 = f(1.0) / f(150000.0) ** (np.arange(D1 // 2, dtype=f) * f(2.0) / f(D1))
    ang1 = (np.arange(S, dtype=f)[:, None] * inv1[None, :]).astype(f)
    scale1 = f(D1 ** (-0.25))
    cos1 = np.repeat(np.cos(ang1), 2, axis=-1) * scale1
    sin1 = np.repeat(np.sin(ang1), 2, axis=-1) * np.tile(np.array([-1, 1], f), D1 // 2) * scale1
    q, k = np.arange(S)[:, None], np.arange(S)[None, :]
    halves = lambda m: m.reshape(2, P, -1).transpose(1, 0, 2).reshape(P, -1)
    values = dict(
        ident=np.eye(P), ones=np.ones((P, P)), hm=part[:, None] // DK0 == np.arange(8),
        hx=part[:, None] // DX == np.arange(4), pm=part[:, None] // D1 == np.arange(2),
        slots=np.tile(np.arange(P), (P, 1)), before=part[:, None] < part,
        pairs=np.arange(TOPK * NT) * P + part[:, None] + 1,
        past=2 * TOPK * NT * P + 1 + part[:, None], cos0=np.cos(ang0).T[row], sin0=np.sin(ang0).T[row] * sign,
        causal=halves(np.where(k <= q, 0.0, -1e30)), window=halves(np.where(abs(q - k) <= 128, 0.0, -1e30)),
        cos1=halves(cos1), sin1=halves(sin1), eps=np.full((P, 1), EPS))
    table = np.concatenate([np.asarray(values[n], f) for n in TABLE], axis=1)
    had = np.array([[1.0]], f)
    while had.shape[0] < I0:
        had = np.block([[had, had], [had, -had]])
    return np.ascontiguousarray(table), np.ascontiguousarray(had.astype(f))


def arrays_of(inputs):
    g = {n: np.asarray(a) for n, a in inputs.items()}
    x, ctx = g["x"], g["ctx_2048"]
    swap = np.arange(D) ^ 1
    wq, wk, wv = g["L0_attn_Wq"], g["L0_attn_Wk"], g["L0_attn_Wv"]
    wo0 = np.zeros((4, 4, 32, D), np.float32)
    wo0[:, :, 0:DK0] = g["L0_attn_Wo"].reshape(4, 4, DK0, D)
    flat = lambda a: a.reshape(D, -1)
    tiled = lambda a: a.reshape(-1, P, a.shape[2]).transpose(1, 0, 2)
    table, had = constants()
    return dict(
        x=x.reshape(NT, P, D), xT=x.reshape(B * S, D).T, ctx=ctx.reshape(NT, P, D),
        ctxT=ctx.transpose(0, 2, 1), tok=g["itok_BxS_13_99985"].reshape(NT, P).T,
        w0=np.stack([wq, wq[:, swap], wk, wk[:, swap], wv]), wo0=wo0.reshape(4, P, D),
        gamma=g["L0_xattn_gamma"].reshape(1, 1), wu=g["L0_ffn_w_up"].T, wd=g["L0_ffn_w_down"].T, had=had,
        w1=np.concatenate([flat(g["L1_attn_Wq"]), flat(g["L1_attn_Wk"]), flat(g["L1_attn_Wv"])], axis=1),
        bias1=np.concatenate([g["L1_attn_bq"].reshape(-1), g["L1_attn_bk"].reshape(-1),
                              g["L1_attn_bv"].reshape(-1)]).reshape(1, -1),
        wo1=g["L1_attn_Wo"].reshape(NQ1, D), bo1=g["L1_attn_bo"].reshape(1, D),
        sinks=g["L1_attn_sinks"].reshape(1, H1), gate=g["L1_ffn_gate_w"].T,
        w_in=tiled(np.concatenate([g["L1_ffn_Wg"], g["L1_ffn_Wu"]], axis=2)),
        w_out=g["L1_ffn_Wd"].transpose(1, 0, 2),
        c_in=tiled(np.concatenate([g["L1_ffn_cWg"], g["L1_ffn_cWu"]], axis=2)),
        c_out=g["L1_ffn_cWd"].transpose(1, 0, 2), table=table)


def kernel(**inputs):
    import concourse.bacc as bacc
    from concourse.bass_utils import run_bass_kernel_spmd

    nc = bacc.Bacc("TRN2", target_bir_lowering=False, num_devices=1)
    arrays, args = {}, []
    for name, a in arrays_of(inputs).items():
        a = np.ascontiguousarray(a)
        arrays["in_" + name] = a
        args.append(nc.dram_tensor("in_" + name, a.shape, mybir.dt.from_np(a.dtype), kind="ExternalInput").ap())
    out = nc.dram_tensor("out_0", (NT, P, D), F32, kind="ExternalOutput").ap()
    decoder(nc, *args, out)
    r = run_bass_kernel_spmd(nc, [arrays], core_ids=[0])
    return r.results[0]["out_0"].reshape(B, S, D)
```

```python
import concourse.bass as bass
from concourse import mybir
from contextlib import ExitStack

F32 = mybir.dt.float32
F32R = mybir.dt.float32r
BF16 = mybir.dt.bfloat16
U32 = mybir.dt.uint32
ALU = mybir.AluOpType
ACT = mybir.ActivationFunctionType
AX = mybir.AxisListType

B, S, D = 4, 256, 256
P = 128
NT = B * S // P
KD = D // P
H0, DK0 = 16, 16
HX, DX = 8, 32
I0 = 512
H1, HKV, D1 = 32, 8, 64
NQ1, NKV1 = H1 * D1, HKV * D1
NE, INTER = 32, 96
NC, CINTER = 16, 128
TOPK = 4
NTILE = TOPK * NT + NE
EPS = 1e-5
SMALL_SCALE = 0.05
MAGIC = 12582912.0


def need(eng, sem, value):
    if not (isinstance(value, int) and value <= 0):
        eng.wait_ge(sem, value)


def hold(eng, passed):
    eng.sem_inc(passed, 1)


class Chain:

    def __init__(self, eng, sem):
        self.eng, self.sem, self.n = eng, sem, 0

    def link(self, ins):
        self.n += 1
        ins.then_inc(self.sem, 1)
        self.eng.wait_ge(self.sem, self.n)


class Store:

    def __init__(self, nc, stack, passing=True):
        self.nc, self.stack, self.passing = nc, stack, passing

    def sb(self, name, shape, dt=F32):
        return self.stack.enter_context(self.nc.sbuf_tensor(name, shape, dt))

    def ps(self, name, shape, dt=F32):
        return self.stack.enter_context(self.nc.psum_tensor(name, shape, dt))

    spent = []

    def sem(self, name):
        sem = self.nc.alloc_semaphore(name)
        if self.passing:
            Store.spent.append(sem)
        return sem


def recycle(nc):
    nc.clear_and_free_semaphores(Store.spent)
    Store.spent.clear()
    nc.all_engine_barrier()



def spread(pool, KM, keys, heads):
    shape = [P, KM.shape[1], S]
    return pool.tensor_tensor(KM, keys.unsqueeze(1).to_broadcast(shape),
                              heads.unsqueeze(2).to_broadcast(shape), ALU.mult)


def attention(nc, consts, name, units, stage_q, stage_k, stage_v, out_of, *, width, pairs, mask=None, causal=False,
              scale=1.0, sinks_of=None):
    NB = units // 2
    with ExitStack() as stack:
        st = Store(nc, stack)
        nq = 2 if pairs else 1
        Qs = st.sb(name + "_Qs", [P, 2, nq, S])
        nk = 2 if pairs else 4
        KM = st.sb(name + "_KM", [P, 2, nk, S])
        Vs = st.sb(name + "_Vs", [P, 2, 2, 64 if pairs else 128])
        Sm = st.sb(name + "_Sm", [P, 2, 4, S])
        Pr = st.sb(name + "_Pr", [P, 4, 4, S])
        PT = st.sb(name + "_PT", [P, 2, 4, 2, P])
        mx = st.sb(name + "_mx", [P, 4, 4])
        nm = st.sb(name + "_nm", [P, 4, 4])
        den = st.sb(name + "_den", [P, 4, 4])
        rd = st.sb(name + "_rd", [P, 4, 4])
        sk = st.sb(name + "_sk", [P, 4, 4])
        es = st.sb(name + "_es", [P, 4, 4])
        psS = st.ps(name + "_psS", [P, 2, 4, S])
        psT = st.ps(name + "_psT", [P, 4, 2, P])
        psO = st.ps(name + "_psO", [P, 2, 512])
        cleared = st.sem(name + "_cleared")
        staged_q = st.sem(name + "_staged_q")
        staged_k = st.sem(name + "_staged_k")
        staged_v = st.sem(name + "_staged_v")
        scored = st.sem(name + "_scored")
        maxed = st.sem(name + "_maxed")
        shifted = st.sem(name + "_shifted")
        expd = st.sem(name + "_expd")
        summed = st.sem(name + "_summed")
        recip = st.sem(name + "_recip")
        normed = st.sem(name + "_normed")
        turned = st.sem(name + "_turned")
        copied_a = st.sem(name + "_copied_a")
        copied_v = st.sem(name + "_copied_v")
        mixed = st.sem(name + "_mixed")
        passed_p = st.sem(name + "_passed_p")
        passed_v = st.sem(name + "_passed_v")
        stored = st.sem(name + "_stored")
        ident = consts["ident"]
        block = stack.enter_context(nc.Block())

        def keys(u):
            return P if causal and u % 2 == 0 else S

        def over_steps(eng, body):
            for k in range(8):
                body(k, k % 4, k // 4)
            with eng.Fori(2, NB - 1) as I:
                for u in range(4):
                    body(I * 4 + u, u, I)
            for u in range(4):
                body(4 * (NB - 1) + u, u, NB - 1)
            for u in range(4):
                body(4 * NB + u, u, NB)

        def lags(k, u, I, lag):
            return not (isinstance(I, int) and I == 0) or u >= lag

        def current(I):
            return not (isinstance(I, int) and I == NB)

        @block.gpsimd
        def _(pool):
            pool.memset(Vs[:], 0.0).then_inc(cleared, 1)
            for w in range(2):
                stage_k(pool, KM[:, w], w, w, 0).then_inc(staged_k, 1)

            def norm(k, u):
                pool.wait_ge(recip, k + 1)
                p = Pr[:, u % 4, :, 0:keys(u)]
                pool.tensor_tensor(p, p, rd[:, u % 4, :].unsqueeze(2).to_broadcast([P, 4, keys(u)]),
                                   ALU.mult).then_inc(normed, 1)

            def rounds(I, last_round):
                for u in range(4):
                    k = 4 * I + u
                    if u % 2 == 1 and not last_round:
                        pool.wait_ge(scored, k + 1)
                        hold(pool, passed_p)
                        stage_k(pool, KM[:, u // 2], 2 * I + 2 + u // 2, u // 2,
                                I + 1).then_inc(staged_k, 1)
                    norm(k, u)

            rounds(0, False)
            with pool.Fori(1, NB - 1) as I:
                rounds(I, False)
            rounds(NB - 1, True)

        @block.tensor
        def _(pe):
            def body(k, u, I):
                if current(I):
                    if u % 2 == 0:
                        pe.wait_ge(staged_q, 2 * I + u // 2 + 1)
                        pe.wait_ge(staged_k, 2 * I + u // 2 + 1)
                    need(pe, shifted if mask is not None else expd, k - 1)
                    n = keys(u)
                    for j in range(2):
                        q = Qs[:, u // 2, j if pairs else 0, (u % 2) * P:(u % 2) * P + P]
                        ks = KM[:, u // 2, 0:2, 0:n] if pairs else KM[:, u // 2, 2 * j:2 * j + 2, 0:n]
                        last = nc.tensor.matmul(psS[:, u % 2, 2 * j:2 * j + 2, 0:n], q, ks,
                                                start=True, stop=True)
                    last.then_inc(scored, 1)
                if lags(k, u, I, 3) and (current(I) or u < 3):
                    v = (u - 3) % 4
                    pe.wait_ge(normed, k - 2)
                    need(pe, copied_a, k - 3)
                    need(pe, copied_v, k - 3)
                    for h in range(4):
                        for t in range(keys(v) // P):
                            last = nc.tensor.transpose(psT[:, h, t, :], Pr[:, v, h, t * P:t * P + P],
                                                       ident[:, :])
                    last.then_inc(turned, 1)
                if lags(k, u, I, 4):
                    v = u
                    pe.wait_ge(copied_a, k - 3)
                    pe.wait_ge(copied_v, k - 3)
                    if v % 2 == 0:
                        pe.wait_ge(staged_v, 2 * I - 1 + u // 2)
                    need(pe, stored, k - 5)
                    nt = keys(v) // P
                    for j in range(2 if pairs else 1):
                        for t in range(nt):
                            for c in range(2 if pairs else 4):
                                h = 2 * j + c if pairs else c
                                vs = (Vs[:, v // 2, t, 0:width] if pairs
                                      else Vs[:, v // 2, t, h * width:(h + 1) * width])
                                last = nc.tensor.matmul(
                                    psO[c * width:(c + 1) * width, v % 2, j * P:(j + 1) * P], vs,
                                    PT[:, v % 2, h, t, :], start=(t == 0), stop=(t == nt - 1))
                    last.then_inc(mixed, 1)

            over_steps(pe, body)

        @block.scalar
        def _(act):
            def body(k, u, I):
                if lags(k, u, I, 3) and (current(I) or u < 3):
                    v = (u - 3) % 4
                    act.wait_ge(turned, k - 2)
                    need(act, mixed, k - 4)
                    n = keys(v) // P
                    nc.scalar.activation(PT[:, v % 2, 0:2, 0:n, :], psT[:, 0:2, 0:n, :],
                                         ACT.Copy).then_inc(copied_a, 1)
                if u % 2 == 0 and lags(k, u, I, 2) and (current(I) or u < 2):
                    if isinstance(k, int) and k == 2:
                        act.wait_ge(cleared, 1)
                    need(act, mixed, k - 4)
                    r = 1 - u // 2
                    stage_v(Vs[:, r], 2 * I + u // 2 - 1, r, I - r).then_inc(staged_v, 1)
                if current(I):
                    act.wait_ge(shifted, k + 1)
                    need(act, turned, k - 3)
                    n = keys(u)
                    for h in range(4):
                        src = Sm[:, u % 2, h, 0:n] if mask is not None else psS[:, u % 2, h, 0:n]
                        last = nc.scalar.activation(Pr[:, u, h, 0:n], src, ACT.Exp,
                                                    bias=nm[:, u, h:h + 1], scale=scale,
                                                    accum_out=den[:, u, h:h + 1])
                    if sinks_of is not None:
                        last = nc.scalar.activation(es[:, u, :], sk[:, u, :], ACT.Exp)
                    last.then_inc(expd, 1)

            over_steps(act, body)

        @block.vector
        def _(dve):
            for w in range(2):
                stage_q(Qs[:, w], w, w, 0).then_inc(staged_q, 1)

            def body(k, u, I):
                if current(I):
                    dve.wait_ge(scored, k + 1)
                    hold(dve, passed_v)
                    n = keys(u)
                    if mask is not None:
                        for h in range(4):
                            last = nc.vector.tensor_tensor_reduce(
                                out=Sm[:, u % 2, h, 0:n], in0=psS[:, u % 2, h, 0:n],
                                in1=mask[:, u % 2, 0:n], scale=1.0, scalar=-3.0e38, op0=ALU.add,
                                op1=ALU.max, accum_out=mx[:, u, h:h + 1])
                    else:
                        last = nc.vector.tensor_reduce(mx[:, u, :], psS[:, u % 2, :, :], AX.X, ALU.max)
                    last.then_inc(maxed, 1)
                before = lags(k, u, I, 1) and (current(I) or u < 1)
                v = (u - 1) % 4
                if before:
                    dve.wait_ge(expd, k)
                    if sinks_of is not None:
                        nc.vector.tensor_tensor(den[:, v, :], den[:, v, :], es[:, v, :],
                                                ALU.add).then_inc(summed, 1)
                if current(I):
                    dve.wait_ge(maxed, (2 * k if sinks_of else k) + 1)
                    if sinks_of is None:
                        nc.vector.tensor_scalar(nm[:, u, :], mx[:, u, :], -scale, None,
                                                ALU.mult).then_inc(shifted, 1)
                    else:
                        sinks, negs = sinks_of(2 * I + u // 2, u // 2, I)
                        nc.vector.scalar_tensor_tensor(out=nm[:, u, :], in0=mx[:, u, :], scalar=-1.0,
                                                       in1=negs, op0=ALU.mult,
                                                       op1=ALU.min).then_inc(maxed, 1)
                if before:
                    if sinks_of is not None:
                        dve.wait_ge(summed, k)
                    nc.vector.reciprocal(rd[:, v, :], den[:, v, :]).then_inc(recip, 1)
                if current(I) and sinks_of is not None:
                    dve.wait_ge(maxed, 2 * k + 2)
                    nc.vector.tensor_tensor(sk[:, u, :], nm[:, u, :], sinks, ALU.add).then_inc(shifted, 1)
                if lags(k, u, I, 3) and (current(I) or u < 3):
                    v = (u - 3) % 4
                    dve.wait_ge(turned, k - 2)
                    need(dve, mixed, k - 4)
                    n = keys(v) // P
                    nc.vector.tensor_copy(PT[:, v % 2, 2:4, 0:n, :],
                                          psT[:, 2:4, 0:n, :]).then_inc(copied_v, 1)
                if lags(k, u, I, 4):
                    v = u
                    dve.wait_ge(mixed, k - 3)
                    src = psO[:, v % 2, 0:2 * P].rearrange("p (j q) -> p j q", j=2) if pairs else psO[:, v % 2, 0:P]
                    w = 2 * I - 2 + u // 2
                    nc.vector.tensor_copy(out_of(w, v % 2), src).then_inc(stored, 1)
                if u % 2 == 1 and not (isinstance(I, int) and I >= NB - 1):
                    stage_q(Qs[:, u // 2], 2 * I + 2 + u // 2, u // 2, I + 1).then_inc(staged_q, 1)

            over_steps(dve, body)



class Norm:

    def __init__(self, nc, consts, st, name):
        self.nc = nc
        self.R = st.sb(name + "_R", [P, NT, D])
        self.stats = st.sb(name + "_stats", [P, NT, 6])
        self.mv = st.sb(name + "_mv", [P, NT, 2])
        self.std = st.sb(name + "_std", [P, NT])
        self.rstd = st.sb(name + "_rstd", [P, NT])
        self.eps = consts["eps"]
        self.has_var = st.sem(name + "_has_var")
        self.has_std = st.sem(name + "_has_std")
        self.chain_sem = st.sem(name + "_dve")
        self.normed = st.sem(name + "_normed")

    def begin(self, dve):
        self.chain = Chain(dve, self.chain_sem)

    def stat(self, t, last=None):
        self.chain.link(self.nc.vector.bn_stats(self.stats[:, t, :], self.R[:, t, :]))
        done = self.nc.vector.bn_aggr(self.mv[:, t, :], self.stats[:, t, :])
        if t == NT - 1 if last is None else last:
            done.then_inc(self.has_var, 1)

    def stats_of(self, tiles):
        for t in tiles:
            done = self.nc.vector.bn_stats(self.stats[:, t, :], self.R[:, t, :])
        self.chain.link(done)
        for t in tiles:
            done = self.nc.vector.bn_aggr(self.mv[:, t, :], self.stats[:, t, :])
        done.then_inc(self.has_var, 1)

    def root(self, act):
        act.wait_ge(self.has_var, 1)
        self.nc.scalar.activation(self.std[:, :], self.mv[:, :, 1], ACT.Sqrt,
                                  bias=self.eps[:, 0:1]).then_inc(self.has_std, 1)

    def apply(self, dve, out):
        dve.wait_ge(self.has_std, 1)
        self.chain.link(self.nc.vector.reciprocal(self.rstd[:, :], self.std[:, :]))
        for t in range(NT):
            self.nc.vector.tensor_scalar(out[:, t, :], self.R[:, t, :], self.mv[:, t, 0:1],
                                         self.rstd[:, t:t + 1], ALU.subtract,
                                         ALU.mult).then_inc(self.normed, 1)


def staggered(stages):
    for time in range(NT + len(stages) - 1):
        for s in reversed(range(len(stages))):
            if 0 <= time - s < NT and stages[s] is not None:
                stages[s](time - s)



class Ternary:

    def __init__(self, st):
        self.TU = st.sb("TU", [P, KD, I0], BF16)
        self.TD = st.sb("TD", [P, I0 // P, D], BF16)
        self.scale = st.sb("w_scale", [P, 2])


def project_0(nc, c, XT, W0, QT, KT, V, WU, WD, ternary, loads):
    with ExitStack() as stack:
        st = Store(nc, stack)
        ps = st.ps("p0_ps", [P, 8, 512])
        T1 = st.sb("p0_T1", [P, 2, 512])
        T2 = st.sb("p0_T2", [P, 2, 512])
        made = st.sem("p0_made")
        rot = st.sem("p0_rot")
        roped = st.sem("p0_roped")
        v_made = st.sem("p0_v_made")
        v_kept = st.sem("p0_v_kept")
        wtmp = st.sb("p0_wtmp", [P, 2, 1024])
        wabs = st.sb("p0_wabs", [P, 2])
        winv = st.sb("p0_winv", [P, 2])
        w_abs = st.sem("p0_w_abs")
        w_mean = st.sem("p0_w_mean")
        order = st.sem("p0_dve")
        block = stack.enter_context(nc.Block())
        jobs = [(a, half, n) for a in range(2) for half in range(KD) for n in range(2)]

        @block.tensor
        def _(pe):
            for i, (a, half, n) in enumerate(jobs):
                pe.wait_ge(loads["w0" + "qk"[a]], 16)
                pe.wait_ge(loads["xT%d" % n], 16)
                need(pe, rot, 2 * (i - 1))
                for sw in range(2):
                    for k in range(KD):
                        last = nc.tensor.matmul(ps[:, 2 * (i % 2) + sw, :],
                                                W0[:, 2 * a + sw, k, half * P:(half + 1) * P],
                                                XT[:, k, n * 512:(n + 1) * 512],
                                                start=(k == 0), stop=(k == KD - 1))
                last.then_inc(made, 1)
            pe.wait_ge(loads["w0v"], 16)
            for t in range(NT):
                need(pe, v_kept, t - 3)
                for k in range(KD):
                    last = nc.tensor.matmul(ps[:, 4 + t % 4, 0:D], XT[:, k, t * P:(t + 1) * P],
                                            W0[:, 4, k, :], start=(k == 0), stop=(k == KD - 1))
                last.then_inc(v_made, 1)
            pe.wait_ge(w_abs, 1)
            need(pe, rot, 2 * len(jobs))
            nc.tensor.matmul(ps[:, 0, 0:2], c["ones"], wabs[:, :], start=True, stop=True).then_inc(w_mean, 1)

        @block.vector
        def _(dve):
            flat = [WU.rearrange("p k n -> p (k n)"), WD.rearrange("p k n -> p (k n)")]
            dve.wait_ge(loads["consts"], 16)
            for i, (a, half, n) in enumerate(jobs):
                dve.wait_ge(made, i + 1)
                need(dve, roped, i - 1)
                for sw, T, table in ((0, T1, c["cos0"]), (1, T2, c["sin0"])):
                    nc.vector.tensor_tensor(
                        T[:, i % 2, :].rearrange("p (b s) -> p b s", b=2),
                        ps[:, 2 * (i % 2) + sw, :].rearrange("p (b s) -> p b s", b=2),
                        table.unsqueeze(1).to_broadcast([P, 2, S]), ALU.mult).then_inc(rot, 1)
            dve.wait_ge(loads["wff"], 32)
            for j, w in enumerate(flat):
                last = nc.vector.tensor_reduce(wabs[:, j:j + 1], w, AX.X, ALU.add, apply_absolute_value=True)
            last.then_inc(w_abs, 1)
            link = Chain(dve, order).link
            dve.wait_ge(w_mean, 1)
            link(nc.vector.tensor_scalar(ternary.scale[:, :], ps[:, 0, 0:2], 1.0 / (D * I0), 1e-5,
                                         ALU.mult, ALU.max))
            link(nc.vector.reciprocal(winv[:, :], ternary.scale[:, :]))
            for j in range(2):
                last = nc.vector.tensor_scalar(wtmp[:, j, :], flat[j], winv[:, j:j + 1], 1.0, ALU.mult, ALU.min)
            link(last)
            for j in range(2):
                last = nc.vector.tensor_scalar(wtmp[:, j, :], wtmp[:, j, :], -1.0, MAGIC, ALU.max, ALU.add)
            link(last)
            for j in range(2):
                out = (ternary.TU, ternary.TD)[j][:, :, :].rearrange("p k n -> p (k n)")
                nc.vector.tensor_scalar(out, wtmp[:, j, :], MAGIC, None, ALU.subtract)

        @block.gpsimd
        def _(pool):
            for i, (a, half, n) in enumerate(jobs):
                pool.wait_ge(rot, 2 * (i + 1))
                out = (QT, KT)[a].rearrange("p (b h) s -> p b h s", h=KD)[:, 2 * n:2 * n + 2, half, :]
                pool.tensor_tensor(out, T1[:, i % 2, :].rearrange("p (b s) -> p b s", b=2),
                                   T2[:, i % 2, :].rearrange("p (b s) -> p b s", b=2),
                                   ALU.add).then_inc(roped, 1)

        @block.scalar
        def _(act):
            for t in range(NT):
                act.wait_ge(v_made, t + 1)
                out = V.rearrange("p (b g) k c -> p b g k c", g=4)[:, t // 2, :, t % 2, :]
                nc.scalar.activation(out, ps[:, 4 + t % 4, 0:D].rearrange("p (g c) -> p g c", g=4),
                                     ACT.Copy).then_inc(v_kept, 1)


def output_norm(nc, c, name, X, product, tiles_in=None):
    with ExitStack() as stack:
        st = Store(nc, stack)
        ps = st.ps(name + "_ps", [P, 4, 512])
        ln = Norm(nc, c, st, name)
        made = st.sem(name + "_made")
        taken = st.sem(name + "_taken")
        block = stack.enter_context(nc.Block())

        @block.tensor
        def _(pe):
            for t in range(NT):
                need(pe, taken, t - 3)
                product(pe, ps[:, t % 4, 0:D], t).then_inc(made, 1)

        @block.vector
        def _(dve):
            ln.begin(dve)
            for t in range(NT):
                dve.wait_ge(made, t + 1)
                nc.vector.tensor_tensor(ln.R[:, t, :], ps[:, t % 4, 0:D], X[:, t, :],
                                        ALU.add).then_inc(taken, 1)
                dve.wait_ge(taken, t + 1)
                ln.stat(t)
            ln.apply(dve, X)

        @block.scalar
        def _(act):
            ln.root(act)


def cross_norm(nc, c, X, Y, gamma):
    with ExitStack() as stack:
        st = Store(nc, stack)
        ln = Norm(nc, c, st, "lx")
        block = stack.enter_context(nc.Block())

        @block.vector
        def _(dve):
            ln.begin(dve)
            for t in range(NT):
                last = nc.vector.scalar_tensor_tensor(
                    out=ln.R[:, t, :], in0=Y[:, t, :], scalar=gamma[:, 0:1], in1=X[:, t, :],
                    op0=ALU.mult, op1=ALU.add)
            ln.chain.link(last)
            ln.stats_of(range(NT))
            ln.apply(dve, X)

        @block.scalar
        def _(act):
            ln.root(act)



def feed_forward_0(nc, c, X, HAD, ternary, loads):
    with ExitStack() as stack:
        st = Store(nc, stack)
        TU, TD, wsc = ternary.TU, ternary.TD, ternary.scale
        xt = st.sb("ff_xt", [P, KD, P])
        q1 = st.sb("ff_q1", [P, D])
        q1b = st.sb("ff_q1b", [P, D], BF16)
        q1T = st.sb("ff_q1T", [P, KD, P], BF16)
        hr = st.sb("ff_hr", [P, I0])
        h = st.sb("ff_h", [P, I0])
        hT = st.sb("ff_hT", [P, 4, P])
        z = st.sb("ff_z", [P, 2, 4, P])
        half = st.sb("ff_half", [P, 4, P])
        full = st.sb("ff_full", [P, 2, 4, P])
        q2 = st.sb("ff_q2", [P, I0])
        q2b = st.sb("ff_q2b", [P, I0], BF16)
        q2T = st.sb("ff_q2T", [P, 4, P], BF16)
        am = st.sb("ff_am", [P, 2, NT])
        m1 = st.sb("ff_m1", [P, 2, NT])
        rc = st.sb("ff_rc", [P, 2, NT])
        sc = st.sb("ff_sc", [P, 2, NT])
        dq = st.sb("ff_dq", [P, 2, NT])
        psX = st.ps("ff_psX", [P, 512])
        psR = st.ps("ff_psR", [P, 512])
        psQ = st.ps("ff_psQ", [P, 1024], BF16)
        psU = st.ps("ff_psU", [P, 512])
        psH = st.ps("ff_psH", [P, 4, P])
        psR2 = st.ps("ff_psR2", [P, 512])
        psQ2 = st.ps("ff_psQ2", [P, 1024], BF16)
        psY = st.ps("ff_psY", [P, 512])
        ln = Norm(nc, c, st, "ff")
        s = {n: st.sem("ff_" + n) for n in (
            "xT", "xt", "rot", "q1", "q1b", "q1T", "q1Tc", "up", "hr", "h",
            "hT", "hTc", "rot2", "rot2c", "mixed", "pool", "q2", "q2b", "q2T", "q2Tc", "down", "taken")}
        ident, identb = c["ident"], c["identb"]

        def in_slots(steps):
            for n in range(NT + 8):
                for step, lag in steps:
                    if 0 <= n - lag < NT:
                        step(n - lag)

        rd0 = 1.0 / 16.0
        rd1 = c["rsqrt512"]
        block = stack.enter_context(nc.Block())

        @block.tensor
        def _(pe):
            pe.wait_ge(loads["had"], 16)

            def x_turn(t):
                need(pe, s["xt"], t)
                for k in range(KD):
                    last = nc.tensor.transpose(psX[:, k * P:(k + 1) * P],
                                               X[:, t, k * P:(k + 1) * P], ident[:, :])
                last.then_inc(s["xT"], 1)

            def rotate(t):
                pe.wait_ge(s["xt"], t + 1)
                need(pe, s["q1"], t)
                for k in range(KD):
                    last = nc.tensor.matmul(psR[:, 0:D], xt[:, k, :], HAD[:, k, 0:D],
                                            start=(k == 0), stop=(k == KD - 1))
                last.then_inc(s["rot"], 1)

            def q_turn(t):
                pe.wait_ge(s["q1b"], t + 1)
                need(pe, s["q1Tc"], t)
                for k in range(KD):
                    last = nc.tensor.transpose(psQ[:, k * P:(k + 1) * P],
                                               q1b[:, k * P:(k + 1) * P], identb[:, :])
                last.then_inc(s["q1T"], 1)

            def up(t):
                pe.wait_ge(s["q1Tc"], t + 1)
                need(pe, s["hr"], t)
                for k in range(KD):
                    last = nc.tensor.matmul(psU[:, :], q1T[:, k, :], TU[:, k, :],
                                            start=(k == 0), stop=(k == KD - 1))
                last.then_inc(s["up"], 1)

            def h_turn(t):
                pe.wait_ge(s["h"], t + 1)
                need(pe, s["hTc"], t)
                for k in range(4):
                    last = nc.tensor.transpose(psH[:, k, :], h[:, k * P:(k + 1) * P], ident[:, :])
                last.then_inc(s["hT"], 1)

            def rotate2(t):
                pe.wait_ge(s["hTc"], t + 1)
                need(pe, s["rot2c"], t)
                for k in range(4):
                    last = nc.tensor.matmul(psR2[:, k * P:(k + 1) * P], hT[:, k, :], HAD[:, 0, 0:P],
                                            start=True, stop=True)
                last.then_inc(s["rot2"], 1)

            def q2_turn(t):
                pe.wait_ge(s["q2b"], t + 1)
                need(pe, s["q2Tc"], t)
                for k in range(4):
                    last = nc.tensor.transpose(psQ2[:, k * P:(k + 1) * P],
                                               q2b[:, k * P:(k + 1) * P], identb[:, :])
                last.then_inc(s["q2T"], 1)

            def down(t):
                pe.wait_ge(s["q2Tc"], t + 1)
                need(pe, s["taken"], t)
                for k in range(4):
                    last = nc.tensor.matmul(psY[:, 0:D], q2T[:, k, :], TD[:, k, :],
                                            start=(k == 0), stop=(k == 3))
                last.then_inc(s["down"], 1)

            in_slots([(rotate, 1), (x_turn, 0), (rotate2, 5), (h_turn, 4), (up, 3), (q_turn, 2), (down, 8),
                      (q2_turn, 7)])

        @block.scalar
        def _(act):
            def keep_xt(t):
                act.wait_ge(s["xT"], t + 1)
                need(act, s["rot"], t)
                nc.scalar.activation(xt[:, :, :], psX[:, 0:D].rearrange("p (k t) -> p k t", k=KD),
                                     ACT.Copy).then_inc(s["xt"], 1)

            def round1(t):
                act.wait_ge(s["q1"], t + 1)
                need(act, s["q1T"], t)
                nc.scalar.activation(q1b[:, :], q1[:, :], ACT.Copy, bias=-MAGIC).then_inc(s["q1b"], 1)

            def keep_q1(t):
                act.wait_ge(s["q1T"], t + 1)
                need(act, s["up"], t)
                nc.scalar.activation(q1T[:, :, :], psQ[:, 0:D].rearrange("p (k t) -> p k t", k=KD),
                                     ACT.Copy).then_inc(s["q1Tc"], 1)

            def relu(t):
                act.wait_ge(s["up"], t + 1)
                nc.scalar.activation(hr[:, :], psU[:, :], ACT.Relu,
                                     scale=dq[:, 0, t:t + 1]).then_inc(s["hr"], 1)
                act.wait_ge(s["hr"], t + 1)
                need(act, s["hT"], t)
                nc.scalar.activation(h[:, :], hr[:, :], ACT.Square).then_inc(s["h"], 1)

            def keep_h(t):
                act.wait_ge(s["hT"], t + 1)
                need(act, s["rot2"], t)
                nc.scalar.activation(hT[:, :, :], psH[:, :, :], ACT.Copy).then_inc(s["hTc"], 1)

            def keep_rot2(t):
                act.wait_ge(s["rot2"], t + 1)
                need(act, s["mixed"], t - 1)
                nc.scalar.activation(z[:, t % 2], psR2.rearrange("p (b n) -> p b n", b=4),
                                     ACT.Copy).then_inc(s["rot2c"], 1)

            def round2(t):
                act.wait_ge(s["q2"], t + 1)
                need(act, s["q2T"], t)
                nc.scalar.activation(q2b[:, :], q2[:, :], ACT.Copy, bias=-MAGIC).then_inc(s["q2b"], 1)

            def keep_q2(t):
                act.wait_ge(s["q2T"], t + 1)
                need(act, s["down"], t)
                nc.scalar.activation(q2T[:, :, :], psQ2[:, 0:I0].rearrange("p (k t) -> p k t", k=4),
                                     ACT.Copy).then_inc(s["q2Tc"], 1)

            in_slots([(keep_xt, 0), (keep_rot2, 5), (keep_h, 4), (relu, 3), (keep_q1, 2), (keep_q2, 7),
                      (round1, 1), (round2, 6)])
            ln.root(act)

        @block.gpsimd
        def _(pool):
            link = Chain(pool, s["pool"]).link

            def mix(t):
                pool.wait_ge(s["rot2c"], t + 1)
                need(pool, s["mixed"], t)
                r = t % 2
                pool.tensor_tensor(half[:, 0::2, :], z[:, r, 0::2, :], z[:, r, 1::2, :], ALU.add)
                link(pool.tensor_tensor(half[:, 1::2, :], z[:, r, 0::2, :], z[:, r, 1::2, :], ALU.subtract))
                need(pool, s["q2"], t - 1)
                pool.tensor_tensor(full[:, r, 0:2, :], half[:, 0:2, :], half[:, 2:4, :], ALU.add)
                pool.tensor_tensor(full[:, r, 2:4, :], half[:, 0:2, :], half[:, 2:4, :],
                                   ALU.subtract).then_inc(s["mixed"], 1)

            for t in range(NT):
                mix(t)

        @block.vector
        def _(dve):
            ln.begin(dve)
            link = ln.chain.link
            def quantise(jobs):
                def each(make):
                    for job in jobs:
                        last = make(*job)
                    return last

                link(each(lambda i, t, src, out, norm, done: nc.vector.tensor_reduce(
                    am[:, i, t:t + 1], src, AX.X, ALU.max, apply_absolute_value=True)))
                link(each(lambda i, t, src, out, norm, done: nc.vector.tensor_scalar(
                    m1[:, i, t:t + 1], am[:, i, t:t + 1], norm, 1e-5, ALU.mult, ALU.max)))
                link(each(lambda i, t, src, out, norm, done: nc.vector.reciprocal(
                    rc[:, i, t:t + 1], m1[:, i, t:t + 1])))
                each(lambda i, t, src, out, norm, done: nc.vector.tensor_scalar(
                    dq[:, i, t:t + 1], m1[:, i, t:t + 1], wsc[:, i:i + 1], 1.0 / 127.0, ALU.mult, ALU.mult))
                link(each(lambda i, t, src, out, norm, done: nc.vector.tensor_scalar(
                    sc[:, i, t:t + 1], rc[:, i, t:t + 1], 127.0, norm, ALU.mult, ALU.mult)))
                link(each(lambda i, t, src, out, norm, done: nc.vector.tensor_scalar(
                    out, src, sc[:, i, t:t + 1], 127.0, ALU.mult, ALU.min)))
                each(lambda i, t, src, out, norm, done: nc.vector.tensor_scalar(
                    out, out, -127.0, MAGIC, ALU.max, ALU.add).then_inc(s[done], 1))

            def quantise_both(time):
                jobs = []
                if 0 <= time - 6 < NT:
                    dve.wait_ge(s["mixed"], time - 5)
                    need(dve, s["q2b"], time - 6)
                    jobs.append((1, time - 6, full[:, (time - 6) % 2].rearrange("p b n -> p (b n)"), q2[:, :], rd1, "q2"))
                if 0 <= time - 1 < NT:
                    dve.wait_ge(s["rot"], time)
                    need(dve, s["q1b"], time - 1)
                    jobs.append((0, time - 1, psR[:, 0:D], q1[:, :], rd0, "q1"))
                if jobs:
                    quantise(jobs)

            def take(t):
                dve.wait_ge(s["down"], t + 1)
                nc.vector.scalar_tensor_tensor(out=ln.R[:, t, :], in0=psY[:, 0:D],
                                               scalar=dq[:, 1, t:t + 1], in1=X[:, t, :],
                                               op0=ALU.mult, op1=ALU.add).then_inc(s["taken"], 1)
                dve.wait_ge(s["taken"], t + 1)
                ln.stat(t)

            for time in range(NT + 8):
                quantise_both(time)
                if time >= 8:
                    take(time - 8)
            ln.apply(dve, X)



def project_1(nc, c, X, W1, BIAS, QT, KT, V, loads):
    CH = (NQ1 + 2 * NKV1) // 512
    with ExitStack() as stack:
        st = Store(nc, stack)
        xt = st.sb("p1_xt", [P, 2, KD, P])
        qs = st.sb("p1_qs", [P, 2, 512])
        T1 = st.sb("p1_T1", [P, 2, 512])
        T2 = st.sb("p1_T2", [P, 2, 512])
        qr = st.sb("p1_qr", [P, 2, 1024])
        ps = st.ps("p1_ps", [P, 2, 512])
        psX = st.ps("p1_psX", [P, 512])
        psT = st.ps("p1_psT", [P, 2, 2, 512])
        xT = st.sem("p1_xT")
        xk = st.sem("p1_xk")
        made = st.sem("p1_made")
        biased = st.sem("p1_biased")
        cosd = st.sem("p1_cosd")
        sind = st.sem("p1_sind")
        roped = st.sem("p1_roped")
        turned = st.sem("p1_turned")
        kept = st.sem("p1_kept")
        block = stack.enter_context(nc.Block())
        chunks = [(t, ch) for t in range(NT) for ch in range(CH)]
        rotary = [(t, ch) for t, ch in chunks if ch < CH - 1]
        seq = {tc: i for i, tc in enumerate(rotary)}
        w_of = lambda kv, t: kv * B + t // 2

        @block.tensor
        def _(pe):
            pe.wait_ge(loads["w1"], 16)

            def turn_x(t):
                need(pe, xk, t)
                for k in range(KD):
                    last = nc.tensor.transpose(psX[:, k * P:(k + 1) * P],
                                               X[:, t, k * P:(k + 1) * P], c["ident"][:, :])
                last.then_inc(xT, 1)

            def turn(r):
                t, ch = rotary[r]
                pe.wait_ge(roped, r + 1)
                need(pe, kept, r - 1)
                for j in range(4 if ch < 4 else 8):
                    last = nc.tensor.transpose(psT[:, r % 2, j // 4, (j % 4) * P:(j % 4 + 1) * P],
                                               qr[:, r % 2, j * P:(j + 1) * P], c["ident"][:, :])
                last.then_inc(turned, 1)

            turn_x(0)
            late = []
            for i, (t, ch) in enumerate(chunks):
                if ch == 0:
                    pe.wait_ge(xk, t + 1)
                need(pe, biased, i - 1)
                for k in range(KD):
                    last = nc.tensor.matmul(ps[:, i % 2, :], xt[:, t % 2, k, :],
                                            W1[:, k, ch * 512:(ch + 1) * 512],
                                            start=(k == 0), stop=(k == KD - 1))
                last.then_inc(made, 1)
                if ch == 2 and t + 1 < NT:
                    turn_x(t + 1)
                if (t, ch) in seq:
                    late.append(seq[(t, ch)])
                if len(late) > 2:
                    turn(late.pop(0))
            for r in late:
                turn(r)

        @block.scalar
        def _(act):
            def keep_x(t):
                act.wait_ge(xT, t + 1)
                need(act, made, (t - 1) * CH)
                nc.scalar.activation(xt[:, t % 2, :, :], psX[:, 0:D].rearrange("p (k t) -> p k t", k=KD),
                                     ACT.Copy).then_inc(xk, 1)

            keep_x(0)
            for r, (t, ch) in enumerate(rotary):
                if ch == 2 and t + 1 < NT:
                    keep_x(t + 1)
                act.wait_ge(turned, r + 1)
                at = slice((t % 2) * P, (t % 2 + 1) * P)
                if ch < 4:
                    for kv in range(2):
                        last = nc.scalar.activation(
                            QT[:, w_of(2 * ch + kv, t), :, at],
                            psT[:, r % 2, 0, kv * D:(kv + 1) * D].rearrange("p (j t) -> p j t", j=2),
                            ACT.Copy)
                else:
                    dst = KT.rearrange("p (v b) s -> p v b s", b=B)[:, :, t // 2, at]
                    last = nc.scalar.activation(dst, psT[:, r % 2, :, :].rearrange(
                        "p a (j t) -> p (a j) t", j=4), ACT.Copy)
                last.then_inc(kept, 1)

        @block.vector
        def _(dve):
            def sum_up(r):
                t, ch = rotary[r]
                dve.wait_ge(sind, r + 1)
                dve.wait_ge(cosd, r + 1)
                need(dve, turned, r - 1)
                if ch < 4:
                    nc.vector.tensor_tensor(qr[:, r % 2, 0:512], T1[:, r % 2, :], T2[:, r % 2, :],
                                            ALU.add).then_inc(roped, 1)
                else:
                    dup = qr[:, r % 2, :].rearrange("p (v a d) -> p v a d", v=HKV, a=2)
                    for a in range(2):
                        last = nc.vector.tensor_tensor(
                            dup[:, :, a, :], T1[:, r % 2, :].rearrange("p (v d) -> p v d", v=HKV),
                            T2[:, r % 2, :].rearrange("p (v d) -> p v d", v=HKV), ALU.add)
                    last.then_inc(roped, 1)

            dve.wait_ge(loads["bias1"], 16)
            for i, (t, ch) in enumerate(chunks):
                dve.wait_ge(made, i + 1)
                if ch == CH - 1:
                    out = V.rearrange("p (v b) k d -> p v b k d", b=B)[:, :, t // 2, t % 2, :]
                    nc.vector.tensor_tensor(out, ps[:, i % 2, :].rearrange("p (v d) -> p v d", v=HKV),
                                            BIAS[:, ch * 512:(ch + 1) * 512].rearrange("p (v d) -> p v d", v=HKV),
                                            ALU.add).then_inc(biased, 1)
                    continue
                r = seq[(t, ch)]
                need(dve, cosd, r - 1)
                nc.vector.tensor_tensor(qs[:, r % 2, :], ps[:, i % 2, :], BIAS[:, ch * 512:(ch + 1) * 512],
                                        ALU.add).then_inc(biased, 1)
                if r > 0:
                    sum_up(r - 1)
                dve.wait_ge(biased, i + 1)
                q = qs[:, r % 2, :].rearrange("p (h j e) -> p h j e", h=8, e=2)
                o = T2[:, r % 2, :].rearrange("p (h j e) -> p h j e", h=8, e=2)
                tab = c["sin1"][:, t % 2, :].rearrange("p (j e) -> p j e", e=2)
                for e in range(2):
                    last = nc.vector.tensor_tensor(
                        o[:, :, :, e], q[:, :, :, 1 - e],
                        tab[:, :, e].unsqueeze(1).to_broadcast([P, 8, 32]), ALU.mult)
                last.then_inc(sind, 1)
            sum_up(len(rotary) - 1)

        @block.gpsimd
        def _(pool):
            for i, (t, ch) in enumerate(chunks):
                if (t, ch) not in seq:
                    continue
                r = seq[(t, ch)]
                pool.wait_ge(biased, i + 1)
                need(pool, roped, r - 1)
                pool.tensor_tensor(T1[:, r % 2, :].rearrange("p (h d) -> p h d", h=8),
                                   qs[:, r % 2, :].rearrange("p (h d) -> p h d", h=8),
                                   c["cos1"][:, t % 2, :].unsqueeze(1).to_broadcast([P, 8, D1]),
                                   ALU.mult).then_inc(cosd, 1)



def token_experts(nc, c, X, CT, TOK, loads):
    with ExitStack() as stack:
        st = Store(nc, stack)
        E = B
        tf = st.sb("te_tf", [P, NT])
        ge = st.sb("te_ge", [P, E + 1, NT])
        own = st.sb("te_own", [P, E, NT])
        xt = st.sb("te_xt", [P, KD, P])
        sg = st.sb("te_sg", [P, E, D])
        a = st.sb("te_a", [P, E, D])
        aT = st.sb("te_aT", [P, E * KD, P])
        psX = st.ps("te_psX", [P, 512])
        psH = st.ps("te_psH", [P, E, D])
        psA = st.ps("te_psA", [P, E * KD, P])
        psY = st.ps("te_psY", [P, 512])
        ln = Norm(nc, c, st, "te")
        s = {n: st.sem("te_" + n) for n in ("xT", "xt", "h", "sg", "a", "aT", "aTa", "aTv", "down", "taken")}
        block = stack.enter_context(nc.Block())

        @block.tensor
        def _(pe):
            pe.wait_ge(loads["ctxT"], 16)

            def x_turn(t):
                need(pe, s["xt"], t)
                for k in range(KD):
                    last = nc.tensor.transpose(psX[:, k * P:(k + 1) * P],
                                               X[:, t, k * P:(k + 1) * P], c["ident"][:, :])
                last.then_inc(s["xT"], 1)

            def up(t):
                pe.wait_ge(s["xt"], t + 1)
                need(pe, s["a"], t)
                for j in range(E // 2):
                    for k in range(KD):
                        last = nc.tensor.matmul(psH[:, 2 * j:2 * j + 2, :], xt[:, k, :],
                                                CT[:, 2 * j:2 * j + 2, k, :],
                                                start=(k == 0), stop=(k == KD - 1))
                last.then_inc(s["h"], 1)

            def a_turn(t):
                pe.wait_ge(s["a"], t + 1)
                need(pe, s["aTa"], t)
                need(pe, s["aTv"], t)
                for e in range(E):
                    for k in range(KD):
                        last = nc.tensor.transpose(psA[:, e * KD + k, :], a[:, e, k * P:(k + 1) * P],
                                                   c["ident"][:, :])
                last.then_inc(s["aT"], 1)

            def down(t):
                pe.wait_ge(s["aTa"], t + 1)
                pe.wait_ge(s["aTv"], t + 1)
                need(pe, s["taken"], t)
                for i in range(E * KD):
                    last = nc.tensor.matmul(psY[:, 0:D], aT[:, i, :], CT[:, i // KD, i % KD, :],
                                            start=(i == 0), stop=(i == E * KD - 1))
                last.then_inc(s["down"], 1)

            staggered([x_turn, up, a_turn, down])

        @block.scalar
        def _(act):
            def keep_xt(t):
                act.wait_ge(s["xT"], t + 1)
                need(act, s["h"], t)
                nc.scalar.activation(xt[:, :, :], psX[:, 0:D].rearrange("p (k t) -> p k t", k=KD),
                                     ACT.Copy).then_inc(s["xt"], 1)

            def silu(t):
                act.wait_ge(s["h"], t + 1)
                need(act, s["a"], t)
                nc.scalar.activation(sg[:, :, :], psH[:, :, :], ACT.Silu).then_inc(s["sg"], 1)

            def keep_a(t):
                act.wait_ge(s["aT"], t + 1)
                need(act, s["down"], t)
                nc.scalar.activation(aT[:, 0:E, :], psA[:, 0:E, :], ACT.Copy).then_inc(s["aTa"], 1)

            staggered([keep_xt, silu, keep_a])
            ln.root(act)

        @block.vector
        def _(dve):
            ln.begin(dve)
            link = ln.chain.link
            dve.wait_ge(loads["tok"], 16)
            link(nc.vector.tensor_copy(tf[:, :], TOK[:, :]))
            link(nc.vector.memset(ge[:, 0, :], 1.0))
            link(nc.vector.memset(ge[:, E, :], 0.0))
            for e in range(1, E):
                link(nc.vector.tensor_scalar(ge[:, e, :], tf[:, :], 3125.0 * e, None, ALU.is_ge))
            link(nc.vector.tensor_tensor(own[:, :, :], ge[:, 0:E, :], ge[:, 1:E + 1, :], ALU.subtract))

            def gated(t):
                dve.wait_ge(s["sg"], t + 1)
                need(dve, s["aT"], t)
                for e in range(E):
                    last = nc.vector.scalar_tensor_tensor(out=a[:, e, :], in0=psH[:, e, :],
                                                          scalar=own[:, e, t:t + 1], in1=sg[:, e, :],
                                                          op0=ALU.mult, op1=ALU.mult)
                last.then_inc(s["a"], 1)

            def keep_a(t):
                dve.wait_ge(s["aT"], t + 1)
                need(dve, s["down"], t)
                nc.vector.tensor_copy(aT[:, E:2 * E, :], psA[:, E:2 * E, :]).then_inc(s["aTv"], 1)

            def take(t):
                dve.wait_ge(s["down"], t + 1)
                nc.vector.tensor_tensor(ln.R[:, t, :], psY[:, 0:D], X[:, t, :],
                                        ALU.add).then_inc(s["taken"], 1)
                dve.wait_ge(s["taken"], t + 1)
                ln.stat(t)

            staggered([None, gated, keep_a, take])
            ln.apply(dve, X)



def route(nc, c, X, GW, tiles, loads, rows):
    with ExitStack() as stack:
        st = Store(nc, stack)
        PAIRS = TOPK * NT
        XT = st.sb("ro_XT", [P, 2, KD, P])
        lg = st.sb("ro_lg", [P, NT, NE])
        nmx = st.sb("ro_nmx", [P, NT])
        sc = st.sb("ro_sc", [P, NT, NE])
        top = st.sb("ro_top", [P, NT, 8])
        idx = st.sb("ro_idx", [P, NT, 8], U32)
        idf = st.sb("ro_idf", [P, NT, 8])
        ex, sel = tiles.ex, tiles.sel
        picked = st.sb("ro_picked", [P, TOPK, NT, NE])
        chosen = st.sb("ro_chosen", [P, NT, NE], BF16)
        before = st.sb("ro_before", [P, P], BF16)
        ones = st.sb("ro_ones", [P, P], BF16)
        full = st.sb("ro_full", [P, NE])
        ends = st.sb("ro_ends", [P, 2, NE + NE // 2])
        first = st.sb("ro_first", [P, NE])
        slot = st.sb("ro_slot", [P, NT, NE])
        pos = st.sb("ro_pos", [P, PAIRS])
        tile = st.sb("ro_tile", [P, PAIRS])
        place = st.sb("ro_place", [P, PAIRS])
        in_tile = st.sb("ro_in_tile", [P, PAIRS, NTILE], F32R)
        in_place = st.sb("ro_in_place", [P, PAIRS, P], F32R)
        number = st.sb("ro_number", [P, NTILE])
        empty = st.sb("ro_empty", [P, NTILE])
        over = st.sb("ro_over", [NTILE, NE])
        owner = st.sb("ro_owner", [NTILE, 2])
        psX = st.ps("ro_psX", [P, 2, 512])
        psL = st.ps("ro_psL", [P, 512])
        psR = st.ps("ro_psR", [P, 512])
        psN = st.ps("ro_psN", [P, 512])
        psP = st.ps("ro_psP", [P, 512])
        s = {n: st.sem("ro_" + n) for n in (
            "xT", "xt", "logits", "shift", "exped", "dve", "bf16", "chosen", "ranked", "located",
            "numbered", "owned", "rowed", "placed", "ordered", "rows")}
        block = stack.enter_context(nc.Block())

        @block.sync
        def _(sp):
            sp.dma_start(rows.rearrange("(t p) d -> p t d", p=P), X[:]).then_inc(s["rows"], 16)
            sp.wait_ge(s["rows"], 16)

        @block.tensor
        def _(pe):
            def turn(t):
                need(pe, s["xt"], t - 1)
                for k in range(KD):
                    last = nc.tensor.transpose(psX[:, t % 2, k * P:(k + 1) * P],
                                               X[:, t, k * P:(k + 1) * P], c["ident"][:, :])
                last.then_inc(s["xT"], 1)

            def logit(t):
                pe.wait_ge(s["xt"], t + 1)
                if t == 0:
                    pe.wait_ge(loads["gate"], 16)
                for k in range(KD):
                    last = nc.tensor.matmul(psL[:, t * NE:(t + 1) * NE], XT[:, t % 2, k, :], GW[:, k, :],
                                            start=(k == 0), stop=(k == KD - 1))
                last.then_inc(s["logits"], 1)

            staggered([turn, None, logit])
            pe.wait_ge(s["bf16"], 1)
            pe.wait_ge(s["chosen"], 1)
            for t in range(NT):
                nc.tensor.matmul(psN[:, 0:NE], ones[:, :], chosen[:, t, :], start=(t == 0), stop=(t == NT - 1))
            nc.tensor.matmul(psR[:, 0:NT * NE], before[:, :], chosen.rearrange("p t e -> p (t e)"),
                             start=True, stop=False)
            for t in range(NT - 1):
                later = NT - 1 - t
                last = nc.tensor.matmul(psR[:, (t + 1) * NE:NT * NE], ones[:, :],
                                        chosen[:, t, :].unsqueeze(1).to_broadcast([P, later, NE]),
                                        start=False, stop=(t == NT - 2))
            last.then_inc(s["ranked"], 1)
            pe.wait_ge(s["owned"], 1)
            for n in range(2):
                last = nc.tensor.matmul(psN[0:1, (n + 1) * P:(n + 1) * P + NTILE], owner[:, n:n + 1],
                                        c["ident"][0:NTILE, 0:NTILE], start=True, stop=True)
            last.then_inc(s["rowed"], 1)
            for i in range(PAIRS):
                if i % NT == 0:
                    pe.wait_ge(s["numbered"], i // NT + 1)
                    pe.wait_ge(s["placed"], i // NT + 1)
                last = nc.tensor.matmul(psP[:, 0:NTILE], in_place[:, i, :], in_tile[:, i, :],
                                        start=(i == 0), stop=(i == PAIRS - 1))
            last.then_inc(s["ordered"], 1)

        @block.scalar
        def _(act):
            nc.scalar.activation(nmx[:, :], c["ones"][:, 0:NT], ACT.Exp)
            nc.scalar.activation(before[:, :], c["before"], ACT.Copy)
            nc.scalar.activation(ones[:, :], c["ones"], ACT.Copy).then_inc(s["bf16"], 1)
            for t in range(NT):
                act.wait_ge(s["xT"], t + 1)
                need(act, s["logits"], t - 1)
                nc.scalar.activation(XT[:, t % 2], psX[:, t % 2, 0:D].rearrange("p (k t) -> p k t", k=KD),
                                     ACT.Copy).then_inc(s["xt"], 1)
            act.wait_ge(s["logits"], NT)
            nc.scalar.activation(sc[:, :, :], psL[:, 0:NT * NE].rearrange("p (t e) -> p t e", t=NT),
                                 ACT.Exp, scale=-1.0).then_inc(s["exped"], 1)
            act.wait_ge(s["shift"], 1)
            for t in range(NT):
                last = nc.scalar.activation(ex[:, t, :], lg[:, t, :], ACT.Exp, bias=nmx[:, t:t + 1])
            last.then_inc(s["exped"], 1)

        @block.gpsimd
        def _(pool):
            for k in range(TOPK):
                which = slice(k * NT, (k + 1) * NT)
                pool.wait_ge(s["located"], k + 1)
                pool.tensor_tensor(in_tile[:, which, :], in_tile[:, which, :].bitcast(F32),
                                   c["pairs"][:, which].unsqueeze(2).to_broadcast([P, NT, NTILE]),
                                   ALU.mult).then_inc(s["numbered"], 1)

        @block.vector
        def _(dve):
            link = Chain(dve, s["dve"]).link
            nc.vector.memset(tiles.owner[:, :], 0)
            nc.vector.memset(tiles.chunk[:, :], 0)
            nc.vector.memset(tiles.index[:, :, :], 0)
            link(nc.vector.memset(ends[:, :, :], 0.0))
            dve.wait_ge(s["exped"], 1)
            link(nc.vector.tensor_scalar(sc[:, :, :], sc[:, :, :], 1.0, None, ALU.add))
            link(nc.vector.reciprocal(sc[:, :, :], sc[:, :, :]))
            for t in range(NT):
                last = nc.vector.max(top[:, t, :], sc[:, t, :])
            link(last)
            for t in range(NT):
                last = nc.vector.max_index(idx[:, t, :], top[:, t, :], sc[:, t, :])
            link(last)
            link(nc.vector.tensor_copy(idf[:, :, :], idx[:, :, :]))
            link(nc.vector.tensor_tensor(
                sel[:, :, :, :], c["slots"][:, 0:NE].unsqueeze(1).unsqueeze(1).to_broadcast([P, TOPK, NT, NE]),
                idf[:, :, 0:TOPK].rearrange("p t k -> p k t").unsqueeze(3).to_broadcast([P, TOPK, NT, NE]),
                ALU.is_equal))
            link(nc.vector.tensor_reduce(lg[:, :, :], sel.rearrange("p k t e -> p t e k"), AX.X, ALU.add))
            nc.vector.tensor_copy(chosen[:, :, :], lg[:, :, :]).then_inc(s["chosen"], 1)
            dve.wait_ge(s["chosen"], 1)
            link(nc.vector.tensor_copy(lg[:, :, :], psL[:, 0:NT * NE].rearrange("p (t e) -> p t e", t=NT)))
            nc.vector.tensor_reduce(nmx[:, :], lg[:, :, :], AX.X, ALU.max, negate=True).then_inc(s["shift"], 1)
            dve.wait_ge(s["ranked"], 1)
            link(nc.vector.tensor_scalar(full[:, :], psN[:, 0:NE], 1.0 / P, (P - 1) / (2.0 * P), ALU.mult, ALU.add))
            link(nc.vector.tensor_scalar(full[:, :], full[:, :], MAGIC, MAGIC, ALU.add, ALU.subtract))
            pad = NE // 2
            link(nc.vector.tensor_copy(ends[:, 0, pad:], full[:, :]))
            a, step = 0, 1
            while step < NE:
                link(nc.vector.tensor_tensor(ends[:, 1 - a, pad:], ends[:, a, pad:],
                                             ends[:, a, pad - step:pad + NE - step], ALU.add))
                a, step = 1 - a, 2 * step
            end = ends[:, a, pad:]
            link(nc.vector.tensor_tensor(first[:, :], end, full[:, :], ALU.subtract))
            link(nc.vector.tensor_scalar(first[:, :], first[:, :], float(P), None, ALU.mult))
            link(nc.vector.tensor_tensor(slot[:, :, :], psR[:, 0:NT * NE].rearrange("p (t e) -> p t e", t=NT),
                                         first[:, :].unsqueeze(1).to_broadcast([P, NT, NE]), ALU.add))
            link(nc.vector.tensor_tensor(picked[:, :, :, :], sel[:, :, :, :],
                                         slot[:, :, :].unsqueeze(1).to_broadcast([P, TOPK, NT, NE]), ALU.mult))
            link(nc.vector.tensor_reduce(pos[:, :], picked.rearrange("p k t e -> p (k t) e"), AX.X, ALU.add))
            link(nc.vector.tensor_scalar(over[:, :], end[0:NTILE, :], c["pairs"][0:NTILE, 0:1], None, ALU.is_lt))
            nc.vector.tensor_reduce(owner[:, 1:2], over.rearrange("p (c g) -> p c g", g=2)[:, :, 1], AX.X, ALU.add)
            nc.vector.tensor_reduce(owner[:, 0:1], over[:, :], AX.X, ALU.add).then_inc(s["owned"], 1)
            link(nc.vector.tensor_scalar(tile[:, :], pos[:, :], 1.0 / P, -(P - 1) / (2.0 * P), ALU.mult, ALU.add))
            link(nc.vector.tensor_scalar(tile[:, :], tile[:, :], MAGIC, MAGIC, ALU.add, ALU.subtract))
            link(nc.vector.scalar_tensor_tensor(out=place[:, :], in0=tile[:, :], scalar=-float(P), in1=pos[:, :],
                                                op0=ALU.mult, op1=ALU.add))
            for k in range(TOPK):
                which = slice(k * NT, (k + 1) * NT)
                for out, width, of, done in ((in_tile, NTILE, tile, "located"), (in_place, P, place, "placed")):
                    nc.vector.tensor_tensor(out[:, which, :],
                                            c["slots"][:, 0:width].unsqueeze(1).to_broadcast([P, NT, width]),
                                            of[:, which].unsqueeze(2).to_broadcast([P, NT, width]),
                                            ALU.is_equal).then_inc(s[done], 1)
            dve.wait_ge(s["rowed"], 1)
            nc.vector.tensor_scalar(tiles.owner[:, 4:4 + NTILE], psN[0:1, P:P + NTILE], NE - 1.0, None, ALU.min)
            nc.vector.tensor_scalar(tiles.chunk[:, 4:4 + NTILE], psN[0:1, 2 * P:2 * P + NTILE], NC - 1.0, None,
                                    ALU.min)
            dve.wait_ge(s["ordered"], 1)
            link(nc.vector.tensor_scalar(empty[:, :], psP[:, 0:NTILE], 0.0, c["past"][:, 0:1],
                                         ALU.is_equal, ALU.mult))
            link(nc.vector.scalar_tensor_tensor(out=number[:, :], in0=psP[:, 0:NTILE], scalar=-1.0,
                                                in1=empty[:, :], op0=ALU.add, op1=ALU.add))
            target = tiles.index[:, LAG:LAG + NTILE, 1]
            link(nc.vector.tensor_copy(target, number[:, :]))
            nc.vector.tensor_scalar(tiles.index[:, 0:NTILE, 0], target, NT * P - 1, None, ALU.bitwise_and)


class Weights:

    def __init__(self, st):
        self.w_in = st.sb("w_in", [P, NE * KD, 2 * INTER])
        self.c_in = st.sb("c_in", [P, NC * KD, 2 * CINTER])
        self.w_out = st.sb("w_out", [P, NE, D])
        self.c_out = st.sb("c_out", [P, NC, D])


LAG = 6


class Tiles:

    def __init__(self, st):
        self.owner = st.sb("ti_owner", [1, NTILE + 8], mybir.dt.int32)
        self.chunk = st.sb("ti_chunk", [1, NTILE + 8], mybir.dt.int32)
        self.index = st.sb("ti_index", [P, NTILE + 8, 2], U32)
        self.ex = st.sb("ti_ex", [P, NT, NE])
        self.sel = st.sb("ti_sel", [P, TOPK, NT, NE])
        self.weight = st.sb("ti_weight", [P, TOPK, NT])
        self.total = st.sb("ti_total", [P, NT])


def experts(nc, c, tiles, W, rows, pairs, loads):
    NB = NTILE // 4
    with ExitStack() as stack:
        st = Store(nc, stack)
        xg = st.sb("ex_xg", [P, 4, D])
        xt = st.sb("ex_xt", [P, 2, KD, P])
        sg = st.sb("ex_sg", [P, 2, INTER + CINTER])
        a = st.sb("ex_a", [P, 2, 2, P])
        aT = st.sb("ex_aT", [P, 2, 2, P])
        y = st.sb("ex_y", [P, 4, D])
        index = st.sb("ex_index", [P, 4, 2], U32)
        picked = st.sb("ex_picked", [P, TOPK, NT, NE])
        psX = st.ps("ex_psX", [P, 2, 512])
        psG = st.ps("ex_psG", [P, 2, 512])
        psA = st.ps("ex_psA", [P, 2, 512])
        psD = st.ps("ex_psD", [P, 2, 512])
        gathered = [st.sem("ex_gathered%d" % i) for i in range(4)]
        scattered = [st.sem("ex_scattered%d" % i) for i in range(4)]
        s = {n: st.sem("ex_" + n) for n in (
            "padded",
            "passed",
            "weighted",
            "aimed",
            "xturned", "xcopied", "hidden", "gated", "acted", "aturned", "acopied", "downed", "ycopied")}
        block = stack.enter_context(nc.Block())

        def run(eng, body, lag, peeled=1):
            for I in range(peeled):
                for u in range(4):
                    body(4 * I + u, u, I)
            with eng.Fori(peeled, NB) as I:
                for u in range(4):
                    body(I * 4 + u, u, I)
            for k in range(NTILE, NTILE + lag):
                body(k, k % 4, k // 4)

        def lagging(k, u, I, lag):
            if isinstance(k, int) and not 0 <= k - lag < NTILE:
                return None
            return k - lag, (u - lag) % 4, I + (u - lag) // 4

        @block.gpsimd
        def _(pool):
            for n in range(2):
                last = pool.memset(a[:, n, 0, :], 0.0)
            last.then_inc(s["padded"], 1)

            def aim(n, K, J):
                for u in (2 * n, 2 * n + 1):
                    need(pool, gathered[u], 16 * (min(J, NB) if isinstance(J, int) else J))
                    need(pool, scattered[(u - LAG) % 4], 16 * (J + (u - LAG) // 4))
                hold(pool, s["passed"])
                pool.tensor_copy(index[:, 2 * n:2 * n + 2, :],
                                 tiles.index[:, bass.ds(K + 2 * n, 2), :]).then_inc(s["aimed"], 1)

            def body(k, u, I):
                if u == 1:
                    aim(1, k - 1, I)
                if u == 3:
                    aim(0, k + 1, I + 1)
                now = lagging(k, u, I, 0)
                if now:
                    pool.wait_ge(s["aimed"], 2 * I + 1 + u // 2)
                    need(pool, s["xturned"], k - 3)
                    hold(pool, s["passed"])
                    pool.indirect_dma_start(
                        out=xg[:, u, :], out_offset=None, in_=rows,
                        in_offset=bass.IndirectOffsetOnAxis(ap=index[:, u, 0:1], axis=0),
                        bounds_check=NT * P - 1, oob_is_err=True).then_inc(gathered[u], 16)
                late = lagging(k, u, I, LAG)
                if late:
                    j, v, J = late
                    pool.wait_ge(s["ycopied"], j + 1)
                    if not now:
                        pool.wait_ge(s["aimed"], 2 * I + 1 + u // 2)
                    hold(pool, s["passed"])
                    pool.indirect_dma_start(
                        out=pairs, out_offset=bass.IndirectOffsetOnAxis(ap=index[:, u, 1:2], axis=0),
                        in_=y[:, v, :], in_offset=None, bounds_check=TOPK * NT * P - 1,
                        oob_is_err=False).then_inc(scattered[v], 16)

            aim(0, 0, 0)
            run(pool, body, LAG, peeled=2)
            for v in range(4):
                pool.wait_ge(scattered[v], 16 * NB)
                pool.wait_ge(gathered[v], 16 * NB)

        @block.tensor
        def _(pe):
            held = []

            def body(k, u, I):
                now = lagging(k, u, I, 0)
                one = lagging(k, u, I, 1)
                if u == 0:
                    held[:] = [nc.values_load_multi_w_load_instructions(
                        table[0:1, bass.ds(k, 8)], engines=(mybir.EngineType.PE,), min_val=0, max_val=n - 1,
                        skip_runtime_bounds_check_because="route takes the minimum with n - 1")[1]
                        for table, n in ((tiles.owner, NE), (tiles.chunk, NC))]

                def expert_of(lag):
                    return held[0][4 + u - lag], held[1][4 + u - lag]

                if now:
                    pe.wait_ge(gathered[u], 16 * I + 16)
                    need(pe, s["xcopied"], k - 1)
                    for kk in range(KD):
                        last = nc.tensor.transpose(psX[:, u % 2, kk * P:(kk + 1) * P],
                                                   xg[:, u, kk * P:(kk + 1) * P], c["ident"][:, :])
                    last.then_inc(s["xturned"], 1)
                if one:
                    j, v, J = one
                    e, ch = expert_of(1)
                    pe.wait_ge(s["xcopied"], j + 1)
                    need(pe, s["acted"], j - 1)
                    if isinstance(j, int) and j == 0:
                        pe.wait_ge(loads["w_in"], 16)
                        pe.wait_ge(loads["c_in"], 16)
                    for kk in range(KD):
                        nc.tensor.matmul(psG[:, v % 2, 0:2 * INTER], xt[:, v % 2, kk, :],
                                         W.w_in[:, bass.ds(e * KD + kk, 1), :].rearrange("p a n -> p (a n)"),
                                         start=(kk == 0), stop=(kk == KD - 1))
                    for kk in range(KD):
                        last = nc.tensor.matmul(psG[:, v % 2, 2 * INTER:2 * (INTER + CINTER)], xt[:, v % 2, kk, :],
                                                W.c_in[:, bass.ds(ch * KD + kk, 1), :].rearrange("p a n -> p (a n)"),
                                                start=(kk == 0), stop=(kk == KD - 1))
                    last.then_inc(s["hidden"], 1)
                three = lagging(k, u, I, 3)
                two = lagging(k, u, I, 2)
                if two:
                    j, v, J = two
                    pe.wait_ge(s["acted"], j + 1)
                    need(pe, s["acopied"], j - 1)
                    for n in range(2):
                        last = nc.tensor.transpose(psA[:, v % 2, n * P:(n + 1) * P], a[:, v % 2, n, :],
                                                   c["ident"][:, :])
                    last.then_inc(s["aturned"], 1)
                if three:
                    j, v, J = three
                    e, ch = expert_of(3)
                    pe.wait_ge(s["acopied"], j + 1)
                    need(pe, s["ycopied"], j - 1)
                    if isinstance(j, int) and j == 0:
                        pe.wait_ge(loads["w_out"], 16)
                        pe.wait_ge(loads["c_out"], 16)
                    nc.tensor.matmul(psD[:, v % 2, 0:D], aT[0:INTER, v % 2, 0, :],
                                     W.w_out[0:INTER, bass.ds(e, 1), :].rearrange("p a n -> p (a n)"),
                                     start=True, stop=False)
                    nc.tensor.matmul(psD[:, v % 2, 0:D], aT[:, v % 2, 1, :],
                                     W.c_out[:, bass.ds(ch, 1), :].rearrange("p a n -> p (a n)"),
                                     start=False, stop=True).then_inc(s["downed"], 1)

            run(pe, body, 3, peeled=2)

        @block.scalar
        def _(act):
            def body(k, u, I):
                now = lagging(k, u, I, 0)
                if now:
                    act.wait_ge(s["xturned"], k + 1)
                    need(act, s["hidden"], k - 1)
                    nc.scalar.activation(xt[:, u % 2], psX[:, u % 2, 0:D].rearrange("p (k t) -> p k t", k=KD),
                                         ACT.Copy).then_inc(s["xcopied"], 1)
                one = lagging(k, u, I, 1)
                if one:
                    j, v, J = one
                    act.wait_ge(s["hidden"], j + 1)
                    need(act, s["acted"], j - 1)
                    nc.scalar.activation(sg[:, v % 2, 0:INTER], psG[:, v % 2, 0:INTER], ACT.Silu)
                    nc.scalar.activation(sg[:, v % 2, INTER:], psG[:, v % 2, 2 * INTER:2 * INTER + CINTER],
                                         ACT.Silu).then_inc(s["gated"], 1)
                three = lagging(k, u, I, 3)
                if three:
                    j, v, J = three
                    act.wait_ge(s["downed"], j + 1)
                    need(act, scattered[v], 16 * J)
                    nc.scalar.activation(y[:, v, :], psD[:, v % 2, 0:D], ACT.Copy).then_inc(s["ycopied"], 1)

            run(act, body, 3, peeled=2)

        @block.vector
        def _(dve):
            dve.wait_ge(s["padded"], 1)

            def body(k, u, I):
                one = lagging(k, u, I, 1)
                if one:
                    j, v, J = one
                    dve.wait_ge(s["gated"], j + 1)
                    need(dve, s["aturned"], j - 1)
                    nc.vector.tensor_tensor(a[:, v % 2, 0, 0:INTER], psG[:, v % 2, INTER:2 * INTER],
                                            sg[:, v % 2, 0:INTER], ALU.mult)
                    nc.vector.scalar_tensor_tensor(out=a[:, v % 2, 1, :],
                                                   in0=psG[:, v % 2, 2 * INTER + CINTER:2 * (INTER + CINTER)],
                                                   scalar=SMALL_SCALE, in1=sg[:, v % 2, INTER:],
                                                   op0=ALU.mult, op1=ALU.mult).then_inc(s["acted"], 1)
                two = lagging(k, u, I, 2)
                if two:
                    j, v, J = two
                    dve.wait_ge(s["aturned"], j + 1)
                    need(dve, s["downed"], j - 1)
                    nc.vector.tensor_copy(aT[:, v % 2], psA[:, v % 2, 0:2 * P].rearrange("p (n t) -> p n t", n=2)
                                          ).then_inc(s["acopied"], 1)

            run(dve, body, 3)
            link = Chain(dve, s["weighted"]).link
            link(nc.vector.tensor_tensor(picked[:, :, :, :], tiles.sel[:, :, :, :],
                                         tiles.ex[:, :, :].unsqueeze(1).to_broadcast([P, TOPK, NT, NE]), ALU.mult))
            link(nc.vector.tensor_reduce(tiles.weight[:, :, :], picked[:, :, :, :], AX.X, ALU.add))
            link(nc.vector.tensor_reduce(tiles.total[:, :], tiles.weight.rearrange("p k t -> p t k"), AX.X, ALU.add))
            link(nc.vector.reciprocal(tiles.total[:, :], tiles.total[:, :]))
            nc.vector.tensor_tensor(tiles.weight[:, :, :], tiles.weight[:, :, :],
                                    tiles.total[:, :].unsqueeze(1).to_broadcast([P, TOPK, NT]), ALU.mult)


def combine(nc, c, X, tiles, pairs, out):
    with ExitStack() as stack:
        st = Store(nc, stack)
        ln = Norm(nc, c, st, "co")
        Z = st.sb("co_Z", [P, NT, D])
        G = st.sb("co_G", [P, NT, TOPK, D])
        came = [st.sem("co_came%d" % t) for t in range(NT)]
        written = st.sem("co_written")
        summed = st.sem("co_summed")
        order = st.sem("co_pool")
        scaled = st.sem("co_scaled")
        by_pool = (1, 3, 6)
        by_vector = ((0, 2), (4, 5), (7,))
        view = pairs.rearrange("(k t p) d -> t p k d", k=TOPK, p=P)
        block = stack.enter_context(nc.Block())

        @block.sync
        def _(sp):
            for t in range(0, NT):
                sp.dma_start(G[:, t], view[t]).then_inc(came[t], 16)
            for n in range(2):
                sp.wait_ge(ln.normed, 4 * n + 4)
                sp.dma_start(out[4 * n:4 * n + 4].rearrange("t p d -> p t d"),
                             Z[:, 4 * n:4 * n + 4, :]).then_inc(written, 16)
            sp.wait_ge(written, 32)

        @block.scalar
        def _(act):
            for t in by_pool:
                act.wait_ge(came[t], 16)
                for k in range(TOPK):
                    last = nc.scalar.activation(G[:, t, k, :], G[:, t, k, :], ACT.Copy,
                                                scale=tiles.weight[:, k, t:t + 1])
                last.then_inc(scaled, 1)
            ln.root(act)

        @block.gpsimd
        def _(pool):
            link = Chain(pool, order).link
            for n, t in enumerate(by_pool):
                pool.wait_ge(scaled, n + 1)
                for k in range(TOPK):
                    last = pool.tensor_tensor(ln.R[:, t, :], X[:, t, :] if k == 0 else ln.R[:, t, :],
                                              G[:, t, k, :], ALU.add)
                    if k < TOPK - 1:
                        link(last)
                last.then_inc(summed, 1)

        @block.vector
        def _(dve):
            ln.begin(dve)
            for group in by_vector:
                for t in group:
                    dve.wait_ge(came[t], 16)
                for k in range(TOPK):
                    for t in group:
                        last = nc.vector.scalar_tensor_tensor(
                            out=ln.R[:, t, :], in0=G[:, t, k, :], scalar=tiles.weight[:, k, t:t + 1],
                            in1=X[:, t, :] if k == 0 else ln.R[:, t, :], op0=ALU.mult, op1=ALU.add)
                    ln.chain.link(last)
                for t in group:
                    ln.stat(t, last=False)
            for n, t in enumerate(by_pool):
                dve.wait_ge(summed, n + 1)
                ln.stat(t, last=(n == len(by_pool) - 1))
            ln.apply(dve, Z)



TABLE = dict(ident=P, ones=P, hm=8, hx=4, pm=2, slots=P, before=P, pairs=TOPK * NT, past=1, cos0=S, sin0=S, causal=2 * S, window=2 * S,
             cos1=2 * D1, sin1=2 * D1, eps=1)


def decoder(nc, x, xT, ctx, ctxT, tok, w0, wo0, gamma, wu, wd, had, w1, bias1, wo1, bo1, sinks, gate,
            w_in, w_out, c_in, c_out, table, out, stop=99):
    stack = ExitStack()
    with stack:
        Store.spent.clear()
        top = Store(nc, stack, passing=False)
        X = top.sb("X", [P, NT, D])
        TB = top.sb("table", [P, sum(TABLE.values())])
        identb = top.sb("identb", [P, P], BF16)
        CT = top.sb("CT", [P, B, KD, D])
        TOK = top.sb("TOK", [P, NT], mybir.dt.int32)
        GM = top.sb("GM", [P, 1])
        loads = {n: top.sem("load_" + n) for n in (
            "x", "xT0", "xT1", "w0q", "w0k", "w0v", "consts", "ctx", "ctxT", "tok", "gamma", "wo0", "wff", "had", "w1",
            "bias1", "wo1", "sinks", "bo1", "gate", "w_in", "c_in", "w_out", "c_out")}
        rows = nc.dram_tensor("rows", (NT * P, D), F32, kind="Internal").ap()
        pairs = nc.dram_tensor("pairs", (TOPK * NT * P, D), F32, kind="Internal").ap()
        c, at = {}, 0
        for n, width in TABLE.items():
            c[n] = TB[:, at:at + width]
            at += width
        for n in ("causal", "window"):
            c[n] = c[n].rearrange("p (h s) -> p h s", h=2)
        for n in ("cos1", "sin1"):
            c[n] = c[n].rearrange("p (h d) -> p h d", h=2)
        c["identb"] = identb
        c["rsqrt512"] = RSQRT512

        early = ExitStack()
        ea = Store(nc, early)
        W1 = ea.sb("W1", [P, KD, NQ1 + 2 * NKV1])
        BO1 = ea.sb("BO1", [P, D])
        SK = ea.sb("SK", [P, H1])
        WO1 = W1.rearrange("p k n -> p (k n)")[:, 0:2 * HKV * D].rearrange("p (v o) -> p v o", o=D)
        with ExitStack() as layer0:
            l0 = Store(nc, layer0)
            CTX = l0.sb("CTX", [P, NT, D])
            WO0 = l0.sb("WO0", [P, 4, D])
            WU = l0.sb("WU", [P, KD, I0])
            WD = l0.sb("WD", [P, I0 // P, D])
            HAD = l0.sb("HAD", [P, KD, D])
            ternary = Ternary(l0)
            with ExitStack() as attn0:
                a0 = Store(nc, attn0)
                XT = a0.sb("XT", [P, KD, B * S])
                W0 = a0.sb("W0", [P, 5, KD, D])
                QT = a0.sb("QT", [P, B * KD, S])
                KT = a0.sb("KT", [P, B * KD, S])
                V = a0.sb("V", [P, 16, 2, 64])
                AT = a0.sb("AT", [P, 16, S])
                with nc.Block() as block:
                    @block.sync
                    def _(sp):
                        xTs = xT.rearrange("(k p) s -> p k s", p=P)
                        for n in range(2):
                            sp.dma_start(XT[:, :, n * 512:(n + 1) * 512],
                                         xTs[:, :, n * 512:(n + 1) * 512]).then_inc(loads["xT%d" % n], 16)
                        sp.dma_start(TB[:], table).then_inc(loads["consts"], 16)
                        sp.dma_start(X[:], x.rearrange("t p d -> p t d")).then_inc(loads["x"], 16)
                        sp.dma_start(WO0[:], wo0.rearrange("g p o -> p g o")).then_inc(loads["wo0"], 16)
                        sp.dma_start(WU[:], wu.rearrange("(k p) o -> p k o", p=P)).then_inc(loads["wff"], 16)
                        sp.dma_start(WD[:], wd.rearrange("(k p) o -> p k o", p=P)).then_inc(loads["wff"], 16)
                        sp.dma_start(HAD[:], had.rearrange("(k p) o -> p k o", p=P)).then_inc(loads["had"], 16)

                    @block.scalar
                    def _(act):
                        for n, m in (("q", slice(0, 2)), ("k", slice(2, 4)), ("v", slice(4, 5))):
                            act.dma_start(W0[:, m], w0[m].rearrange("m (k p) o -> p m k o", p=P)
                                          ).then_inc(loads["w0" + n], 16)
                        act.dma_start(CTX[:], ctx.rearrange("t p d -> p t d")).then_inc(loads["ctx"], 16)
                        act.dma_start(CT[:], ctxT.rearrange("b (k p) s -> p (b k) s", p=P)).then_inc(loads["ctxT"], 16)
                        act.dma_start(TOK[:], tok).then_inc(loads["tok"], 16)
                        act.dma_start(GM[:], gamma.to_broadcast([P, 1])).then_inc(loads["gamma"], 16)
                        act.dma_start(W1[:], w1.rearrange("(k p) o -> p k o", p=P)).then_inc(loads["w1"], 16)
                        act.dma_start(SK[:], sinks.to_broadcast([P, H1])).then_inc(loads["sinks"], 16)
                        act.dma_start(BO1[:], bo1.to_broadcast([P, D])).then_inc(loads["bo1"], 16)

                project_0(nc, c, XT, W0, QT, KT, V, WU, WD, ternary, loads)

                def stage_q0(Qs, w, r, I):
                    return nc.vector.tensor_copy(Qs[:, 0, :], QT[:, I, :])

                def stage_k0(pool, KM, w, r, I):
                    return spread(pool, KM, KT[:, I, :], c["hm"][:, 4 * r:4 * r + 4])

                def stage_v0(Vs, w, r, I):
                    return nc.scalar.activation(
                        Vs.rearrange("p k (h d) -> p k h d", h=4)[:, :, :, 0:DK0],
                        V[:, w, :, :].rearrange("p k (h d) -> p k h d", h=4), ACT.Copy)

                attention(nc, c, "a0", 16, stage_q0, stage_k0, stage_v0,
                          lambda w, half: AT[:, w, half * P:(half + 1) * P], width=32, pairs=False,
                          mask=c["causal"], causal=True, scale=0.25)

                def product0(pe, out, t):
                    if t == 0:
                        pe.wait_ge(loads["wo0"], 16)
                    for g in range(4):
                        last = nc.tensor.matmul(out, AT[:, (t // 2) * 4 + g, (t % 2) * P:(t % 2 + 1) * P],
                                                WO0[:, g, :], start=(g == 0), stop=(g == 3))
                    return last

                with nc.Block() as block:
                    @block.vector
                    def _(dve):
                        dve.wait_ge(loads["x"], 16)
                        nc.vector.tensor_copy(identb[:], c["ident"])
                output_norm(nc, c, "o0", X, product0)

            if stop > 1:
                with ExitStack() as attnx:
                    ax = Store(nc, attnx)
                    Y = ax.sb("Y", [P, NT, D])

                    def stage_qx(Qs, w, r, I):
                        return nc.vector.tensor_copy(Qs[:, 0, :], X[:, w, :])

                    def stage_kx(pool, KM, w, r, I):
                        if isinstance(w, int) and w == 0:
                            pool.wait_ge(loads["ctx"], 16)
                        return spread(pool, KM, CTX[:, w, :], c["hx"])

                    def stage_vx(Vs, w, r, I):
                        if isinstance(w, int) and w == 0:
                            nc.scalar.wait_ge(loads["ctxT"], 16)
                        return nc.scalar.activation(Vs, CT[:, I, :, r * P:(r + 1) * P], ACT.Copy)

                    attention(nc, c, "ax", 8, stage_qx, stage_kx, stage_vx,
                              lambda w, half: Y[:, w, half * P:(half + 1) * P], width=32, pairs=False,
                              scale=INV_SQRT32)
                    with nc.Block() as block:
                        @block.vector
                        def _(dve):
                            dve.wait_ge(loads["gamma"], 16)
                    cross_norm(nc, c, X, Y, GM)

            if stop > 2:
                feed_forward_0(nc, c, X, HAD, ternary, loads)

        recycle(nc)
        if stop > 3:
            with ExitStack() as layer1:
                l1 = Store(nc, layer1)
                NSK = l1.sb("NSK", [P, H1])
                QT1 = l1.sb("QT1", [P, 32, 2, S])
                KT1 = l1.sb("KT1", [P, 32, S])
                V1 = l1.sb("V1", [P, 32, 2, D1])
                with ExitStack() as proj1:
                    BIAS = Store(nc, proj1).sb("BIAS", [P, NQ1 + 2 * NKV1])
                    with nc.Block() as block:
                        @block.sync
                        def _(sp):
                            sp.dma_start(BIAS[:], bias1.to_broadcast([P, NQ1 + 2 * NKV1])).then_inc(loads["bias1"], 16)
                    project_1(nc, c, X, W1, BIAS, QT1, KT1, V1, loads)
                with nc.Block() as block:
                    @block.sync
                    def _(sp):
                        sp.dma_start(WO1, wo1.rearrange("(v p) o -> p v o", p=P)).then_inc(loads["wo1"], 16)

                    @block.vector
                    def _(dve):
                        dve.wait_ge(loads["sinks"], 16)
                        nc.vector.tensor_scalar(NSK[:], SK[:], -1.0, None, ALU.mult)

                def stage_q1(Qs, w, r, I):
                    return nc.vector.tensor_copy(Qs, QT1[:, w, :, :])

                def stage_k1(pool, KM, w, r, I):
                    return spread(pool, KM, KT1[:, w, :], c["pm"])

                def stage_v1(Vs, w, r, I):
                    return nc.scalar.activation(Vs, V1[:, w, :, :], ACT.Copy)

                def sinks_of(w, r, I):
                    at = bass.ds((I // 2) * 4, 4)
                    return SK[:, at], NSK[:, at]

                attention(nc, c, "a1", 32, stage_q1, stage_k1, stage_v1,
                          lambda w, half: QT1[:, w, :, half * P:(half + 1) * P], width=64, pairs=True,
                          mask=c["window"], sinks_of=sinks_of)

                with nc.Block() as block:

                    @block.vector
                    def _(dve):
                        dve.wait_ge(loads["bo1"], 16)
                        for t in range(NT):
                            nc.vector.tensor_tensor(X[:, t, :], X[:, t, :], BO1[:], ALU.add)

                def product1(pe, out, t):
                    if t == 0:
                        pe.wait_ge(loads["wo1"], 16)
                    for i in range(2 * HKV):
                        last = nc.tensor.matmul(
                            out, QT1[:, (i // 2) * B + t // 2, i % 2, (t % 2) * P:(t % 2 + 1) * P],
                            WO1[:, i, :], start=(i == 0), stop=(i == 2 * HKV - 1))
                    return last

                output_norm(nc, c, "o1", X, product1)

        early.close()
        tiles = Tiles(top)
        if stop > 4:
            with ExitStack() as moe:
                m = Store(nc, moe)
                W = Weights(m)
                GW = m.sb("GW", [P, KD, NE])
                with nc.Block() as block:
                    @block.sync
                    def _(sp):
                        sp.dma_start(GW[:], gate.rearrange("(k p) e -> p k e", p=P)).then_inc(loads["gate"], 16)
                        sp.dma_start(W.w_in[:], w_in).then_inc(loads["w_in"], 16)
                        sp.dma_start(W.c_in[:], c_in).then_inc(loads["c_in"], 16)
                        sp.dma_start(W.w_out[0:INTER], w_out).then_inc(loads["w_out"], 16)
                        sp.dma_start(W.c_out[:], c_out).then_inc(loads["c_out"], 16)
                token_experts(nc, c, X, CT, TOK, loads)
                if stop > 5:
                    route(nc, c, X, GW, tiles, loads, rows)
                    experts(nc, c, tiles, W, rows, pairs, loads)
            if stop > 5:
                combine(nc, c, X, tiles, pairs, out)
        if stop > 5:
            pass
        else:
            with nc.Block() as block:
                @block.sync
                def _(sp):
                    wr = top.sem("dbg")
                    sp.dma_start(out.rearrange("t p d -> p t d"), X[:]).then_inc(wr, 16)
                    sp.wait_ge(wr, 16)
                    for n in ("ctx", "ctxT", "tok", "gamma","wo0","had","x","consts","w1","sinks","bo1"):
                        sp.wait_ge(loads[n],16)
                    sp.wait_ge(loads["wff"],32)


import numpy as np

RSQRT512 = float(np.float32(1.0) / np.sqrt(np.float32(512.0)))
INV_SQRT32 = float(np.float32(1.0) / np.sqrt(np.float32(32.0)))


def constants():
    f = np.float32
    part = np.arange(P)
    inv0 = f(1.0) / f(10000.0) ** (np.arange(0, DK0, 2, dtype=f) / f(DK0))
    ang0 = np.outer(np.arange(S, dtype=f), inv0).astype(f)
    row = (part % DK0) // 2
    sign = np.where(part % 2 == 0, -1.0, 1.0).astype(f)[:, None]
    inv1 = f(1.0) / f(150000.0) ** (np.arange(D1 // 2, dtype=f) * f(2.0) / f(D1))
    ang1 = (np.arange(S, dtype=f)[:, None] * inv1[None, :]).astype(f)
    scale1 = f(D1 ** (-0.25))
    cos1 = np.repeat(np.cos(ang1), 2, axis=-1) * scale1
    sin1 = np.repeat(np.sin(ang1), 2, axis=-1) * np.tile(np.array([-1, 1], f), D1 // 2) * scale1
    q, k = np.arange(S)[:, None], np.arange(S)[None, :]
    halves = lambda m: m.reshape(2, P, -1).transpose(1, 0, 2).reshape(P, -1)
    values = dict(
        ident=np.eye(P), ones=np.ones((P, P)), hm=part[:, None] // DK0 == np.arange(8),
        hx=part[:, None] // DX == np.arange(4), pm=part[:, None] // D1 == np.arange(2),
        slots=np.tile(np.arange(P), (P, 1)), before=part[:, None] < part,
        pairs=np.arange(TOPK * NT) * P + part[:, None] + 1,
        past=2 * TOPK * NT * P + 1 + part[:, None], cos0=np.cos(ang0).T[row], sin0=np.sin(ang0).T[row] * sign,
        causal=halves(np.where(k <= q, 0.0, -1e30)), window=halves(np.where(abs(q - k) <= 128, 0.0, -1e30)),
        cos1=halves(cos1), sin1=halves(sin1), eps=np.full((P, 1), EPS))
    table = np.concatenate([np.asarray(values[n], f) for n in TABLE], axis=1)
    had = np.array([[1.0]], f)
    while had.shape[0] < D:
        had = np.block([[had, had], [had, -had]])
    return np.ascontiguousarray(table), np.ascontiguousarray(had.astype(f))


def arrays_of(inputs):
    g = {n: np.asarray(a) for n, a in inputs.items()}
    x, ctx = g["x"], g["ctx_2048"]
    swap = np.arange(D) ^ 1
    wq, wk, wv = g["L0_attn_Wq"], g["L0_attn_Wk"], g["L0_attn_Wv"]
    wo0 = np.zeros((4, 4, 32, D), np.float32)
    wo0[:, :, 0:DK0] = g["L0_attn_Wo"].reshape(4, 4, DK0, D)
    flat = lambda a: a.reshape(D, -1)
    tiled = lambda a: a.reshape(-1, P, a.shape[2]).transpose(1, 0, 2)
    table, had = constants()
    return dict(
        x=x.reshape(NT, P, D), xT=x.reshape(B * S, D).T, ctx=ctx.reshape(NT, P, D),
        ctxT=ctx.transpose(0, 2, 1), tok=g["itok_BxS_13_99985"].reshape(NT, P).T,
        w0=np.stack([wq, wq[:, swap], wk, wk[:, swap], wv]), wo0=wo0.reshape(4, P, D),
        gamma=g["L0_xattn_gamma"].reshape(1, 1), wu=g["L0_ffn_w_up"].T, wd=g["L0_ffn_w_down"].T, had=had,
        w1=np.concatenate([flat(g["L1_attn_Wq"]), flat(g["L1_attn_Wk"]), flat(g["L1_attn_Wv"])], axis=1),
        bias1=np.concatenate([g["L1_attn_bq"].reshape(-1), g["L1_attn_bk"].reshape(-1),
                              g["L1_attn_bv"].reshape(-1)]).reshape(1, -1),
        wo1=g["L1_attn_Wo"].reshape(NQ1, D), bo1=g["L1_attn_bo"].reshape(1, D),
        sinks=g["L1_attn_sinks"].reshape(1, H1), gate=g["L1_ffn_gate_w"].T,
        w_in=tiled(np.concatenate([g["L1_ffn_Wg"], g["L1_ffn_Wu"]], axis=2)),
        w_out=g["L1_ffn_Wd"].transpose(1, 0, 2),
        c_in=tiled(np.concatenate([g["L1_ffn_cWg"], g["L1_ffn_cWu"]], axis=2)),
        c_out=g["L1_ffn_cWd"].transpose(1, 0, 2), table=table)


def kernel(**inputs):
    import concourse.bacc as bacc
    from concourse.bass_utils import run_bass_kernel_spmd

    nc = bacc.Bacc("TRN2", target_bir_lowering=False, num_devices=1)
    arrays, args = {}, []
    for name, a in arrays_of(inputs).items():
        a = np.ascontiguousarray(a)
        arrays["in_" + name] = a
        args.append(nc.dram_tensor("in_" + name, a.shape, mybir.dt.from_np(a.dtype), kind="ExternalInput").ap())
    out = nc.dram_tensor("out_0", (NT, P, D), F32, kind="ExternalOutput").ap()
    decoder(nc, *args, out)
    r = run_bass_kernel_spmd(nc, [arrays], core_ids=[0])
    return r.results[0]["out_0"].reshape(B, S, D)
```
